# Optimizing a Trainium2 kernel written in Bass

```python
import numpy as np
import jax
import jax.numpy as jnp

def _softmax(x, axis=-1):
    return jax.nn.softmax(x, axis=axis)

def _gelu(x):
    return jax.nn.gelu(x, approximate=True)

def _silu(x):
    return jax.nn.silu(x)

def _sigmoid(x):
    return jax.nn.sigmoid(x)

def _layernorm(x, axis=-1, eps=1e-05):
    m = jnp.mean(x, axis=axis, keepdims=True)
    v = jnp.var(x, axis=axis, keepdims=True)
    return (x - m) / jnp.sqrt(v + eps)

def _scatter_add(tgt, idx, src, axis=0):
    return tgt.at[idx].add(src)

def _segment_sum(src, seg, n):
    return jax.ops.segment_sum(src, seg, n)
kernel_name = 'mk_gnn_preln_d4_gnn_r8_ac69ca'

def setup_inputs(seed: int=0):
    np.random.seed(seed)
    _w = jnp.asarray

    def _rec_inputs():
        import jax
        import jax.numpy as jnp
        _gk = jax.random.key(seed)
        x = -0.000202 + 1 * jax.random.normal(jax.random.fold_in(_gk, 1), (6250, 64), jnp.float32)
        _s = jax.random.randint(jax.random.fold_in(_gk, 2), (100000,), 0, 6250, jnp.int32)
        _d = jax.random.randint(jax.random.fold_in(_gk, 3), (100000,), 0, 6250, jnp.int32)
        _loop = jnp.arange(6250, dtype=jnp.int32)
        src = jnp.concatenate([_s, _d, _loop])
        dst = jnp.concatenate([_d, _s, _loop])
        _o = jnp.argsort(dst, stable=True)
        src = src[_o]
        dst = dst[_o]
        edge_attr_64 = -9.77346e-05 + 0.999888 * jax.random.normal(jax.random.fold_in(_gk, 12), (206250, 64), jnp.float32)
        edge_type_4 = jax.random.randint(jax.random.fold_in(_gk, 14), (206250,), 0, 4, jnp.int32)
        return (x, src, dst, edge_attr_64, edge_type_4)
    x, src, dst, edge_attr_64, edge_type_4 = _rec_inputs()

    def _L0_gnn_setup():
        import jax, jax.numpy as jnp
        import numpy as np
        import math
        N_NODES = 12500
        D = 64
        N_EDGES = 160000
        LN_EPS = 1e-05
        key = jax.random.key(seed)
        ks = jax.random.split(key, 8)
        x = jax.random.normal(ks[0], (N_NODES, D), dtype=jnp.float32)
        edge_index = jax.random.randint(ks[1], (2, N_EDGES), 0, N_NODES, dtype=jnp.int64)
        limit = 0.1 * math.sqrt(6.0 / (D + D))
        qk_w = jax.random.uniform(ks[2], (D, D), dtype=jnp.float32, minval=-limit, maxval=limit)
        v_w = jax.random.uniform(ks[3], (D, D), dtype=jnp.float32, minval=-limit, maxval=limit)
        o_w = jax.random.uniform(ks[4], (D, D), dtype=jnp.float32, minval=-limit, maxval=limit)
        qk_b = jnp.zeros((D,), dtype=jnp.float32)
        v_b = jnp.zeros((D,), dtype=jnp.float32)
        o_b = jnp.zeros((D,), dtype=jnp.float32)
        ln_g = jnp.ones((D,), dtype=jnp.float32)
        ln_b = jnp.zeros((D,), dtype=jnp.float32)
        return {'x': x, 'edge_index': edge_index, 'qk_w': qk_w, 'qk_b': qk_b, 'v_w': v_w, 'v_b': v_b, 'o_w': o_w, 'o_b': o_b, 'ln_g': ln_g, 'ln_b': ln_b}
    _L0_gnn_all = _L0_gnn_setup()
    _L0_gnn_in = {k: v for k, v in _L0_gnn_all.items() if k in ('qk_w', 'qk_b', 'v_w', 'v_b', 'o_w', 'o_b', 'ln_g', 'ln_b')}
    del _L0_gnn_all

    def _L1_gnn_setup():
        import jax, jax.numpy as jnp
        import numpy as np
        N_NODES = 6250
        N_EDGES = 100000
        D_IN = 64
        D_OUT = 64
        key = jax.random.key(seed)
        k1, k2, k3, k4 = jax.random.split(key, 4)
        feat = jax.random.normal(k1, (N_NODES, D_IN), dtype=jnp.float32)
        limit = float(np.sqrt(6.0 / (D_IN + D_OUT)))
        weight = jax.random.uniform(k2, (D_IN, D_OUT), dtype=jnp.float32, minval=-limit, maxval=limit)
        bias = jnp.zeros((D_OUT,), dtype=jnp.float32)
        src = jax.random.randint(k3, (N_EDGES,), 0, N_NODES, dtype=jnp.int32)
        dst = jax.random.randint(k4, (N_EDGES,), 0, N_NODES, dtype=jnp.int32)
        return {'feat': feat, 'weight': weight, 'bias': bias, 'src': src, 'dst': dst}
    _L1_gnn_all = _L1_gnn_setup()
    _L1_gnn_in = {k: v for k, v in _L1_gnn_all.items() if k in ('weight', 'bias')}
    del _L1_gnn_all

    def _L2_gnn_setup():
        import jax, jax.numpy as jnp
        import numpy as np
        N_NODES = 6250
        N_EDGES = 100000
        D_NODE = 64
        D_EDGE = 64
        D_MSG = 128
        D_EIN = 2 * D_NODE + D_EDGE
        D_NIN = D_MSG + D_NODE

        def _mlp2(x, W1, b1, W2, b2):
            return jax.nn.relu(x @ W1 + b1) @ W2 + b2
        key = jax.random.key(seed)
        ks = jax.random.split(key, 16)
        s = 0.05
        return {'node_states': jax.random.normal(ks[0], (N_NODES, D_NODE), jnp.float32), 'edge_features': jax.random.normal(ks[1], (N_EDGES, D_EDGE), jnp.float32), 'W1_f': jax.random.normal(ks[2], (D_EIN, D_MSG), jnp.float32) * s, 'b1_f': jnp.zeros((D_MSG,), jnp.float32), 'W2_f': jax.random.normal(ks[3], (D_MSG, D_MSG), jnp.float32) * s, 'b2_f': jnp.zeros((D_MSG,), jnp.float32), 'W1_r': jax.random.normal(ks[4], (D_EIN, D_MSG), jnp.float32) * s, 'b1_r': jnp.zeros((D_MSG,), jnp.float32), 'W2_r': jax.random.normal(ks[5], (D_MSG, D_MSG), jnp.float32) * s, 'b2_r': jnp.zeros((D_MSG,), jnp.float32), 'Wn1': jax.random.normal(ks[6], (D_NIN, D_MSG), jnp.float32) * s, 'bn1': jnp.zeros((D_MSG,), jnp.float32), 'Wn2': jax.random.normal(ks[7], (D_MSG, D_NODE), jnp.float32) * s, 'bn2': jnp.zeros((D_NODE,), jnp.float32), 'from_idx': jax.random.randint(ks[8], (N_EDGES,), 0, N_NODES, jnp.int32), 'to_idx': jax.random.randint(ks[9], (N_EDGES,), 0, N_NODES, jnp.int32)}
    _L2_gnn_all = _L2_gnn_setup()
    _L2_gnn_in = {k: v for k, v in _L2_gnn_all.items() if k in ('W1_f', 'b1_f', 'W2_f', 'b2_f', 'W1_r', 'b1_r', 'W2_r', 'b2_r', 'Wn1', 'bn1', 'Wn2', 'bn2')}
    del _L2_gnn_all

    def _L3_gnn_setup():
        import jax, jax.numpy as jnp
        import numpy as np
        N = 6250
        E = 100000
        H = 64
        K = 4
        STEPS = 4

        def _gru_cell(a, feat, w_ih, w_hh, b_ih, b_hh):
            gi = a @ w_ih.T + b_ih
            gh = feat @ w_hh.T + b_hh
            i_r, i_z, i_n = jnp.split(gi, 3, axis=-1)
            h_r, h_z, h_n = jnp.split(gh, 3, axis=-1)
            r = jax.nn.sigmoid(i_r + h_r)
            z = jax.nn.sigmoid(i_z + h_z)
            n = jnp.tanh(i_n + r * h_n)
            return (1.0 - z) * n + z * feat
        key = jax.random.key(seed)
        ks = jax.random.split(key, 10)
        s = 0.05
        return {'h': jax.random.normal(ks[0], (N, H), jnp.float32), 'W': jax.random.normal(ks[1], (K, H, H), jnp.float32) * s, 'b': jax.random.normal(ks[2], (K, H), jnp.float32) * s, 'w_ih': jax.random.normal(ks[3], (3 * H, H), jnp.float32) * s, 'w_hh': jax.random.normal(ks[4], (3 * H, H), jnp.float32) * s, 'b_ih': jax.random.normal(ks[5], (3 * H,), jnp.float32) * s, 'b_hh': jax.random.normal(ks[6], (3 * H,), jnp.float32) * s, 'src': jax.random.randint(ks[7], (E,), 0, N, dtype=jnp.int32), 'dst': jax.random.randint(ks[8], (E,), 0, N, dtype=jnp.int32), 'etypes': jax.random.randint(ks[9], (E,), 0, K, dtype=jnp.int32)}
    _L3_gnn_all = _L3_gnn_setup()
    _L3_gnn_in = {k: v for k, v in _L3_gnn_all.items() if k in ('W', 'b', 'w_ih', 'w_hh', 'b_ih', 'b_hh')}
    del _L3_gnn_all
    return {'x': x, 'src': src, 'dst': dst, 'edge_attr_64': edge_attr_64, 'edge_type_4': edge_type_4, 'L0_gnn_qk_w': _L0_gnn_in['qk_w'], 'L0_gnn_qk_b': _L0_gnn_in['qk_b'], 'L0_gnn_v_w': _L0_gnn_in['v_w'], 'L0_gnn_v_b': _L0_gnn_in['v_b'], 'L0_gnn_o_w': _L0_gnn_in['o_w'], 'L0_gnn_o_b': _L0_gnn_in['o_b'], 'L0_gnn_ln_g': _L0_gnn_in['ln_g'], 'L0_gnn_ln_b': _L0_gnn_in['ln_b'], 'L1_gnn_weight': _L1_gnn_in['weight'], 'L1_gnn_bias': _L1_gnn_in['bias'], 'L2_gnn_W1_f': _L2_gnn_in['W1_f'], 'L2_gnn_b1_f': _L2_gnn_in['b1_f'], 'L2_gnn_W2_f': _L2_gnn_in['W2_f'], 'L2_gnn_b2_f': _L2_gnn_in['b2_f'], 'L2_gnn_W1_r': _L2_gnn_in['W1_r'], 'L2_gnn_b1_r': _L2_gnn_in['b1_r'], 'L2_gnn_W2_r': _L2_gnn_in['W2_r'], 'L2_gnn_b2_r': _L2_gnn_in['b2_r'], 'L2_gnn_Wn1': _L2_gnn_in['Wn1'], 'L2_gnn_bn1': _L2_gnn_in['bn1'], 'L2_gnn_Wn2': _L2_gnn_in['Wn2'], 'L2_gnn_bn2': _L2_gnn_in['bn2'], 'L3_gnn_W': _L3_gnn_in['W'], 'L3_gnn_b': _L3_gnn_in['b'], 'L3_gnn_w_ih': _L3_gnn_in['w_ih'], 'L3_gnn_w_hh': _L3_gnn_in['w_hh'], 'L3_gnn_b_ih': _L3_gnn_in['b_ih'], 'L3_gnn_b_hh': _L3_gnn_in['b_hh']}

def reference(x, src, dst, edge_attr_64, edge_type_4, L0_gnn_qk_w, L0_gnn_qk_b, L0_gnn_v_w, L0_gnn_v_b, L0_gnn_o_w, L0_gnn_o_b, L0_gnn_ln_g, L0_gnn_ln_b, L1_gnn_weight, L1_gnn_bias, L2_gnn_W1_f, L2_gnn_b1_f, L2_gnn_W2_f, L2_gnn_b2_f, L2_gnn_W1_r, L2_gnn_b1_r, L2_gnn_W2_r, L2_gnn_b2_r, L2_gnn_Wn1, L2_gnn_bn1, L2_gnn_Wn2, L2_gnn_bn2, L3_gnn_W, L3_gnn_b, L3_gnn_w_ih, L3_gnn_w_hh, L3_gnn_b_ih, L3_gnn_b_hh):
    import jax
    import jax.numpy as jnp

    def _L0_gnn_ref(x, edge_index, qk_w, qk_b, v_w, v_b, o_w, o_b, ln_g, ln_b):
        import jax, jax.numpy as jnp
        import numpy as np
        import math
        N_NODES = 12500
        D = 64
        N_EDGES = 160000
        LN_EPS = 1e-05
        n = x.shape[0]
        qk = x @ qk_w.T + qk_b
        v = x @ v_w.T + v_b
        src = edge_index[0]
        dst = edge_index[1]
        scores = jnp.sum(qk[dst] * qk[src], axis=-1) / math.sqrt(v.shape[-1])
        scores = jnp.clip(scores, -5.0, 5.0)
        seg_max = jax.ops.segment_max(scores, dst, num_segments=n)
        e = jnp.exp(scores - seg_max[dst])
        seg_sum = jax.ops.segment_sum(e, dst, num_segments=n)
        attn = e / seg_sum[dst]
        out = jax.ops.segment_sum(attn[:, None] * v[src], dst, num_segments=n)
        out = out @ o_w.T + o_b
        h = out + x
        mu = jnp.mean(h, axis=-1, keepdims=True)
        var = jnp.mean(jnp.square(h - mu), axis=-1, keepdims=True)
        h = (h - mu) * jax.lax.rsqrt(var + LN_EPS)
        return h * ln_g + ln_b

    def _L1_gnn_ref(feat, weight, bias, src, dst):
        import jax, jax.numpy as jnp
        import numpy as np
        N_NODES = 6250
        N_EDGES = 100000
        D_IN = 64
        D_OUT = 64
        n = feat.shape[0]
        deg = jax.ops.segment_sum(jnp.ones_like(dst, dtype=feat.dtype), dst, num_segments=n)
        norm = jnp.clip(deg, 1.0) ** (-0.5)
        h = feat * norm[:, None]
        agg = jax.ops.segment_sum(h[src], dst, num_segments=n)
        rst = agg @ weight
        rst = rst * norm[:, None] + bias
        return rst

    def _L2_gnn_ref(node_states, edge_features, W1_f, b1_f, W2_f, b2_f, W1_r, b1_r, W2_r, b2_r, Wn1, bn1, Wn2, bn2, from_idx, to_idx):
        import jax, jax.numpy as jnp
        import numpy as np
        N_NODES = 6250
        N_EDGES = 100000
        D_NODE = 64
        D_EDGE = 64
        D_MSG = 128
        D_EIN = 2 * D_NODE + D_EDGE
        D_NIN = D_MSG + D_NODE

        def _mlp2(x, W1, b1, W2, b2):
            return jax.nn.relu(x @ W1 + b1) @ W2 + b2
        n_nodes = node_states.shape[0]
        edge_in_f = jnp.concatenate([node_states[from_idx], node_states[to_idx], edge_features], axis=-1)
        msgs_f = _mlp2(edge_in_f, W1_f, b1_f, W2_f, b2_f)
        agg = jax.ops.segment_sum(msgs_f, to_idx, num_segments=n_nodes)
        edge_in_r = jnp.concatenate([node_states[to_idx], node_states[from_idx], edge_features], axis=-1)
        msgs_r = _mlp2(edge_in_r, W1_r, b1_r, W2_r, b2_r)
        agg = agg + jax.ops.segment_sum(msgs_r, from_idx, num_segments=n_nodes)
        node_in = jnp.concatenate([agg, node_states], axis=-1)
        return node_states + _mlp2(node_in, Wn1, bn1, Wn2, bn2)

    def _L3_gnn_ref(h, W, b, w_ih, w_hh, b_ih, b_hh, src, dst, etypes):
        import jax, jax.numpy as jnp
        import numpy as np
        N = 6250
        E = 100000
        H = 64
        K = 4
        STEPS = 4

        def _gru_cell(a, feat, w_ih, w_hh, b_ih, b_hh):
            gi = a @ w_ih.T + b_ih
            gh = feat @ w_hh.T + b_hh
            i_r, i_z, i_n = jnp.split(gi, 3, axis=-1)
            h_r, h_z, h_n = jnp.split(gh, 3, axis=-1)
            r = jax.nn.sigmoid(i_r + h_r)
            z = jax.nn.sigmoid(i_z + h_z)
            n = jnp.tanh(i_n + r * h_n)
            return (1.0 - z) * n + z * feat
        num_nodes = h.shape[0]

        def step(feat, _):
            transformed = jnp.einsum('nd,khd->knh', feat, W) + b[:, None, :]
            msgs = transformed[etypes, src]
            a = jax.ops.segment_sum(msgs, dst, num_segments=num_nodes)
            feat = _gru_cell(a, feat, w_ih, w_hh, b_ih, b_hh)
            return (feat, None)
        feat, _ = jax.lax.scan(step, h, None, length=STEPS)
        return feat
    edge_index = jnp.stack([src, dst])
    h = jnp.maximum(_layernorm(x, axis=-1), 0.0)
    x = x + _L0_gnn_ref(h, edge_index, L0_gnn_qk_w, L0_gnn_qk_b, L0_gnn_v_w, L0_gnn_v_b, L0_gnn_o_w, L0_gnn_o_b, L0_gnn_ln_g, L0_gnn_ln_b)
    h = jnp.maximum(_layernorm(x, axis=-1), 0.0)
    x = x + _L1_gnn_ref(h, L1_gnn_weight, L1_gnn_bias, src, dst)
    h = jnp.maximum(_layernorm(x, axis=-1), 0.0)
    x = x + _L2_gnn_ref(h, edge_attr_64, L2_gnn_W1_f, L2_gnn_b1_f, L2_gnn_W2_f, L2_gnn_b2_f, L2_gnn_W1_r, L2_gnn_b1_r, L2_gnn_W2_r, L2_gnn_b2_r, L2_gnn_Wn1, L2_gnn_bn1, L2_gnn_Wn2, L2_gnn_bn2, src, dst)
    h = jnp.maximum(_layernorm(x, axis=-1), 0.0)
    x = x + _L3_gnn_ref(h, L3_gnn_W, L3_gnn_b, L3_gnn_w_ih, L3_gnn_w_hh, L3_gnn_b_ih, L3_gnn_b_hh, src, dst, edge_type_4)
    return x

_drawn_inputs = setup_inputs


def setup_inputs(seed=0):
    import zlib

    import numpy as np

    out = dict(_drawn_inputs(seed))
    spreads = {'L0_gnn_qk_b': (0.0, 0.8),
     'L0_gnn_v_b': (0.0, 0.8),
     'L0_gnn_o_b': (0.0, 0.1),
     'L0_gnn_ln_g': (1.0, 0.2),
     'L0_gnn_ln_b': (0.0, 0.1),
     'L1_gnn_bias': (0.0, 0.1),
     'L2_gnn_b1_f': (0.0, 0.1),
     'L2_gnn_b2_f': (0.0, 0.1),
     'L2_gnn_b1_r': (0.0, 0.1),
     'L2_gnn_b2_r': (0.0, 0.1),
     'L2_gnn_bn1': (0.0, 0.8),
     'L2_gnn_bn2': (0.0, 0.1)}
    factors = {'L0_gnn_qk_w': 8.0,
     'L0_gnn_v_w': 8.0,
     'L0_gnn_o_w': 5.961,
     'L3_gnn_b_ih': 4.631,
     'L3_gnn_b_hh': 8.0}
    for name, (base, spread) in spreads.items():
        noise = np.random.default_rng([zlib.crc32(name.encode()), seed]).standard_normal(out[name].shape)
        drawn = base * np.exp(spread * noise) if base else spread * noise
        out[name] = jnp.asarray(drawn.astype(out[name].dtype))
    for name, factor in factors.items():
        out[name] = (out[name] * factor).astype(out[name].dtype)
    return out
```

```python
from contextlib import ExitStack

import concourse.bass as bass
from concourse import mybir

P = 128
N = 6250
D = 64
E = 206250
NB = -(-N // P)
NPAD = NB * P
T = -(-E // P)
STEPS = T + NB - 1
CG = -(-STEPS // P)
SPAD = CG * P
M = 128
KT = 4
LAYERS = 4
KV = 2 * D + 1
AC = D + 2
RC = M + 1
R = 4
TRASH = NPAD
RROWS = NPAD + P
U = 20
HALF = U // 2
NIT = STEPS // U
UN = 6
OHR = 10
MR = 4
EPS = 1e-5
TINY = 1e-30
PADDST = NPAD - 1
IDXQ = -(-CG // 4)
assert STEPS % U == 0 and OHR <= U and U % OHR == 0

F32 = mybir.dt.float32
I32 = mybir.dt.int32
ALU = mybir.AluOpType
ACT = mybir.ActivationFunctionType
AXX = mybir.AxisListType.X

WCOLS = {}
_at = 0
for _n, _w in (("qkv", 2 * D), ("attn", D), ("conv", D), ("pair", 2 * M), ("edge", 2 * M), ("f2", M), ("r2", M),
               ("n1a", M), ("n1b", M), ("n2", D), ("types", KT * D), ("gru", 4 * D), ("b2", M), ("bn1", 1),
               ("bn2", D), ("gb0", 4 * D), ("gb1", 4 * D)):
    WCOLS[_n] = (_at, _at + _w)
    _at += _w
WTOTAL = _at


def known(k):
    return isinstance(k, int)


def pipeline(eng, n, unroll, lag, emit):
    for j in range(unroll):
        emit(0, j)
    with eng.Fori(1, n // unroll) as it:
        for j in range(unroll):
            emit(it, j)
    for i in range(n // unroll * unroll, n + lag):
        emit(i // unroll, i % unroll)


def stage(n, unroll, it, j, lag, body):
    k, slot, kit = it * unroll + (j - lag), (j - lag) % unroll, it + (j - lag) // unroll
    if known(k) and not 0 <= k < n:
        return
    body(k, slot, kit)


def build(nc, a, out):
    ctx = ExitStack()
    with ctx:
        def sb(name, shape, dt=F32):
            return ctx.enter_context(nc.sbuf_tensor(name, shape, dt))

        def sem(name):
            return ctx.enter_context(nc.semaphore(name))

        def dram(name, shape, dt=F32):
            return nc.dram_tensor(name, shape, dt).ap()

        kv_table = dram("kv_table", (NPAD, KV))
        h_table = dram("h_table", (NPAD, D))
        type_table = dram("type_table", (KT * NPAD, D))
        reverse = [dram(f"reverse{r}", (RROWS, RC)) for r in range(R)]
        path_rows = dram("path_rows", (2 * CG, P), I32)

        X = sb("X", [P, NB, D])
        H = sb("H", [P, NB, D])
        tmp = sb("tmp", [P, NB, D])
        acc = sb("acc", [P, 50 * RC])
        big = sb("big", [P, NB * 2 * M])
        small = sb("small", [P, 4, NB])
        norm = sb("norm", [P, NB])
        deg = sb("deg", [P, NB])
        dloc = sb("dloc", [P, SPAD])
        key = sb("key", [P, SPAD])
        srci = sb("srci", [P, SPAD], I32)
        tsrci = sb("tsrci", [P, SPAD], I32)
        path = sb("path", [1, 2 * SPAD], I32)
        icol = sb("icol", [P, CG], I32)
        fcol = sb("fcol", [P, 4, CG])
        tcol = sb("tcol", [P, CG], I32)
        pcol = sb("pcol", [CG, 2, P], I32)
        ident = sb("ident", [P, P])
        iota = sb("iota", [P, P])
        earlier = sb("earlier", [P, P])
        trash = sb("trash", [P, 1])
        ones = sb("ones", [1, P])
        hold_in = sb("hold_in", [P, 1])
        hold_out = sb("hold_out", [P, 1])
        scatter_hold = sb("scatter_hold", [P, 1])
        types_hold = sb("types_hold", [P, 1])
        hold2 = sb("hold2", [P, 1])
        hidden = sb("hidden", [P, 2, P])
        idx = sb("idx", [P, U], I32)
        G = sb("G", [P, U, KV + 1])
        OH = sb("OH", [P, OHR, P])
        OT = sb("OT", [P, 2, 2 * P])
        prod = sb("prod", [P, 2, P])
        sc = sb("sc", [P, 3, MR])
        MS = sb("MS", [P, MR, 2 * M + 2])
        EQ = sb("EQ", [P, MR, P])
        cnt = sb("cnt", [P, 2, MR])
        sidx = sb("sidx", [P, U], I32)
        SD = sb("SD", [P, R, RC])
        keyslot = sb("keyslot", [P, U])
        keyless = sb("keyless", [P, U])
        S = sb("S", [P, 2, 3 * M])
        ST = sb("ST", [P, 2, 3 * P])
        NX = sb("NX", [P, 2, 4 * M])
        revs = sb("revs", [P, 2, R, RC])
        W = sb("W", [P, WTOTAL])
        lng = sb("lng", [P, 3, D])
        bank = [ctx.enter_context(nc.psum_tensor(f"bank{i}", [P, 512], F32)) for i in range(8)]

        def w(name, rows=P):
            lo, hi = WCOLS[name]
            return W[0:rows, lo:hi]

        acc_ = {c: acc[:, 0:NB * c] for c in (AC, D, M)}
        big_kv = big[:, 0:NB * KV]
        X_, H_, tmp_ = X[:, :, :], H[:, :, :], tmp[:, :, :]
        flat = {id(t): t.rearrange("p b d -> p (b d)") for t in (X_, H_, tmp_)}
        Xf, Hf, tmpf = (flat[id(t)] for t in (X_, H_, tmp_))

        def part(t, k, width, lo=0, hi=None):
            hi = width if hi is None else hi
            if known(k):
                return t[:, k * width + lo:k * width + hi]
            return t[:, bass.ds(k * width + lo, hi - lo)]

        x_loaded, dst_loaded, w_loaded, reverse_zero = (sem(n) for n in ("x_loaded", "dst_loaded", "w_loaded", "reverse_zero"))
        acc_zero, consts, path_f, tiles_known = (sem(n) for n in ("acc_zero", "consts", "path_f", "tiles_known"))
        tiles_read = sem("tiles_read")
        path_turned, path_copied, path_stored, path_loaded = (sem(n) for n in ("path_turned", "path_copied", "path_stored", "path_loaded"))
        idx_made, idx_turned, idx_tabled = (sem(n) for n in ("idx_made", "idx_turned", "idx_tabled"))
        chain = sem("chain")
        root_in, root_out = sem("root_in"), sem("root_out")
        table_ready, table_stored = sem("table_ready"), sem("table_stored")
        gathered = [sem(f"gathered{j}") for j in range(U)]
        tile_rows = [sem(f"tile_rows{q}") for q in range(3)]
        edge_loaded = [sem(f"edge_loaded{j}") for j in range(HALF)]
        scattered = [sem(f"scattered{r}") for r in range(R)]
        idx_copied, scatter_go = sem("idx_copied"), sem("scatter_go")
        rev_loaded = [sem(f"rev_loaded{r}") for r in range(2)]
        pass_begun = sem("pass_begun")
        gru_acc_zero = sem("gru_acc_zero")
        types_stored, types_go = sem("types_stored"), sem("types_go")
        result, result_stored = sem("result"), sem("result_stored")

        class Sems:
            def __init__(self, phase, names):
                self.at = {n: sem(f"{phase}_{n}") for n in names.split()}

            def __getitem__(self, n):
                return self.at[n]

        node = Sems("node", "rows turned copied product finished")
        QKV, ATTN, CONV, PAIR, TYPES = (n * NB for n in range(5))
        att = Sems("att", "onehot turned copied query score clipped exp msg seg summed")
        mes = Sems("mes", "less keys keyrow equal count rep index onehot turned copied pre relu seg summed rowsout")
        plain = Sems("plain", "onehot seg summed")
        upd = Sems("upd", "sums rows turned copied agg aggout hid hidout product finished")
        gru = Sems("gru", "rows turned copied product gates mul add tanh diff blend finished")

        block = ctx.enter_context(nc.Block())

        def node_pe(pe, s, rows, wt, width, base=0):
            def turn(k, j, it):
                pe.wait_ge(s["rows"], base + k + 1)
                if not (known(k) and k < 2):
                    pe.wait_ge(s["copied"], base + k - 1)
                nc.tensor.transpose(bank[j % 2][0:rows, 0:P], S[:, j % 2, 0:rows], ident[:, :]).then_inc(s["turned"], 1)

            def mul(k, j, it):
                pe.wait_ge(s["copied"], base + k + 1)
                if not (known(k) and k < 2):
                    pe.wait_ge(s["finished"], base + k - 1)
                nc.tensor.matmul(bank[2 + j % 2][:, 0:width], ST[0:rows, j % 2, 0:P], wt,
                                 start=True, stop=True).then_inc(s["product"], 1)

            def emit(it, j):
                stage(NB, UN, it, j, 0, turn)
                stage(NB, UN, it, j, 1, mul)
            pipeline(pe, NB, UN, 1, emit)

        def node_act(act, s, rows, base=0):
            def copy(k, j, it):
                act.wait_ge(s["turned"], base + k + 1)
                if not (known(k) and k < 2):
                    act.wait_ge(s["product"], base + k - 1)
                nc.scalar.activation(ST[0:rows, j % 2, 0:P], bank[j % 2][0:rows, 0:P], ACT.Copy).then_inc(s["copied"], 1)
            pipeline(act, NB, UN, 0, lambda it, j: stage(NB, UN, it, j, 0, copy))

        def node_dve(v, s, source, finish, base=0):
            def rows(k, j, it):
                if not (known(k) and k < 2):
                    v.wait_ge(s["turned"], base + k - 1)
                nc.vector.tensor_copy(S[:, j % 2, 0:D], source(k)).then_inc(s["rows"], 1)

            def end(k, j, it):
                v.wait_ge(s["product"], base + k + 1)
                finish(k, bank[2 + j % 2]).then_inc(s["finished"], 1)

            def emit(it, j):
                stage(NB, UN, it, j, 0, rows)
                stage(NB, UN, it, j, 2, end)
            pipeline(v, NB, UN, 2, emit)

        def gather(pool, turns, table, index, width, used, used_base, also=None, lag=0):
            def get(k, j, it):
                if j % HALF == 0:
                    copied = (turns + it) * 6 + j // HALF * 3
                    if not (known(k) and k < U):
                        for q in range(j, j + HALF):
                            pool.wait_ge(gathered[q], (turns + it) * 16)
                        pool.wait_ge(used, used_base + k - HALF)
                    pool.wait_ge(idx_copied, copied + 1)
                    nc.gpsimd.tensor_tensor(hold_out[:, :], hold_in[:, :], hold_in[:, :], ALU.add)\
                        .then_inc(idx_copied, 1)
                    nc.gpsimd.tensor_copy(idx[:, j:j + HALF],
                                          index[:, k:k + HALF] if known(k) else index[:, bass.ds(k, HALF)])\
                        .then_inc(idx_copied, 1)
                    pool.wait_ge(idx_copied, copied + 3)
                    nc.gpsimd.tensor_tensor(hold_out[:, :], hold_in[:, :], hold_in[:, :], ALU.add)\
                        .then_inc(idx_copied, 1)
                nc.gpsimd.indirect_dma_start(G[:, j, 0:width], None, table,
                                             bass.IndirectOffsetOnAxis(idx[:, j:j + 1], 0))\
                    .then_inc(gathered[j], 16)

            def emit(it, j):
                stage(STEPS, U, it, j, 0, get)
                if also:
                    stage(STEPS, U, it, j, lag, also)
            pipeline(pool, STEPS, U, lag, emit)

        def onehot(v, s, base, free_lag=OHR):
            def body(k, j, it):
                if not (known(k) and k < OHR):
                    v.wait_ge(s["seg"], base + k - OHR + 1)
                nc.vector.tensor_scalar(OH[:, j % OHR, :], iota[:, :], part(dloc[:, :], k, 1), None,
                                        ALU.is_equal).then_inc(s["onehot"], 1)
            return body

        def sum_up(v, s, base, width, banks):
            def body(k, j, it):
                b = v.value_load(path[0:1, k:k + 1] if known(k) else path[0:1, bass.ds(k, 1)], min_val=0, max_val=NB - 1)
                v.wait_ge(s["seg"], base + k + 1)
                if not (known(k) and k < 1):
                    v.wait_ge(s["summed"], base + k)
                to = acc_[width][:, bass.ds(b * width, width)]
                nc.vector.tensor_tensor(to, to, banks[j % 2][:, 0:width], ALU.add).then_inc(s["summed"], 1)
            return body

        def plain_pe(pe, s, turns, base):
            def seg(k, j, it):
                pe.wait_ge(gathered[j], (turns + it + 1) * 16)
                pe.wait_ge(s["onehot"], base + k + 1)
                if not (known(k) and k < 2):
                    pe.wait_ge(s["summed"], base + k - 1)
                nc.tensor.matmul(bank[j % 2][:, 0:D], OH[:, j % OHR, :], G[:, j, 0:D],
                                 start=True, stop=True).then_inc(s["seg"], 1)
            pipeline(pe, STEPS, U, 0, lambda it, j: stage(STEPS, U, it, j, 0, seg))

        def plain_dve(v, s, base):
            hot, add = onehot(v, s, base), sum_up(v, s, base, D, bank[0:2])

            def emit(it, j):
                stage(STEPS, U, it, j, 0, hot)
                stage(STEPS, U, it, j, 3, add)
            pipeline(v, STEPS, U, 3, emit)

        @block.sync
        def _(sp):
            sp.dma_start(big[:, 0:T].bitcast(I32), a["dst_last"].partition_broadcast(P)).then_inc(dst_loaded, 16)
            sp.dma_start(X_, a["x"].rearrange("(b p) d -> p b d", p=P)).then_inc(x_loaded, 16)
            sp.dma_start(W[:, :], a["weights"]).then_inc(w_loaded, 16)
            sp.dma_start(lng[:, :, :].rearrange("p a d -> p (a d)"), a["vectors"].partition_broadcast(P)).then_inc(w_loaded, 16)
            sp.wait_ge(acc_zero, 1)
            for r in range(R):
                sp.dma_start(reverse[r].rearrange("(p q) d -> p (q d)", p=P), acc[:, 0:50 * RC]).then_inc(reverse_zero, 16)
            sp.wait_ge(path_copied, 2)
            sp.dma_start(path_rows.rearrange("(a c) p -> c a p", a=2), pcol[:, :, :]).then_inc(path_stored, 16)
            sp.wait_ge(path_stored, 16)
            sp.dma_start(path[:, :], path_rows.rearrange("(o c) p -> o (c p)", o=1)).then_inc(path_loaded, 16)

            def store(table, source, n, width):
                sp.wait_ge(table_ready, n)
                sp.dma_start(table.rearrange("(b p) d -> p b d", p=P),
                             source.rearrange("p (b d) -> p b d", d=width)).then_inc(table_stored, 16)

            store(kv_table, big_kv, 1, KV)
            store(h_table, tmpf, 2, D)
            store(h_table, Hf, 3, D)

            sp.wait_ge(table_stored, 48)
            sp.wait_ge(path_loaded, 16)
            def features(k, j, it):
                t = sp.value_load(path[0:1, SPAD + k:SPAD + k + 1] if known(k) else path[0:1, bass.ds(k + SPAD, 1)],
                                  min_val=0, max_val=T)
                first = sp.snap(t * P)
                if not (known(k) and k < HALF):
                    sp.wait_ge(mes["turned"], k - HALF + 1)
                sp.dma_start(G[:, j, D:2 * D], a["edge"][bass.ds(first, P), :]).then_inc(edge_loaded[j % HALF], 16)
            pipeline(sp, STEPS, U, 0, lambda it, j: stage(STEPS, U, it, j, 0, features))

            for r in range(R):
                sp.wait_ge(scattered[r], 16 * (STEPS // R))
            def sums(k, j, it):
                first = k * P if known(k) else sp.snap(k * P)
                if not (known(k) and k < 2):
                    sp.wait_ge(upd["rows"], k - 1)
                for r in range(R):
                    sp.dma_start(revs[:, j % 2, r, :], reverse[r][bass.ds(first, P), :]).then_inc(rev_loaded[j % 2], 16)
            pipeline(sp, NB, UN, 0, lambda it, j: stage(NB, UN, it, j, 0, sums))

            with sp.Fori(0, LAYERS) as layer:
                sp.wait_ge(node["finished"], layer * NB + (TYPES + NB))
                for t in range(KT):
                    sp.dma_start(type_table[t * NPAD:(t + 1) * NPAD, :].rearrange("(b p) d -> p b d", p=P),
                                 big[:, :].rearrange("p (b d) -> p b d", d=KT * D)[:, :, t * D:(t + 1) * D])\
                        .then_inc(types_stored, 16)
            sp.wait_ge(types_stored, 16 * KT * LAYERS)
            sp.wait_ge(result, 1)
            full = N // P
            sp.dma_start(out[0:full * P, :].rearrange("(b p) d -> p b d", p=P), X[:, 0:full, :]).then_inc(result_stored, 16)
            sp.dma_start(out[full * P:N, :], X[0:N - full * P, full, :]).then_inc(result_stored, 16)
            sp.wait_ge(result_stored, 32)

        @block.gpsimd
        def _(pool):
            nc.gpsimd.iota(G[:, 0:14, 0:KV + 1].rearrange("p a b -> p (a b)")[:, 0:T].bitcast(I32), pattern=[[1, T]], base=0,
                           channel_multiplier=0).then_inc(consts, 1)
            nc.gpsimd.iota(icol[:, :], pattern=[[P, CG]], base=0, channel_multiplier=1).then_inc(consts, 1)
            nc.gpsimd.iota(srci[:, :], pattern=[[0, CG], [1, P]], base=TRASH, channel_multiplier=0).then_inc(consts, 1)
            nc.gpsimd.iota(idx[:, 0:1], pattern=[[0, 1]], base=TRASH, channel_multiplier=1).then_inc(consts, 1)
            nc.gpsimd.iota(tsrci[:, 0:P], pattern=[[1, P]], base=0, channel_multiplier=0).then_inc(consts, 1)
            nc.gpsimd.memset(ident[:, :], 0.0).then_inc(consts, 1)
            nc.gpsimd.memset(earlier[:, :], 1.0).then_inc(consts, 1)
            nc.gpsimd.memset(hold_in[:, :], 0.0).then_inc(consts, 1)
            nc.gpsimd.memset(ones[:, :], 1.0).then_inc(consts, 1)
            pool.wait_ge(consts, 9)
            nc.gpsimd.affine_select(out=ident[:, :], in_=ident[:, :], compare_op=ALU.not_equal, fill=1.0, base=0,
                                    pattern=[[-1, P]], channel_multiplier=1).then_inc(consts, 1)
            nc.gpsimd.affine_select(out=earlier[:, :], in_=earlier[:, :], compare_op=ALU.is_gt, fill=0.0, base=0,
                                    pattern=[[-1, P]], channel_multiplier=1).then_inc(consts, 1)
            nc.gpsimd.tensor_tensor(hold_out[:, :], hold_in[:, :], hold_in[:, :], ALU.add).then_inc(idx_copied, 1)

            pool.wait_ge(tiles_known, 1)
            for q, name in enumerate(("dst", "src", "type")):
                for c in range(CG):
                    lo = (2 + q) * SPAD + c * P
                    nc.gpsimd.indirect_dma_start(big[:, lo:lo + P].bitcast(I32), None, a[name],
                                                 bass.IndirectOffsetOnAxis(tcol[:, c:c + 1], 0))\
                        .then_inc(tile_rows[q], 16)
            for q in range(3):
                pool.wait_ge(tile_rows[q], 16 * CG)
            nc.gpsimd.tensor_copy(hold_in[:, :], hold_in[:, :]).then_inc(tiles_read, 1)
            pool.wait_ge(tiles_read, 1)

            pool.wait_ge(idx_tabled, 4 * IDXQ)
            pool.wait_ge(table_stored, 16)
            gather(pool, 0, kv_table, srci, KV, att["msg"], 0)
            pool.wait_ge(table_stored, 32)
            gather(pool, NIT, h_table, srci, D, plain["seg"], 0)
            pool.wait_ge(table_stored, 48)
            pool.wait_ge(reverse_zero, 16 * R)

            def scatter(k, j, it):
                pool.wait_ge(mes["index"], k + 1)
                pool.wait_ge(mes["rowsout"], k + 1)
                if not (known(k) and k < R):
                    pool.wait_ge(scattered[j % R], (it * (U // R) + j // R) * 16)
                if not (known(k) and k < 1):
                    pool.wait_ge(scatter_go, k)
                nc.gpsimd.tensor_tensor(scatter_hold[:, :], hold_in[:, :], hold_in[:, :], ALU.add).then_inc(scatter_go, 1)
                nc.gpsimd.indirect_dma_start(reverse[j % R], bass.IndirectOffsetOnAxis(sidx[:, j:j + 1], 0),
                                             SD[:, j % R, :], None, compute_op=ALU.add).then_inc(scattered[j % R], 16)
            gather(pool, 2 * NIT, h_table, srci, D, mes["turned"], 0, also=scatter, lag=6)
            with pool.Fori(0, LAYERS) as layer:
                pool.wait_ge(types_stored, layer * (16 * KT) + 16 * KT)
                nc.gpsimd.tensor_tensor(types_hold[:, :], hold_in[:, :], hold_in[:, :], ALU.add).then_inc(types_go, 1)
                pool.wait_ge(types_go, layer + 1)
                gather(pool, layer * NIT + 3 * NIT, type_table, tsrci, D, plain["seg"], layer * STEPS + STEPS)

        @block.scalar
        def _(act):
            def root(n):
                act.wait_ge(root_in, n)
                nc.scalar.activation(small[:, 0, :], small[:, 3, :], ACT.Sqrt).then_inc(root_out, 1)

            root(1)
            node_act(act, node, D + 1, QKV)

            def copy(k, j, it):
                act.wait_ge(att["turned"], k + 1)
                if not (known(k) and k < 2):
                    act.wait_ge(att["query"], k - 1)
                nc.scalar.activation(OT[:, j % 2, 0:P], bank[j % 2][:, 0:P], ACT.Copy).then_inc(att["copied"], 1)

            def exp(k, j, it):
                act.wait_ge(att["clipped"], k + 1)
                nc.scalar.activation(sc[:, 2, j % MR:j % MR + 1], sc[:, 1, j % MR:j % MR + 1], ACT.Exp).then_inc(att["exp"], 1)

            def msg(k, j, it):
                act.wait_ge(att["exp"], k + 1)
                if not (known(k) and k < MR):
                    act.wait_ge(att["seg"], k - MR + 1)
                nc.scalar.activation(MS[:, j % MR, 0:D + 1], G[:, j, D:KV], ACT.Copy,
                                     scale=sc[:, 2, j % MR:j % MR + 1]).then_inc(att["msg"], 1)

            def emit(it, j):
                stage(STEPS, U, it, j, 3, exp)
                stage(STEPS, U, it, j, 0, copy)
                stage(STEPS, U, it, j, 3, msg)
            pipeline(act, STEPS, U, 3, emit)
            root(2)
            node_act(act, node, D + 1, ATTN)
            root(3)
            root(4)
            node_act(act, node, D + 1, CONV)
            root(5)
            node_act(act, node, D + 1, PAIR)

            def copy2(k, j, it):
                act.wait_ge(mes["turned"], k + 1)
                if not (known(k) and k < 2):
                    act.wait_ge(mes["pre"], k - 1)
                nc.scalar.activation(OT[:, j % 2, :], bank[j % 2][:, 0:2 * P], ACT.Copy).then_inc(mes["copied"], 1)

            def relu(k, j, it):
                act.wait_ge(mes["pre"], k + 1)
                if not (known(k) and k < MR):
                    act.wait_ge(mes["seg"], k - MR + 1)
                nc.scalar.activation(MS[:, j % MR, 0:2 * M], bank[2 + j % 2][:, 0:2 * M], ACT.Relu).then_inc(mes["relu"], 1)

            def rowsout(k, j, it):
                act.wait_ge(mes["seg"], k + 1)
                if not (known(k) and k < R):
                    act.wait_ge(scattered[j % R], (it * (U // R) + j // R) * 16)
                nc.scalar.activation(SD[:, j % R, :], bank[4 + j % 2][:, 0:RC], ACT.Copy).then_inc(mes["rowsout"], 1)

            def emit2(it, j):
                stage(STEPS, U, it, j, 0, copy2)
                stage(STEPS, U, it, j, 2, relu)
                stage(STEPS, U, it, j, 4, rowsout)
            pipeline(act, STEPS, U, 4, emit2)

            def turned(k, j, it):
                act.wait_ge(upd["turned"], k + 1)
                if not (known(k) and k < 2):
                    act.wait_ge(upd["hid"], k - 1)
                nc.scalar.activation(ST[:, j % 2, 0:2 * P], bank[j % 2][:, 0:2 * P], ACT.Copy)
                nc.scalar.activation(ST[0:D + 2, j % 2, 2 * P:3 * P], bank[j % 2][0:D + 2, 2 * P:3 * P], ACT.Copy)\
                    .then_inc(upd["copied"], 1)

            def aggout(k, j, it):
                act.wait_ge(upd["agg"], k + 1)
                if not (known(k) and k < 2):
                    act.wait_ge(upd["hid"], k - 1)
                nc.scalar.activation(NX[:, j % 2, 2 * RC:2 * RC + P], bank[2 + j % 2][:, 0:P], ACT.Copy).then_inc(upd["aggout"], 1)

            def hidout(k, j, it):
                act.wait_ge(upd["hid"], k + 1)
                if not (known(k) and k < 2):
                    act.wait_ge(upd["product"], k - 1)
                nc.scalar.activation(hidden[:, j % 2, :], bank[4 + j % 2][:, 0:P], ACT.Relu, bias=w("bn1"))\
                    .then_inc(upd["hidout"], 1)

            def emit3(it, j):
                stage(NB, UN, it, j, 0, turned)
                stage(NB, UN, it, j, 1, aggout)
                stage(NB, UN, it, j, 2, hidout)
            pipeline(act, NB, UN, 2, emit3)
            root(6)

            with act.Fori(0, LAYERS) as layer:
                nbase = layer * NB
                node_act(act, node, D + 1, nbase + TYPES)

                def gturned(k, j, it):
                    act.wait_ge(gru["turned"], nbase + k + 1)
                    if not (known(k) and k < 2):
                        act.wait_ge(gru["product"], nbase + k - 1)
                    nc.scalar.activation(ST[:, j % 2, 0:P], bank[j % 2][:, 0:P], ACT.Copy).then_inc(gru["copied"], 1)

                def gates(k, j, it):
                    act.wait_ge(gru["product"], nbase + k + 1)
                    if not (known(k) and k < 2):
                        act.wait_ge(gru["finished"], nbase + k - 1)
                    nc.scalar.activation(NX[:, j % 2, 0:2 * D], bank[2 + j % 2][:, 0:2 * D], ACT.Sigmoid)\
                        .then_inc(gru["gates"], 1)

                def tanh(k, j, it):
                    act.wait_ge(gru["add"], nbase + k + 1)
                    nc.scalar.activation(NX[:, j % 2, 4 * D:5 * D], NX[:, j % 2, 3 * D:4 * D], ACT.Tanh)\
                        .then_inc(gru["tanh"], 1)

                def gemit(it, j):
                    stage(NB, UN, it, j, 0, gturned)
                    stage(NB, UN, it, j, 1, gates)
                    stage(NB, UN, it, j, 2, tanh)
                pipeline(act, NB, UN, 2, gemit)

        @block.tensor
        def _(pe):
            pe.wait_ge(consts, 11)
            pe.wait_ge(path_f, 1)
            for q in range(2):
                nc.tensor.transpose(bank[4 + q][0:CG, 0:P], fcol[:, 2 - q, :], ident[:, :]).then_inc(path_turned, 1)
            for q, srct in enumerate((big[:, 0:SPAD], Hf[:, 0:SPAD], tmpf[:, 0:SPAD], big[:, 5 * SPAD:6 * SPAD])):
                pe.wait_ge(idx_made, 4)
                for g in range(IDXQ):
                    n = q * IDXQ + g
                    if n >= 2:
                        pe.wait_ge(idx_tabled, n - 1)
                    cols = range(4 * g, min(4 * g + 4, CG))
                    for c in cols:
                        last = nc.tensor.transpose(bank[n % 2][:, (c - 4 * g) * P:(c - 4 * g + 1) * P],
                                                   srct[:, c * P:(c + 1) * P], ident[:, :])
                    last.then_inc(idx_turned, 1)
            pe.wait_ge(idx_tabled, 4 * IDXQ)
            pe.wait_ge(w_loaded, 32)
            node_pe(pe, node, D + 1, w("qkv", D + 1), 2 * D, QKV)

            def block_of(k):
                return pe.value_load(path[0:1, k:k + 1] if known(k) else path[0:1, bass.ds(k, 1)], min_val=0, max_val=NB - 1)

            def turn(k, j, it):
                pe.wait_ge(att["onehot"], k + 1)
                if not (known(k) and k < 2):
                    pe.wait_ge(att["copied"], k - 1)
                nc.tensor.transpose(bank[j % 2][:, 0:P], OH[:, j % OHR, :], ident[:, :]).then_inc(att["turned"], 1)

            def query(k, j, it):
                b = block_of(k)
                pe.wait_ge(att["copied"], k + 1)
                if not (known(k) and k < 2):
                    pe.wait_ge(att["score"], k - 1)
                nc.tensor.matmul(bank[2 + j % 2][:, 0:D], OT[:, j % 2, 0:P], big_kv[:, bass.ds(b * KV, D)],
                                 start=True, stop=True).then_inc(att["query"], 1)

            def seg(k, j, it):
                pe.wait_ge(att["msg"], k + 1)
                if not (known(k) and k < 2):
                    pe.wait_ge(att["summed"], k - 1)
                nc.tensor.matmul(bank[4 + j % 2][:, 0:AC], OH[:, j % OHR, :], MS[:, j % MR, 0:AC],
                                 start=True, stop=True).then_inc(att["seg"], 1)

            pe.wait_ge(path_loaded, 16)
            pe.wait_ge(pass_begun, 1)

            def emit(it, j):
                stage(STEPS, U, it, j, 0, turn)
                stage(STEPS, U, it, j, 1, query)
                stage(STEPS, U, it, j, 4, seg)
            pipeline(pe, STEPS, U, 4, emit)
            node_pe(pe, node, D + 1, w("attn", D + 1), D, ATTN)
            plain_pe(pe, plain, NIT, 0)
            node_pe(pe, node, D + 1, w("conv", D + 1), D, CONV)
            node_pe(pe, node, D + 1, w("pair", D + 1), 2 * M, PAIR)

            def keyrow(k, j, it):
                pe.wait_ge(mes["keys"], it * 2 + j // HALF + 1)
                if not (known(k) and k < 1):
                    pe.wait_ge(mes["equal"], k)
                nc.tensor.transpose(bank[7][:, 0:P], keyslot[:, j:j + 1].to_broadcast([P, P]), ident[:, :])\
                    .then_inc(mes["keyrow"], 1)

            def turn2(k, j, it):
                pe.wait_ge(mes["onehot"], k + 1)
                pe.wait_ge(gathered[j], (2 * NIT + it + 1) * 16)
                pe.wait_ge(edge_loaded[j % HALF], (it * 2 + j // HALF + 1) * 16)
                if not (known(k) and k < 2):
                    pe.wait_ge(mes["copied"], k - 1)
                nc.tensor.transpose(bank[j % 2][:, P:2 * P], OH[:, j % OHR, :], ident[:, :])
                nc.tensor.transpose(bank[j % 2][:, 0:P], G[:, j, 0:2 * D], ident[:, :]).then_inc(mes["turned"], 1)

            def pre(k, j, it):
                b = block_of(k)
                pe.wait_ge(mes["copied"], k + 1)
                if not (known(k) and k < 2):
                    pe.wait_ge(mes["relu"], k - 1)
                nc.tensor.matmul(bank[2 + j % 2][:, 0:2 * M], OT[:, j % 2, 0:P], w("edge"), start=True, stop=False)
                nc.tensor.matmul(bank[2 + j % 2][:, 0:2 * M], OT[:, j % 2, P:2 * P], big[:, bass.ds(b * 2 * M, 2 * M)],
                                 start=False, stop=True).then_inc(mes["pre"], 1)

            def seg2(k, j, it):
                pe.wait_ge(mes["relu"], k + 1)
                pe.wait_ge(mes["equal"], k + 1)
                if not (known(k) and k < 1):
                    pe.wait_ge(mes["summed"], k)
                if not (known(k) and k < 2):
                    pe.wait_ge(mes["rowsout"], k - 1)
                nc.tensor.matmul(bank[6][:, 0:M], OH[:, j % OHR, :], MS[:, j % MR, 0:M], start=True, stop=True)
                nc.tensor.matmul(bank[4 + j % 2][:, 0:RC], EQ[:, j % MR, :], MS[:, j % MR, M:M + RC],
                                 start=True, stop=True).then_inc(mes["seg"], 1)

            pe.wait_ge(pass_begun, 2)

            def emit2(it, j):
                stage(STEPS, U, it, j, 0, keyrow)
                stage(STEPS, U, it, j, 0, turn2)
                stage(STEPS, U, it, j, 1, pre)
                stage(STEPS, U, it, j, 3, seg2)
            pipeline(pe, STEPS, U, 3, emit2)

            def uturn(k, j, it):
                pe.wait_ge(upd["rows"], k + 1)
                if not (known(k) and k < 2):
                    pe.wait_ge(upd["copied"], k - 1)
                for c, width in ((0, P), (1, P), (2, D + 2)):
                    last = nc.tensor.transpose(bank[j % 2][0:width, c * P:(c + 1) * P],
                                               S[:, j % 2, c * P:c * P + width], ident[:, :])
                last.then_inc(upd["turned"], 1)

            def agg(k, j, it):
                pe.wait_ge(upd["copied"], k + 1)
                if not (known(k) and k < 2):
                    pe.wait_ge(upd["aggout"], k - 1)
                o = bank[2 + j % 2][:, 0:P]
                nc.tensor.matmul(o, w("f2"), ST[:, j % 2, 0:P], start=True, stop=False)
                nc.tensor.matmul(o, w("r2"), ST[:, j % 2, P:2 * P], start=False, stop=False)
                nc.tensor.matmul(o, w("b2", 2), ST[0:2, j % 2, 2 * P:3 * P], start=False, stop=True).then_inc(upd["agg"], 1)

            def hid(k, j, it):
                pe.wait_ge(upd["aggout"], k + 1)
                if not (known(k) and k < 2):
                    pe.wait_ge(upd["hidout"], k - 1)
                o = bank[4 + j % 2][:, 0:P]
                nc.tensor.matmul(o, w("n1a"), NX[:, j % 2, 2 * RC:2 * RC + P], start=True, stop=False)
                nc.tensor.matmul(o, w("n1b", D + 2), ST[0:D + 2, j % 2, 2 * P:3 * P], start=False, stop=True)\
                    .then_inc(upd["hid"], 1)

            def product(k, j, it):
                pe.wait_ge(upd["hidout"], k + 1)
                if not (known(k) and k < 2):
                    pe.wait_ge(upd["finished"], k - 1)
                o = bank[6 + j % 2][:, 0:D]
                nc.tensor.matmul(o, hidden[:, j % 2, :], w("n2"), start=True, stop=False)
                nc.tensor.matmul(o, ones[0:1, :], w("bn2", 1), start=False, stop=True).then_inc(upd["product"], 1)

            def emit3(it, j):
                stage(NB, UN, it, j, 0, uturn)
                stage(NB, UN, it, j, 1, agg)
                stage(NB, UN, it, j, 2, hid)
                stage(NB, UN, it, j, 3, product)
            pipeline(pe, NB, UN, 3, emit3)

            with pe.Fori(0, LAYERS) as layer:
                nbase = layer * NB
                node_pe(pe, node, D + 1, w("types", D + 1), KT * D, nbase + TYPES)
                plain_pe(pe, plain, layer * NIT + 3 * NIT, layer * STEPS + STEPS)

                def gturn(k, j, it):
                    pe.wait_ge(gru["rows"], nbase + k + 1)
                    if not (known(k) and k < 2):
                        pe.wait_ge(gru["copied"], nbase + k - 1)
                    nc.tensor.transpose(bank[j % 2][:, 0:P], S[:, j % 2, 0:P], ident[:, :]).then_inc(gru["turned"], 1)

                def gmul(k, j, it):
                    pe.wait_ge(gru["copied"], nbase + k + 1)
                    if not (known(k) and k < 2):
                        pe.wait_ge(gru["add"], nbase + k - 1)
                    o = bank[2 + j % 2][:, 0:4 * D]
                    nc.tensor.matmul(o, ST[:, j % 2, 0:P], w("gru"), start=True, stop=False)
                    nc.tensor.matmul(o, ones[0:1, :], w("gb0", 1), start=False, stop=False)
                    nc.tensor.matmul(o, ones[0:1, :], w("gb1", 1), start=False, stop=True).then_inc(gru["product"], 1)

                def gemit(it, j):
                    stage(NB, UN, it, j, 0, gturn)
                    stage(NB, UN, it, j, 1, gmul)
                pipeline(pe, NB, UN, 1, gemit)

        @block.vector
        def _(v):
            done = [0]

            def link(ins):
                done[0] += 1
                ins.then_inc(chain, 1)
                v.wait_ge(chain, done[0])

            def bc(t):
                return t.unsqueeze(2).to_broadcast([P, NB, D])

            def vec(n):
                return lng[:, n, :].unsqueeze(1).to_broadcast([P, NB, D])

            roots = [0]

            def root(src):
                roots[0] += 1
                src.then_inc(root_in, 1)
                v.wait_ge(root_out, roots[0])

            def layer_norm(src, dst, relu):
                link(nc.vector.reduce_sum(small[:, 0, :], src, AXX))
                link(nc.vector.tensor_scalar(small[:, 1, :], small[:, 0, :], 1.0 / D, None, ALU.mult))
                link(nc.vector.tensor_tensor(dst, src, bc(small[:, 1, :]), ALU.subtract))
                link(nc.vector.tensor_tensor(tmp_, dst, dst, ALU.mult))
                link(nc.vector.reduce_sum(small[:, 2, :], tmp_, AXX))
                root(nc.vector.tensor_scalar(small[:, 3, :], small[:, 2, :], 1.0 / D, EPS, ALU.mult, ALU.add))
                link(nc.vector.reciprocal(small[:, 1, :], small[:, 0, :]))
                link(nc.vector.tensor_tensor(dst, dst, bc(small[:, 1, :]), ALU.mult))
                if relu:
                    link(nc.vector.tensor_scalar(dst, dst, 0.0, None, ALU.max))

            nc.vector.memset(acc[:, :], 0.0).then_inc(acc_zero, 1)
            v.wait_ge(dst_loaded, 16)
            v.wait_ge(consts, 5)
            blocks = big[:, SPAD:SPAD + T].bitcast(I32)
            link(nc.vector.tensor_scalar(blocks, big[:, 0:T].bitcast(I32), 7, None, ALU.arith_shift_right))
            numbers = G[:, 0:14, 0:KV + 1].rearrange("p a b -> p (a b)")[:, 0:T].bitcast(I32)
            last_step = big[:, 0:T]
            link(nc.vector.tensor_tensor(last_step, blocks, numbers, ALU.add))
            link(nc.vector.tensor_copy(fcol[:, 0, :], icol[:, :]))
            before = big[:, SPAD:SPAD + T]
            for c in range(CG):
                link(nc.vector.tensor_scalar(before, last_step, fcol[:, 0, c:c + 1], None, ALU.is_lt))
                link(nc.vector.reduce_sum(fcol[:, 1, c:c + 1], before, AXX))
            nc.vector.tensor_copy(tcol[:, :], fcol[:, 1, :]).then_inc(tiles_known, 1)
            link(nc.vector.tensor_tensor(fcol[:, 2, :], fcol[:, 0, :], fcol[:, 1, :], ALU.subtract))
            nc.vector.tensor_scalar(fcol[:, 3, :], fcol[:, 2, :], float(P), None, ALU.mult).then_inc(path_f, 1)
            for q in range(2):
                v.wait_ge(path_turned, q + 1)
                nc.vector.tensor_copy(pcol[:, q, :], bank[4 + q][0:CG, 0:P]).then_inc(path_copied, 1)

            v.wait_ge(consts, 11)
            nc.vector.tensor_copy(iota[:, :], tsrci[:, 0:P])
            nc.vector.memset(S[:, :, :], 1.0)
            nc.vector.memset(MS[:, :, :], 1.0)
            link(nc.vector.tensor_copy(trash[:, :], idx[:, 0:1]))

            v.wait_ge(x_loaded, 16)
            v.wait_ge(tiles_read, 1)
            v.wait_ge(path_f, 1)
            rowsi = [big[:, (2 + q) * SPAD:(3 + q) * SPAD].bitcast(I32) for q in range(3)]
            dst, valid, local, rtrash = (big[:, q * SPAD:(q + 1) * SPAD] for q in (5, 6, 0, 1))
            srcf, tsrcf = Hf[:, 0:SPAD], tmpf[:, 0:SPAD]
            link(nc.vector.tensor_copy(dst, rowsi[0]))
            link(nc.vector.tensor_copy(srcf, rowsi[1]))
            link(nc.vector.tensor_copy(rtrash, srci[:, :]))
            link(nc.vector.tensor_copy(tsrcf, rowsi[2]))
            for c in range(CG):
                link(nc.vector.tensor_scalar(local[:, c * P:(c + 1) * P], dst[:, c * P:(c + 1) * P], fcol[:, 3, c:c + 1], None,
                                             ALU.subtract))
            link(nc.vector.tensor_scalar(valid, dst, float(N), None, ALU.is_lt))
            link(nc.vector.scalar_tensor_tensor(out=valid, in0=local, scalar=0.0, in1=valid, op0=ALU.is_ge, op1=ALU.mult))
            link(nc.vector.scalar_tensor_tensor(out=valid, in0=local, scalar=float(P - 1), in1=valid, op0=ALU.is_le, op1=ALU.mult))
            link(nc.vector.scalar_tensor_tensor(out=tsrcf, in0=tsrcf, scalar=float(NPAD), in1=srcf, op0=ALU.mult, op1=ALU.add))
            keyf = dst
            link(nc.vector.tensor_tensor(keyf, srcf, rtrash, ALU.subtract))
            link(nc.vector.tensor_tensor(keyf, keyf, valid, ALU.mult))
            link(nc.vector.tensor_tensor(keyf, keyf, rtrash, ALU.add))
            nc.vector.memset(hold2[:, :], 0.0).then_inc(idx_made, 4)
            for q, to in enumerate((dloc, srci, tsrci, key)):
                for g in range(IDXQ):
                    v.wait_ge(idx_turned, q * IDXQ + g + 1)
                    lo, hi = g * 4 * P, min((g + 1) * 4 * P, SPAD)
                    nc.vector.tensor_copy(to[:, lo:hi], bank[(q * IDXQ + g) % 2][:, 0:hi - lo]).then_inc(idx_tabled, 1)
            v.wait_ge(idx_tabled, 4 * IDXQ)

            layer_norm(X_, H_, True)
            link(nc.vector.memset(big_kv.rearrange("p (b d) -> p b d", d=KV)[:, :, KV - 1:KV], 1.0))
            node_dve(v, node, lambda k: part(Hf, k, D),
                     lambda k, ps: nc.vector.tensor_copy(part(big_kv, k, KV, 0, 2 * D), ps[:, 0:2 * D]), QKV)
            v.wait_ge(node["finished"], QKV + NB)
            nc.vector.memset(hold2[:, :], 0.0).then_inc(table_ready, 1)
            v.wait_ge(table_ready, 1)
            v.wait_ge(reverse_zero, 16 * R)
            v.wait_ge(path_loaded, 16)
            link(nc.vector.memset(hold2[:, :], 0.0))
            nc.vector.memset(hold2[:, :], 0.0).then_inc(pass_begun, 1)
            v.wait_ge(pass_begun, 1)

            hot, add = onehot(v, att, 0), sum_up(v, att, 0, AC, bank[4:6])

            def score(k, j, it):
                v.wait_ge(gathered[j], (it + 1) * 16)
                v.wait_ge(att["query"], k + 1)
                if not (known(k) and k < MR):
                    v.wait_ge(att["exp"], k - MR + 1)
                if not (known(k) and k < 2):
                    v.wait_ge(att["score"], k - 1)
                nc.vector.tensor_tensor_reduce(prod[:, j % 2, 0:D], bank[2 + j % 2][:, 0:D], G[:, j, 0:D], 1.0 / D ** 0.5, 0.0,
                                               ALU.mult, ALU.add, sc[:, 0, j % MR:j % MR + 1]).then_inc(att["score"], 1)

            def clip(k, j, it):
                v.wait_ge(att["score"], k + 1)
                nc.vector.tensor_scalar(sc[:, 1, j % MR:j % MR + 1], sc[:, 0, j % MR:j % MR + 1], 5.0, -5.0,
                                        ALU.min, ALU.max).then_inc(att["clipped"], 1)

            def emit(it, j):
                stage(STEPS, U, it, j, 0, hot)
                stage(STEPS, U, it, j, 2, score)
                stage(STEPS, U, it, j, 5, add)
                stage(STEPS, U, it, j, 2, clip)
            pipeline(v, STEPS, U, 5, emit)
            v.wait_ge(att["summed"], STEPS)

            sums = acc_[AC].rearrange("p (b d) -> p b d", d=AC)
            link(nc.vector.tensor_copy(deg[:, :], sums[:, :, D + 1]))
            link(nc.vector.tensor_scalar(small[:, 2, :], sums[:, :, D], TINY, None, ALU.max))
            link(nc.vector.reciprocal(small[:, 1, :], small[:, 2, :]))
            link(nc.vector.tensor_tensor(tmp_, sums[:, :, 0:D], bc(small[:, 1, :]), ALU.mult))
            root(nc.vector.tensor_scalar(small[:, 3, :], deg[:, :], 1.0, None, ALU.max))
            link(nc.vector.reciprocal(norm[:, :], small[:, 0, :]))
            node_dve(v, node, lambda k: part(tmpf, k, D),
                     lambda k, ps: nc.vector.tensor_tensor(part(Hf, k, D), part(Hf, k, D), ps[:, 0:D], ALU.add), ATTN)
            v.wait_ge(node["finished"], ATTN + NB)
            layer_norm(H_, H_, False)
            link(nc.vector.tensor_tensor(H_, H_, vec(0), ALU.mult))
            link(nc.vector.tensor_tensor(H_, H_, vec(1), ALU.add))
            link(nc.vector.tensor_tensor(X_, X_, H_, ALU.add))

            layer_norm(X_, H_, True)
            nc.vector.tensor_tensor(tmp_, H_, bc(norm[:, :]), ALU.mult).then_inc(table_ready, 1)
            link(nc.vector.memset(acc_[D], 0.0))
            plain_dve(v, plain, 0)
            v.wait_ge(plain["summed"], STEPS)
            v.wait_ge(table_stored, 32)
            node_dve(v, node, lambda k: part(acc_[D], k, D),
                     lambda k, ps: nc.vector.tensor_copy(part(tmpf, k, D), ps[:, 0:D]), CONV)
            v.wait_ge(node["finished"], CONV + NB)
            link(nc.vector.tensor_tensor(tmp_, tmp_, bc(norm[:, :]), ALU.mult))
            link(nc.vector.tensor_tensor(tmp_, tmp_, vec(2), ALU.add))
            link(nc.vector.tensor_tensor(X_, X_, tmp_, ALU.add))

            layer_norm(X_, H_, True)
            nc.vector.memset(hold2[:, :], 0.0).then_inc(table_ready, 1)
            v.wait_ge(table_ready, 3)
            link(nc.vector.memset(acc_[M], 0.0))
            node_dve(v, node, lambda k: part(Hf, k, D),
                     lambda k, ps: nc.vector.tensor_copy(part(big[:, :], k, 2 * M), ps[:, 0:2 * M]), PAIR)
            v.wait_ge(node["finished"], PAIR + NB)
            link(nc.vector.memset(MS[:, :, 2 * M:2 * M + 1], 1.0))
            nc.vector.memset(hold2[:, :], 0.0).then_inc(pass_begun, 1)
            v.wait_ge(pass_begun, 2)
            hot2, add2 = onehot(v, mes, 0), sum_up(v, mes, 0, M, (bank[6], bank[6]))

            def keys(k, j, it):
                if j % HALF:
                    return
                if not (known(k) and k < U):
                    v.wait_ge(mes["keyrow"], k - HALF)
                    v.wait_ge(mes["rep"], k - HALF)
                nc.vector.tensor_scalar(keyless[:, j:j + HALF], part(key[:, :], k, 1, 0, HALF), trash[:, 0:1], None,
                                        ALU.subtract).then_inc(mes["less"], 1)
                nc.vector.tensor_copy(keyslot[:, j:j + HALF], part(key[:, :], k, 1, 0, HALF)).then_inc(mes["keys"], 1)

            def equal(k, j, it):
                v.wait_ge(mes["keyrow"], k + 1)
                if not (known(k) and k < MR):
                    v.wait_ge(mes["seg"], k - MR + 1)
                nc.vector.tensor_scalar(EQ[:, j % MR, :], bank[7][:, 0:P], part(key[:, :], k, 1), None,
                                        ALU.is_equal).then_inc(mes["equal"], 1)

            def count(k, j, it):
                v.wait_ge(mes["equal"], k + 1)
                if not (known(k) and k < 2):
                    v.wait_ge(mes["rep"], k - 1)
                nc.vector.tensor_tensor_reduce(prod[:, j % 2, :], EQ[:, j % MR, :], earlier[:, :], 1.0, 0.0, ALU.mult, ALU.add,
                                               cnt[:, 0, j % 2:j % 2 + 1]).then_inc(mes["count"], 1)

            def rep(k, j, it):
                v.wait_ge(mes["count"], k + 1)
                v.wait_ge(mes["less"], it * 2 + j // HALF + 1)
                if not (known(k) and k < 2):
                    v.wait_ge(mes["index"], k - 1)
                nc.vector.tensor_scalar(cnt[:, 1, j % 2:j % 2 + 1], cnt[:, 0, j % 2:j % 2 + 1], 0.0,
                                        keyless[:, j:j + 1], ALU.is_equal, ALU.mult).then_inc(mes["rep"], 1)

            def index(k, j, it):
                v.wait_ge(mes["rep"], k + 1)
                if not (known(k) and k < U):
                    v.wait_ge(scattered[j % R], (it * (U // R) + j // R - U // R + 1) * 16)
                nc.vector.tensor_scalar(sidx[:, j:j + 1], cnt[:, 1, j % 2:j % 2 + 1], trash[:, 0:1], None,
                                        ALU.add).then_inc(mes["index"], 1)

            def emit2(it, j):
                stage(STEPS, U, it, j, 0, keys)
                stage(STEPS, U, it, j, 0, hot2)
                stage(STEPS, U, it, j, 1, equal)
                stage(STEPS, U, it, j, 2, rep)
                stage(STEPS, U, it, j, 1, count)
                stage(STEPS, U, it, j, 4, add2)
                stage(STEPS, U, it, j, 2, index)
            pipeline(v, STEPS, U, 4, emit2)
            v.wait_ge(mes["summed"], STEPS)

            def urows(k, j, it):
                r = j % 2
                if not (known(k) and k < 2):
                    v.wait_ge(upd["turned"], k - 1)
                nc.vector.tensor_copy(S[:, r, 0:M], part(acc_[M], k, M))
                nc.vector.tensor_copy(S[:, r, 2 * M + 2:2 * M + 2 + D], part(Hf, k, D))
                nc.vector.tensor_copy(S[:, r, 2 * M + 1:2 * M + 2], part(deg[:, :], k, 1))
                v.wait_ge(rev_loaded[r], (k // 2 + 1) * (16 * R) if known(k) else (it * (UN // 2) + j // 2 + 1) * (16 * R))
                if not (known(k) and k < 2):
                    v.wait_ge(upd["rows"], k - 1)
                nc.vector.tensor_tensor(NX[:, r, 0:RC], revs[:, r, 0, :], revs[:, r, 1, :], ALU.add).then_inc(upd["sums"], 1)
                nc.vector.tensor_tensor(NX[:, r, RC:2 * RC], revs[:, r, 2, :], revs[:, r, 3, :], ALU.add).then_inc(upd["sums"], 1)
                v.wait_ge(upd["sums"], k * 2 + 2)
                nc.vector.tensor_tensor(S[:, r, M:M + RC], NX[:, r, 0:RC], NX[:, r, RC:2 * RC], ALU.add).then_inc(upd["rows"], 1)

            def uend(k, j, it):
                v.wait_ge(upd["product"], k + 1)
                nc.vector.tensor_copy(part(tmpf, k, D), bank[6 + j % 2][:, 0:D]).then_inc(upd["finished"], 1)

            def uemit(it, j):
                stage(NB, UN, it, j, 0, urows)
                stage(NB, UN, it, j, 4, uend)
            pipeline(v, NB, UN, 4, uemit)
            v.wait_ge(upd["finished"], NB)
            link(nc.vector.tensor_tensor(tmp_, tmp_, H_, ALU.add))
            link(nc.vector.tensor_tensor(X_, X_, tmp_, ALU.add))
            layer_norm(X_, H_, True)
            link(nc.vector.memset(S[:, :, :], 1.0))

            with v.Fori(0, LAYERS) as layer:
                nbase = layer * NB
                node_dve(v, node, lambda k: part(Hf, k, D),
                         lambda k, ps: nc.vector.tensor_copy(part(big[:, :], k, KT * D), ps[:, 0:KT * D]), nbase + TYPES)
                v.wait_ge(node["finished"], nbase + (TYPES + NB))
                nc.vector.memset(acc_[D], 0.0).then_inc(gru_acc_zero, 1)
                v.wait_ge(gru_acc_zero, layer * 2 + 1)
                plain_dve(v, plain, layer * STEPS + STEPS)
                v.wait_ge(plain["summed"], layer * STEPS + 2 * STEPS)

                def grows(k, j, it):
                    if not (known(k) and k < 2):
                        v.wait_ge(gru["turned"], nbase + k - 1)
                    nc.vector.tensor_copy(S[:, j % 2, D:2 * D], part(Hf, k, D))
                    nc.vector.tensor_copy(S[:, j % 2, 0:D], part(acc_[D], k, D)).then_inc(gru["rows"], 1)

                def gate(k, j, it):
                    r = j % 2
                    v.wait_ge(gru["gates"], nbase + k + 1)
                    nc.vector.tensor_tensor(NX[:, r, 2 * D:3 * D], NX[:, r, 0:D], bank[2 + r][:, 3 * D:4 * D], ALU.mult)\
                        .then_inc(gru["mul"], 1)
                    v.wait_ge(gru["mul"], nbase + k + 1)
                    nc.vector.tensor_tensor(NX[:, r, 3 * D:4 * D], NX[:, r, 2 * D:3 * D], bank[2 + r][:, 2 * D:3 * D], ALU.add)\
                        .then_inc(gru["add"], 1)

                def blend(k, j, it):
                    r = j % 2
                    v.wait_ge(gru["tanh"], nbase + k + 1)
                    nc.vector.tensor_tensor(NX[:, r, 5 * D:6 * D], part(Hf, k, D), NX[:, r, 4 * D:5 * D], ALU.subtract)\
                        .then_inc(gru["diff"], 1)
                    v.wait_ge(gru["diff"], nbase + k + 1)
                    nc.vector.tensor_tensor(NX[:, r, 6 * D:7 * D], NX[:, r, D:2 * D], NX[:, r, 5 * D:6 * D], ALU.mult)\
                        .then_inc(gru["blend"], 1)
                    v.wait_ge(gru["blend"], nbase + k + 1)
                    nc.vector.tensor_tensor(part(Hf, k, D), NX[:, r, 4 * D:5 * D], NX[:, r, 6 * D:7 * D], ALU.add)\
                        .then_inc(gru["finished"], 1)

                def gemit(it, j):
                    stage(NB, UN, it, j, 0, grows)
                    stage(NB, UN, it, j, 2, gate)
                    stage(NB, UN, it, j, 3, blend)
                pipeline(v, NB, UN, 3, gemit)
                v.wait_ge(gru["finished"], nbase + NB)
                nc.vector.memset(S[:, :, D:D + 1], 1.0).then_inc(gru_acc_zero, 1)
                v.wait_ge(gru_acc_zero, layer * 2 + 2)
            nc.vector.tensor_tensor(X_, X_, H_, ALU.add).then_inc(result, 1)


def pack(i):
    import numpy as np
    g = {k: np.asarray(v) for k, v in i.items()}
    W = np.zeros((P, WTOTAL), np.float32)

    def put(name, block, row=0, col=0):
        lo = WCOLS[name][0] + col
        W[row:row + block.shape[0], lo:lo + block.shape[1]] = block

    put("qkv", g["L0_gnn_qk_w"].T)
    put("qkv", g["L0_gnn_v_w"].T, col=D)
    put("qkv", g["L0_gnn_qk_b"][None], row=D)
    put("qkv", g["L0_gnn_v_b"][None], row=D, col=D)
    put("attn", g["L0_gnn_o_w"].T)
    put("attn", g["L0_gnn_o_b"][None], row=D)
    put("conv", g["L1_gnn_weight"])
    f, r = g["L2_gnn_W1_f"], g["L2_gnn_W1_r"]
    put("pair", f[D:2 * D])
    put("pair", r[0:D], col=M)
    put("pair", g["L2_gnn_b1_f"][None], row=D)
    put("pair", g["L2_gnn_b1_r"][None], row=D, col=M)
    put("edge", f[0:D])
    put("edge", r[D:2 * D], col=M)
    put("edge", f[2 * D:], row=D)
    put("edge", r[2 * D:], row=D, col=M)
    put("f2", g["L2_gnn_W2_f"])
    put("r2", g["L2_gnn_W2_r"])
    put("b2", g["L2_gnn_b2_r"][None])
    put("b2", g["L2_gnn_b2_f"][None], row=1)
    put("n1a", g["L2_gnn_Wn1"][0:M])
    put("n1b", g["L2_gnn_Wn1"][M:], row=2)
    put("bn1", g["L2_gnn_bn1"][:, None])
    put("n2", g["L2_gnn_Wn2"])
    put("bn2", g["L2_gnn_bn2"][None])
    for t in range(KT):
        put("types", g["L3_gnn_W"][t].T, col=t * D)
        put("types", g["L3_gnn_b"][t][None], row=D, col=t * D)
    ih, hh = g["L3_gnn_w_ih"].T, g["L3_gnn_w_hh"].T
    put("gru", ih)
    put("gru", hh[:, 0:2 * D], row=D)
    put("gru", hh[:, 2 * D:], row=D, col=3 * D)
    put("gb0", g["L3_gnn_b_ih"][None])
    put("gb1", g["L3_gnn_b_hh"][None, 0:2 * D])
    put("gb1", g["L3_gnn_b_hh"][None, 2 * D:], col=3 * D)
    vectors = np.concatenate([g["L0_gnn_ln_g"], g["L0_gnn_ln_b"], g["L1_gnn_bias"]])
    return W, vectors


def kernel(**inputs):
    import numpy as np
    import concourse.bacc as bacc
    from concourse.bass_utils import run_bass_kernel_spmd

    def tiles(name, fill):
        a = np.full(((T + 1) * P,), fill, np.int32)
        a[:E] = np.asarray(inputs[name])
        return a.reshape(T + 1, P)

    x = np.zeros((NPAD, D), np.float32)
    x[:N] = np.asarray(inputs["x"])
    edge = np.zeros(((T + 1) * P, D), np.float32)
    edge[:E] = np.asarray(inputs["edge_attr_64"])
    dst = tiles("dst", PADDST)
    W, vectors = pack(inputs)
    arrays = {"x": x, "src": tiles("src", 0), "dst": dst, "type": tiles("edge_type_4", 0), "edge": edge,
              "dst_last": np.ascontiguousarray(dst[:T, P - 1]), "weights": W, "vectors": vectors}
    nc = bacc.Bacc("TRN2", target_bir_lowering=False, num_devices=1)
    aps = {n: nc.dram_tensor(f"in_{n}", v.shape, mybir.dt.from_np(v.dtype), kind="ExternalInput").ap()
           for n, v in arrays.items()}
    out = nc.dram_tensor("out_0", (N, D), F32, kind="ExternalOutput").ap()
    build(nc, aps, out)
    r = run_bass_kernel_spmd(nc, [{f"in_{n}": v for n, v in arrays.items()}], core_ids=[0])
    return r.results[0]["out_0"]
```

```python
from contextlib import ExitStack

import concourse.bass as bass
from concourse import mybir

P = 128
N = 6250
D = 64
E = 206250
NB = -(-N // P)
NPAD = NB * P
T = -(-E // P)
STEPS = T + NB - 1
CG = -(-STEPS // P)
SPAD = CG * P
M = 128
KT = 4
LAYERS = 4
KV = 2 * D + 1
AC = D + 2
RC = M + 1
R = 4
TRASH = NPAD
RROWS = NPAD + P
SLOTS = 40
HS = SLOTS // 2
ROUNDS = (-(-STEPS // SLOTS), STEPS // SLOTS)
TURNS = sum(ROUNDS)
HALF = 10
HOT = 20
GR = 4
NG = STEPS // GR
U = 40
UP = 40
UGR = UP // GR
UN = 6
OHG = HOT // GR
MR = 4
EPS = 1e-5
TINY = 1e-30
PADDST = NPAD - 1
IDXQ = -(-CG // 4)
assert STEPS % HS == 0 and STEPS % SLOTS and HS % GR == 0 and U == UP == SLOTS and U % HALF == 0 and UGR % 2 == 0

F32 = mybir.dt.float32
I32 = mybir.dt.int32
I16 = mybir.dt.int16
ALU = mybir.AluOpType
ACT = mybir.ActivationFunctionType
AXX = mybir.AxisListType.X

WCOLS = {}
_at = 0
for _n, _w in (("qkv", 2 * D), ("attn", D), ("conv", D), ("pair", 2 * M), ("edge", 2 * M), ("f2", M), ("r2", M),
               ("n1a", M), ("n1b", M), ("n2", D), ("types", KT * D), ("gru", 4 * D), ("b2", M), ("bn1", 1),
               ("bn2", D), ("gb0", 4 * D), ("gb1", 4 * D)):
    WCOLS[_n] = (_at, _at + _w)
    _at += _w
WTOTAL = _at


def known(k):
    return isinstance(k, int)


def pipeline(eng, n, unroll, lag, emit):
    for j in range(unroll):
        emit(0, j)
    with eng.Fori(1, n // unroll) as it:
        for j in range(unroll):
            emit(it, j)
    for i in range(n // unroll * unroll, n + lag):
        emit(i // unroll, i % unroll)


def stage(n, unroll, it, j, lag, body):
    k, slot, kit = it * unroll + (j - lag), (j - lag) % unroll, it + (j - lag) // unroll
    if known(k) and not 0 <= k < n:
        return
    body(k, slot, kit)


def build(nc, a, out):
    ctx = ExitStack()
    with ctx:
        def sb(name, shape, dt=F32):
            return ctx.enter_context(nc.sbuf_tensor(name, shape, dt))

        def sem(name):
            return ctx.enter_context(nc.semaphore(name))

        def dram(name, shape, dt=F32):
            return nc.dram_tensor(name, shape, dt).ap()

        kv_table = dram("kv_table", (NPAD, KV))
        h_table = dram("h_table", (NPAD, D))
        type_table = dram("type_table", (KT * NPAD, D))
        reverse = [dram(f"reverse{r}", (RROWS, RC)) for r in range(R)]
        path_rows = dram("path_rows", (2 * CG, P), I32)

        X = sb("X", [P, NB, D])
        H = sb("H", [P, NB, D])
        tmp = sb("tmp", [P, NB, D])
        acc = sb("acc", [P, 50 * RC])
        big = sb("big", [P, NB * 2 * M])
        small = sb("small", [P, 4, NB])
        norm = sb("norm", [P, NB])
        deg = sb("deg", [P, NB])
        dloc = sb("dloc", [P, SPAD], I16)
        key = sb("key", [P, SPAD])
        srci = sb("srci", [P, SPAD], I16)
        tsrci = sb("tsrci", [P, SPAD], I16)
        path = sb("path", [1, 2 * SPAD], I32)
        icol = sb("icol", [P, CG], I32)
        fcol = sb("fcol", [P, 4, CG])
        tcol = sb("tcol", [P, CG], I32)
        pcol = sb("pcol", [CG, 2, P], I32)
        ident = sb("ident", [P, P])
        iota = sb("iota", [P, P])
        earlier = sb("earlier", [P, P])
        trash = sb("trash", [P, 1])
        ones = sb("ones", [1, P])
        hold_in = sb("hold_in", [P, 1])
        hold_out = sb("hold_out", [P, 1])
        scatter_hold = sb("scatter_hold", [P, 1])
        types_hold = sb("types_hold", [P, 1])
        hold2 = sb("hold2", [P, 1])
        hidden = sb("hidden", [P, 2, P])
        idx = sb("idx", [P, SLOTS], I32)
        G = sb("G", [P, SLOTS, KV])
        OH = sb("OH", [P, HOT, P])
        OT = sb("OT", [P, 2, GR * P])
        prod = sb("prod", [P, 2, P])
        sc = sb("sc", [P, 3, 2, GR])
        MS = sb("MS", [P, MR, 2 * M + 2])
        EQ = sb("EQ", [P, MR, P])
        cnt = sb("cnt", [P, 2, MR])
        sidx = sb("sidx", [P, U], I32)
        SD = sb("SD", [P, R, RC])
        keyslot = sb("keyslot", [P, U])
        keyless = sb("keyless", [P, U])
        S = sb("S", [P, 2, 3 * M])
        ST = OT[:, :, 0:3 * P]
        NX = sb("NX", [P, 2, 4 * M])
        Gf = G[:, :, :].rearrange("p a b -> p (a b)")
        itile, irtrash, iiota = (Gf[:, lo:hi].bitcast(I32) for lo, hi in ((0, T), (T, T + SPAD), (T + SPAD, T + SPAD + P)))
        revs = Gf[:, 0:2 * R * RC].rearrange("p (s r c) -> p s r c", s=2, r=R)
        W = sb("W", [P, WTOTAL])
        lng = sb("lng", [P, 3, D])
        bank = [ctx.enter_context(nc.psum_tensor(f"bank{i}", [P, 512], F32)) for i in range(8)]

        def w(name, rows=P):
            lo, hi = WCOLS[name]
            return W[0:rows, lo:hi]

        messages = MS[:, :, :].rearrange("p a b -> p (a b)")[:, 0:2 * GR * AC].rearrange("p (s n c) -> p s n c", s=2, n=GR)
        acc_ = {c: acc[:, 0:NB * c] for c in (AC, D, M)}
        big_kv = big[:, 0:NB * KV]
        X_, H_, tmp_ = X[:, :, :], H[:, :, :], tmp[:, :, :]
        flat = {id(t): t.rearrange("p b d -> p (b d)") for t in (X_, H_, tmp_)}
        Xf, Hf, tmpf = (flat[id(t)] for t in (X_, H_, tmp_))

        def part(t, k, width, lo=0, hi=None):
            hi = width if hi is None else hi
            if known(k):
                return t[:, k * width + lo:k * width + hi]
            return t[:, bass.ds(k * width + lo, hi - lo)]

        x_loaded, dst_loaded, w_loaded, reverse_zero = (sem(n) for n in ("x_loaded", "dst_loaded", "w_loaded", "reverse_zero"))
        acc_zero, consts, path_f, tiles_known = (sem(n) for n in ("acc_zero", "consts", "path_f", "tiles_known"))
        tiles_read = sem("tiles_read")
        path_turned, path_copied, path_stored, path_loaded = (sem(n) for n in ("path_turned", "path_copied", "path_stored", "path_loaded"))
        idx_made, idx_turned, idx_tabled = (sem(n) for n in ("idx_made", "idx_turned", "idx_tabled"))
        chain = sem("chain")
        root_in, root_out = sem("root_in"), sem("root_out")
        table_ready, table_stored = sem("table_ready"), sem("table_stored")
        gathered = [sem(f"gathered{j}") for j in range(UGR)]
        tile_rows = [sem(f"tile_rows{q}") for q in range(3)]
        edge_loaded = [sem(f"edge_loaded{j}") for j in range(HALF)]
        scattered = [sem(f"scattered{r}") for r in range(R)]
        idx_copied, scatter_go = sem("idx_copied"), sem("scatter_go")
        rev_loaded = [sem(f"rev_loaded{r}") for r in range(2)]
        pass_begun = sem("pass_begun")
        gru_acc_zero = sem("gru_acc_zero")
        types_stored, types_go = sem("types_stored"), sem("types_go")
        result, result_stored = sem("result"), sem("result_stored")

        class Sems:
            def __init__(self, phase, names):
                self.at = {n: sem(f"{phase}_{n}") for n in names.split()}

            def __getitem__(self, n):
                return self.at[n]

        node = Sems("node", "rows turned copied product finished")
        QKV, ATTN, CONV, PAIR, TYPES = (n * NB for n in range(5))
        att = Sems("att", "onehot turned copied query score scored clipped exp msg seg summed")
        mes = Sems("mes", "less keys keyrow equal count rep index onehot turned copied pre relu seg summed rowsout")
        plain = Sems("plain", "onehot seg summed")
        upd = Sems("upd", "sums rows turned copied agg aggout hid hidout product finished")
        gru = Sems("gru", "rows turned copied product gates mul add tanh diff blend finished")

        block = ctx.enter_context(nc.Block())

        def node_pe(pe, s, rows, wt, width, base=0):
            def turn(k, j, it):
                pe.wait_ge(s["rows"], base + k + 1)
                if not (known(k) and k < 2):
                    pe.wait_ge(s["copied"], base + k - 1)
                nc.tensor.transpose(bank[j % 2][0:rows, 0:P], S[:, j % 2, 0:rows], ident[:, :]).then_inc(s["turned"], 1)

            def mul(k, j, it):
                pe.wait_ge(s["copied"], base + k + 1)
                if not (known(k) and k < 2):
                    pe.wait_ge(s["finished"], base + k - 1)
                nc.tensor.matmul(bank[2 + j % 2][:, 0:width], ST[0:rows, j % 2, 0:P], wt,
                                 start=True, stop=True).then_inc(s["product"], 1)

            def emit(it, j):
                stage(NB, UN, it, j, 0, turn)
                stage(NB, UN, it, j, 1, mul)
            pipeline(pe, NB, UN, 1, emit)

        def node_act(act, s, rows, base=0):
            def copy(k, j, it):
                act.wait_ge(s["turned"], base + k + 1)
                if not (known(k) and k < 2):
                    act.wait_ge(s["product"], base + k - 1)
                nc.scalar.activation(ST[0:rows, j % 2, 0:P], bank[j % 2][0:rows, 0:P], ACT.Copy).then_inc(s["copied"], 1)
            pipeline(act, NB, UN, 0, lambda it, j: stage(NB, UN, it, j, 0, copy))

        def node_dve(v, s, source, finish, base=0):
            def rows(k, j, it):
                if not (known(k) and k < 2):
                    v.wait_ge(s["turned"], base + k - 1)
                nc.vector.tensor_copy(S[:, j % 2, 0:D], source(k)).then_inc(s["rows"], 1)

            def end(k, j, it):
                v.wait_ge(s["product"], base + k + 1)
                finish(k, bank[2 + j % 2]).then_inc(s["finished"], 1)

            def emit(it, j):
                stage(NB, UN, it, j, 0, rows)
                stage(NB, UN, it, j, 2, end)
            pipeline(v, NB, UN, 2, emit)

        def gather(pool, before, turns, table, index, width, used, used_base, also=None, lag=0, per=1):
            def get(k, j, it):
                if j % HS == 0:
                    half = j // HS
                    copied = (turns + (it * 2 + half)) * 3
                    if not (known(k) and k < SLOTS and known(before[half]) and before[half] == 0):
                        for g in range(half * UGR // 2, (half + 1) * UGR // 2):
                            pool.wait_ge(gathered[g], (before[half] + it) * (16 * GR))
                    if not (known(k) and k < SLOTS):
                        pool.wait_ge(used, used_base + it * (UP // per) + (j - HS) // per)
                    pool.wait_ge(idx_copied, copied + 1)
                    nc.gpsimd.tensor_tensor(hold_out[:, :], hold_in[:, :], hold_in[:, :], ALU.add)\
                        .then_inc(idx_copied, 1)
                    nc.gpsimd.tensor_copy(idx[:, j:j + HS], index[:, k:k + HS] if known(k) else index[:, bass.ds(k, HS)])\
                        .then_inc(idx_copied, 1)
                    pool.wait_ge(idx_copied, copied + 3)
                    nc.gpsimd.tensor_tensor(hold_out[:, :], hold_in[:, :], hold_in[:, :], ALU.add)\
                        .then_inc(idx_copied, 1)
                nc.gpsimd.indirect_dma_start(G[:, j, 0:width], None, table,
                                             bass.IndirectOffsetOnAxis(idx[:, j:j + 1], 0))\
                    .then_inc(gathered[j // GR], 16)

            def emit(it, j):
                stage(STEPS, UP, it, j, 0, get)
                if also:
                    stage(STEPS, UP, it, j, lag, also)
            pipeline(pool, STEPS, UP, lag, emit)

        def arrived(before, j, it):
            return (before[j // (UGR // 2)] + it + 1) * (16 * GR)

        def passes(n):
            return tuple(n * r for r in ROUNDS)

        def layers(layer):
            return tuple(layer * r + 3 * r for r in ROUNDS)

        def blocks_of(eng, k):
            _, b = nc.values_load_multi_w_load_instructions(
                path[0:1, k:k + GR] if known(k) else path[0:1, bass.ds(k, GR)], engines=(eng.engine,), min_val=0, max_val=NB - 1)
            return b

        def near(eng, held, k, j):
            if known(k):
                return eng.value_load(path[0:1, k:k + 1], min_val=0, max_val=NB - 1)
            if j % GR == 0:
                held["blocks"] = blocks_of(eng, k)
            return held["blocks"][j % GR]

        def onehots(group, slot):
            n = slot * GR % HOT
            return nc.vector.tensor_tensor(
                OH[:, n:n + GR, :], iota[:, :].unsqueeze(1).to_broadcast([P, GR, P]),
                part(dloc[:, :], group, GR).unsqueeze(2).to_broadcast([P, GR, P]), ALU.is_equal)

        def hot(v, s, base):
            def body(q, j, it):
                if not (known(q) and q < OHG):
                    v.wait_ge(s["seg"], base + q - OHG + 1)
                onehots(q, j).then_inc(s["onehot"], 1)
            return body

        def sum_up(v, s, base, width, banks):
            held = {}

            def addition(n):
                def body(q, j, it):
                    if n == 0:
                        held["blocks"] = blocks_of(v, q * GR)
                        v.wait_ge(s["seg"], base + q + 1)
                    if not (known(q) and q == 0 and n == 0):
                        v.wait_ge(s["summed"], (base + q) * GR + n)
                    to = acc_[width][:, bass.ds(held["blocks"][n] * width, width)]
                    nc.vector.tensor_tensor(to, to, banks[j % 2][:, n * width:(n + 1) * width], ALU.add)\
                        .then_inc(s["summed"], 1)
                return body
            return [addition(n) for n in range(GR)]

        def plain_pe(pe, s, before, base):
            def seg(q, j, it):
                pe.wait_ge(gathered[j], arrived(before, j, it))
                pe.wait_ge(s["onehot"], base + q + 1)
                if not (known(q) and q < 2):
                    pe.wait_ge(s["summed"], (base + q - 1) * GR)
                for n in range(GR):
                    last = nc.tensor.matmul(bank[j % 2][:, n * D:(n + 1) * D], OH[:, (j * GR + n) % HOT, :],
                                            G[:, j * GR + n, 0:D],
                                            start=True, stop=True)
                last.then_inc(s["seg"], 1)
            pipeline(pe, NG, UGR, 0, lambda it, j: stage(NG, UGR, it, j, 0, seg))

        def plain_dve(v, s, base):
            one, adds = hot(v, s, base), sum_up(v, s, base, D, bank[0:2])

            def emit(it, j):
                stage(NG, UGR, it, j, 0, one)
                for add in adds:
                    stage(NG, UGR, it, j, 1, add)
            pipeline(v, NG, UGR, 1, emit)

        @block.sync
        def _(sp):
            sp.dma_start(big[:, 0:T].bitcast(I32), a["dst_last"].partition_broadcast(P)).then_inc(dst_loaded, 16)
            sp.dma_start(X_, a["x"].rearrange("(b p) d -> p b d", p=P)).then_inc(x_loaded, 16)
            sp.dma_start(W[:, :], a["weights"]).then_inc(w_loaded, 16)
            sp.dma_start(lng[:, :, :].rearrange("p a d -> p (a d)"), a["vectors"].partition_broadcast(P)).then_inc(w_loaded, 16)
            sp.wait_ge(acc_zero, 1)
            for r in range(R):
                sp.dma_start(reverse[r].rearrange("(p q) d -> p (q d)", p=P), acc[:, 0:50 * RC]).then_inc(reverse_zero, 16)
            sp.wait_ge(path_copied, 2)
            sp.dma_start(path_rows.rearrange("(a c) p -> c a p", a=2), pcol[:, :, :]).then_inc(path_stored, 16)
            sp.wait_ge(path_stored, 16)
            sp.dma_start(path[:, :], path_rows.rearrange("(o c) p -> o (c p)", o=1)).then_inc(path_loaded, 16)

            def store(table, source, n, width):
                sp.wait_ge(table_ready, n)
                sp.dma_start(table.rearrange("(b p) d -> p b d", p=P),
                             source.rearrange("p (b d) -> p b d", d=width)).then_inc(table_stored, 16)

            store(kv_table, big_kv, 1, KV)
            store(h_table, tmpf, 2, D)
            store(h_table, Hf, 3, D)

            sp.wait_ge(table_stored, 48)
            sp.wait_ge(path_loaded, 16)
            def features(k, j, it):
                t = sp.value_load(path[0:1, SPAD + k:SPAD + k + 1] if known(k) else path[0:1, bass.ds(k + SPAD, 1)],
                                  min_val=0, max_val=T)
                first = sp.snap(t * P)
                if not (known(k) and k < HALF):
                    sp.wait_ge(mes["turned"], k - HALF + 1)
                sp.dma_start(G[:, j, D:2 * D], a["edge"][bass.ds(first, P), :]).then_inc(edge_loaded[j % HALF], 16)
            pipeline(sp, STEPS, U, 0, lambda it, j: stage(STEPS, U, it, j, 0, features))

            for r in range(R):
                sp.wait_ge(scattered[r], 16 * (STEPS // R))
            def sums(k, j, it):
                first = k * P if known(k) else sp.snap(k * P)
                if not (known(k) and k < 2):
                    sp.wait_ge(upd["rows"], k - 1)
                for r in range(R):
                    sp.dma_start(revs[:, j % 2, r, :], reverse[r][bass.ds(first, P), :]).then_inc(rev_loaded[j % 2], 16)
            pipeline(sp, NB, UN, 0, lambda it, j: stage(NB, UN, it, j, 0, sums))

            with sp.Fori(0, LAYERS) as layer:
                sp.wait_ge(node["finished"], layer * NB + (TYPES + NB))
                for t in range(KT):
                    sp.dma_start(type_table[t * NPAD:(t + 1) * NPAD, :].rearrange("(b p) d -> p b d", p=P),
                                 big[:, :].rearrange("p (b d) -> p b d", d=KT * D)[:, :, t * D:(t + 1) * D])\
                        .then_inc(types_stored, 16)
            sp.wait_ge(types_stored, 16 * KT * LAYERS)
            sp.wait_ge(result, 1)
            full = N // P
            sp.dma_start(out[0:full * P, :].rearrange("(b p) d -> p b d", p=P), X[:, 0:full, :]).then_inc(result_stored, 16)
            sp.dma_start(out[full * P:N, :], X[0:N - full * P, full, :]).then_inc(result_stored, 16)
            sp.wait_ge(result_stored, 32)

        @block.gpsimd
        def _(pool):
            nc.gpsimd.iota(itile, pattern=[[1, T]], base=0, channel_multiplier=0).then_inc(consts, 1)
            nc.gpsimd.iota(icol[:, :], pattern=[[P, CG]], base=0, channel_multiplier=1).then_inc(consts, 1)
            nc.gpsimd.iota(irtrash, pattern=[[0, CG], [1, P]], base=TRASH, channel_multiplier=0).then_inc(consts, 1)
            nc.gpsimd.iota(idx[:, 0:1], pattern=[[0, 1]], base=TRASH, channel_multiplier=1).then_inc(consts, 1)
            nc.gpsimd.iota(iiota, pattern=[[1, P]], base=0, channel_multiplier=0).then_inc(consts, 1)
            nc.gpsimd.memset(ident[:, :], 0.0).then_inc(consts, 1)
            nc.gpsimd.memset(earlier[:, :], 1.0).then_inc(consts, 1)
            nc.gpsimd.memset(hold_in[:, :], 0.0).then_inc(consts, 1)
            nc.gpsimd.memset(ones[:, :], 1.0).then_inc(consts, 1)
            pool.wait_ge(consts, 9)
            nc.gpsimd.affine_select(out=ident[:, :], in_=ident[:, :], compare_op=ALU.not_equal, fill=1.0, base=0,
                                    pattern=[[-1, P]], channel_multiplier=1).then_inc(consts, 1)
            nc.gpsimd.affine_select(out=earlier[:, :], in_=earlier[:, :], compare_op=ALU.is_gt, fill=0.0, base=0,
                                    pattern=[[-1, P]], channel_multiplier=1).then_inc(consts, 1)
            nc.gpsimd.tensor_tensor(hold_out[:, :], hold_in[:, :], hold_in[:, :], ALU.add).then_inc(idx_copied, 1)

            pool.wait_ge(tiles_known, 1)
            for q, name in enumerate(("dst", "src", "type")):
                for c in range(CG):
                    lo = (2 + q) * SPAD + c * P
                    nc.gpsimd.indirect_dma_start(big[:, lo:lo + P].bitcast(I32), None, a[name],
                                                 bass.IndirectOffsetOnAxis(tcol[:, c:c + 1], 0))\
                        .then_inc(tile_rows[q], 16)
            for q in range(3):
                pool.wait_ge(tile_rows[q], 16 * CG)
            nc.gpsimd.tensor_copy(hold_in[:, :], hold_in[:, :]).then_inc(tiles_read, 1)
            pool.wait_ge(tiles_read, 1)

            pool.wait_ge(idx_tabled, 4 * IDXQ)
            pool.wait_ge(table_stored, 16)
            gather(pool, passes(0), 0, kv_table, srci, KV, att["msg"], 0, per=GR)
            pool.wait_ge(table_stored, 32)
            gather(pool, passes(1), TURNS, h_table, srci, D, plain["seg"], 0, per=GR)
            pool.wait_ge(table_stored, 48)
            pool.wait_ge(reverse_zero, 16 * R)

            def scatter(k, j, it):
                if j % 2 == 0:
                    pool.wait_ge(mes["index"], k + 2)
                    pool.wait_ge(mes["rowsout"], k + 2)
                    if not (known(k) and k < R):
                        for r in (j % R, j % R + 1):
                            pool.wait_ge(scattered[r], (it * (UP // R) + j // R) * 16)
                    if not (known(k) and k < 1):
                        pool.wait_ge(scatter_go, k // 2 if known(k) else it * (UP // 2) + j // 2)
                    nc.gpsimd.tensor_tensor(scatter_hold[:, :], hold_in[:, :], hold_in[:, :], ALU.add).then_inc(scatter_go, 1)
                nc.gpsimd.indirect_dma_start(reverse[j % R], bass.IndirectOffsetOnAxis(sidx[:, j:j + 1], 0),
                                             SD[:, j % R, :], None, compute_op=ALU.add).then_inc(scattered[j % R], 16)
            gather(pool, passes(2), 2 * TURNS, h_table, srci, D, mes["turned"], 0, also=scatter, lag=16)
            with pool.Fori(0, LAYERS) as layer:
                pool.wait_ge(types_stored, layer * (16 * KT) + 16 * KT)
                nc.gpsimd.tensor_tensor(types_hold[:, :], hold_in[:, :], hold_in[:, :], ALU.add).then_inc(types_go, 1)
                pool.wait_ge(types_go, layer + 1)
                gather(pool, layers(layer), layer * TURNS + 3 * TURNS, type_table, tsrci, D, plain["seg"], layer * NG + NG, per=GR)

        @block.scalar
        def _(act):
            def root(n):
                act.wait_ge(root_in, n)
                nc.scalar.activation(small[:, 0, :], small[:, 3, :], ACT.Sqrt).then_inc(root_out, 1)

            root(1)
            node_act(act, node, D + 1, QKV)

            def copy(q, j, it):
                act.wait_ge(att["turned"], q + 1)
                if not (known(q) and q < 2):
                    act.wait_ge(att["query"], q - 1)
                nc.scalar.activation(OT[:, j % 2, :], bank[j % 2][:, :], ACT.Copy).then_inc(att["copied"], 1)

            def exp(q, j, it):
                act.wait_ge(att["clipped"], q + 1)
                if not (known(q) and q < 2):
                    act.wait_ge(att["msg"], q - 1)
                nc.scalar.activation(sc[:, 2, j % 2, :], sc[:, 1, j % 2, :], ACT.Exp).then_inc(att["exp"], 1)

            def emit(it, j):
                stage(NG, UGR, it, j, 0, copy)
                stage(NG, UGR, it, j, 2, exp)
            pipeline(act, NG, UGR, 2, emit)
            root(2)
            node_act(act, node, D + 1, ATTN)
            root(3)
            root(4)
            node_act(act, node, D + 1, CONV)
            root(5)
            node_act(act, node, D + 1, PAIR)

            def copy2(k, j, it):
                act.wait_ge(mes["turned"], k + 1)
                if not (known(k) and k < 2):
                    act.wait_ge(mes["pre"], k - 1)
                nc.scalar.activation(OT[:, j % 2, 0:2 * P], bank[j % 2][:, 0:2 * P], ACT.Copy).then_inc(mes["copied"], 1)

            def relu(k, j, it):
                act.wait_ge(mes["pre"], k + 1)
                if not (known(k) and k < MR):
                    act.wait_ge(mes["seg"], k - MR + 1)
                nc.scalar.activation(MS[:, j % MR, 0:2 * M], bank[2 + j % 2][:, 0:2 * M], ACT.Relu).then_inc(mes["relu"], 1)

            def rowsout(k, j, it):
                act.wait_ge(mes["seg"], k + 1)
                if not (known(k) and k < R):
                    act.wait_ge(scattered[j % R], (it * (U // R) + j // R) * 16)
                nc.scalar.activation(SD[:, j % R, :], bank[4 + j % 2][:, 0:RC], ACT.Copy).then_inc(mes["rowsout"], 1)

            def emit2(it, j):
                stage(STEPS, U, it, j, 0, copy2)
                stage(STEPS, U, it, j, 2, relu)
                stage(STEPS, U, it, j, 4, rowsout)
            pipeline(act, STEPS, U, 4, emit2)

            def turned(k, j, it):
                act.wait_ge(upd["turned"], k + 1)
                if not (known(k) and k < 2):
                    act.wait_ge(upd["hid"], k - 1)
                nc.scalar.activation(ST[:, j % 2, 0:2 * P], bank[j % 2][:, 0:2 * P], ACT.Copy)
                nc.scalar.activation(ST[0:D + 2, j % 2, 2 * P:3 * P], bank[j % 2][0:D + 2, 2 * P:3 * P], ACT.Copy)\
                    .then_inc(upd["copied"], 1)

            def aggout(k, j, it):
                act.wait_ge(upd["agg"], k + 1)
                if not (known(k) and k < 2):
                    act.wait_ge(upd["hid"], k - 1)
                nc.scalar.activation(NX[:, j % 2, 2 * RC:2 * RC + P], bank[2 + j % 2][:, 0:P], ACT.Copy).then_inc(upd["aggout"], 1)

            def hidout(k, j, it):
                act.wait_ge(upd["hid"], k + 1)
                if not (known(k) and k < 2):
                    act.wait_ge(upd["product"], k - 1)
                nc.scalar.activation(hidden[:, j % 2, :], bank[4 + j % 2][:, 0:P], ACT.Relu, bias=w("bn1"))\
                    .then_inc(upd["hidout"], 1)

            def emit3(it, j):
                stage(NB, UN, it, j, 0, turned)
                stage(NB, UN, it, j, 1, aggout)
                stage(NB, UN, it, j, 2, hidout)
            pipeline(act, NB, UN, 2, emit3)
            root(6)

            with act.Fori(0, LAYERS) as layer:
                nbase = layer * NB
                node_act(act, node, D + 1, nbase + TYPES)

                def gturned(k, j, it):
                    act.wait_ge(gru["turned"], nbase + k + 1)
                    if not (known(k) and k < 2):
                        act.wait_ge(gru["product"], nbase + k - 1)
                    nc.scalar.activation(ST[:, j % 2, 0:P], bank[j % 2][:, 0:P], ACT.Copy).then_inc(gru["copied"], 1)

                def gates(k, j, it):
                    act.wait_ge(gru["product"], nbase + k + 1)
                    if not (known(k) and k < 2):
                        act.wait_ge(gru["finished"], nbase + k - 1)
                    nc.scalar.activation(NX[:, j % 2, 0:2 * D], bank[2 + j % 2][:, 0:2 * D], ACT.Sigmoid)\
                        .then_inc(gru["gates"], 1)

                def tanh(k, j, it):
                    act.wait_ge(gru["add"], nbase + k + 1)
                    nc.scalar.activation(NX[:, j % 2, 4 * D:5 * D], NX[:, j % 2, 3 * D:4 * D], ACT.Tanh)\
                        .then_inc(gru["tanh"], 1)

                def gemit(it, j):
                    stage(NB, UN, it, j, 0, gturned)
                    stage(NB, UN, it, j, 1, gates)
                    stage(NB, UN, it, j, 2, tanh)
                pipeline(act, NB, UN, 2, gemit)

        @block.tensor
        def _(pe):
            pe.wait_ge(consts, 11)
            pe.wait_ge(path_f, 1)
            for q in range(2):
                nc.tensor.transpose(bank[4 + q][0:CG, 0:P], fcol[:, 2 - q, :], ident[:, :]).then_inc(path_turned, 1)
            for q, srct in enumerate((big[:, 0:SPAD], Hf[:, 0:SPAD], tmpf[:, 0:SPAD], big[:, 5 * SPAD:6 * SPAD])):
                pe.wait_ge(idx_made, 4)
                for g in range(IDXQ):
                    n = q * IDXQ + g
                    if n >= 2:
                        pe.wait_ge(idx_tabled, n - 1)
                    cols = range(4 * g, min(4 * g + 4, CG))
                    for c in cols:
                        last = nc.tensor.transpose(bank[n % 2][:, (c - 4 * g) * P:(c - 4 * g + 1) * P],
                                                   srct[:, c * P:(c + 1) * P], ident[:, :])
                    last.then_inc(idx_turned, 1)
            pe.wait_ge(idx_tabled, 4 * IDXQ)
            pe.wait_ge(w_loaded, 32)
            node_pe(pe, node, D + 1, w("qkv", D + 1), 2 * D, QKV)

            def turn(q, j, it):
                pe.wait_ge(att["onehot"], q + 1)
                if not (known(q) and q < 2):
                    pe.wait_ge(att["copied"], q - 1)
                for n in range(GR):
                    last = nc.tensor.transpose(bank[j % 2][:, n * P:(n + 1) * P], OH[:, (j * GR + n) % HOT, :], ident[:, :])
                last.then_inc(att["turned"], 1)

            def query(q, j, it):
                blocks = blocks_of(pe, q * GR)
                pe.wait_ge(att["copied"], q + 1)
                if not (known(q) and q < 2):
                    pe.wait_ge(att["score"], q - 1)
                for n, b in enumerate(blocks):
                    last = nc.tensor.matmul(bank[2 + j % 2][:, n * D:(n + 1) * D], OT[:, j % 2, n * P:(n + 1) * P],
                                            big_kv[:, bass.ds(b * KV, D)], start=True, stop=True)
                last.then_inc(att["query"], 1)

            def seg(q, j, it):
                pe.wait_ge(att["msg"], q + 1)
                if not (known(q) and q < 2):
                    pe.wait_ge(att["summed"], (q - 1) * GR)
                for n in range(GR):
                    last = nc.tensor.matmul(bank[4 + j % 2][:, n * AC:(n + 1) * AC], OH[:, (j * GR + n) % HOT, :],
                                            messages[:, j % 2, n, :], start=True, stop=True)
                last.then_inc(att["seg"], 1)

            pe.wait_ge(path_loaded, 16)
            pe.wait_ge(pass_begun, 1)

            def emit(it, j):
                stage(NG, UGR, it, j, 4, seg)
                stage(NG, UGR, it, j, 0, turn)
                stage(NG, UGR, it, j, 1, query)
            pipeline(pe, NG, UGR, 4, emit)
            node_pe(pe, node, D + 1, w("attn", D + 1), D, ATTN)
            plain_pe(pe, plain, passes(1), 0)
            node_pe(pe, node, D + 1, w("conv", D + 1), D, CONV)
            node_pe(pe, node, D + 1, w("pair", D + 1), 2 * M, PAIR)

            def keyrow(k, j, it):
                pe.wait_ge(mes["keys"], it * (U // HALF) + j // HALF + 1)
                if not (known(k) and k < 1):
                    pe.wait_ge(mes["equal"], k)
                nc.tensor.transpose(bank[7][:, 0:P], keyslot[:, j:j + 1].to_broadcast([P, P]), ident[:, :])\
                    .then_inc(mes["keyrow"], 1)

            def turn2(k, j, it):
                if j % GR == 0:
                    pe.wait_ge(mes["onehot"], it * (U // GR) + j // GR + 1)
                    pe.wait_ge(gathered[j // GR], arrived(passes(2), j // GR, it))
                pe.wait_ge(edge_loaded[j % HALF], (it * (U // HALF) + j // HALF + 1) * 16)
                if not (known(k) and k < 2):
                    pe.wait_ge(mes["copied"], k - 1)
                nc.tensor.transpose(bank[j % 2][:, P:2 * P], OH[:, j % HOT, :], ident[:, :])
                nc.tensor.transpose(bank[j % 2][:, 0:P], G[:, j, 0:2 * D], ident[:, :]).then_inc(mes["turned"], 1)

            held = {}

            def pre(k, j, it):
                b = near(pe, held, k, j + 1)
                pe.wait_ge(mes["copied"], k + 1)
                if not (known(k) and k < 2):
                    pe.wait_ge(mes["relu"], k - 1)
                nc.tensor.matmul(bank[2 + j % 2][:, 0:2 * M], OT[:, j % 2, 0:P], w("edge"), start=True, stop=False)
                nc.tensor.matmul(bank[2 + j % 2][:, 0:2 * M], OT[:, j % 2, P:2 * P], big[:, bass.ds(b * 2 * M, 2 * M)],
                                 start=False, stop=True).then_inc(mes["pre"], 1)

            def seg2(k, j, it):
                pe.wait_ge(mes["relu"], k + 1)
                pe.wait_ge(mes["equal"], k + 1)
                if not (known(k) and k < 1):
                    pe.wait_ge(mes["summed"], k)
                if not (known(k) and k < 2):
                    pe.wait_ge(mes["rowsout"], k - 1)
                nc.tensor.matmul(bank[6][:, 0:M], OH[:, j % HOT, :], MS[:, j % MR, 0:M], start=True, stop=True)
                nc.tensor.matmul(bank[4 + j % 2][:, 0:RC], EQ[:, j % MR, :], MS[:, j % MR, M:M + RC],
                                 start=True, stop=True).then_inc(mes["seg"], 1)

            pe.wait_ge(pass_begun, 2)

            def emit2(it, j):
                stage(STEPS, U, it, j, 0, keyrow)
                stage(STEPS, U, it, j, 0, turn2)
                stage(STEPS, U, it, j, 1, pre)
                stage(STEPS, U, it, j, 3, seg2)
            pipeline(pe, STEPS, U, 3, emit2)

            def uturn(k, j, it):
                pe.wait_ge(upd["rows"], k + 1)
                if not (known(k) and k < 2):
                    pe.wait_ge(upd["copied"], k - 1)
                for c, width in ((0, P), (1, P), (2, D + 2)):
                    last = nc.tensor.transpose(bank[j % 2][0:width, c * P:(c + 1) * P],
                                               S[:, j % 2, c * P:c * P + width], ident[:, :])
                last.then_inc(upd["turned"], 1)

            def agg(k, j, it):
                pe.wait_ge(upd["copied"], k + 1)
                if not (known(k) and k < 2):
                    pe.wait_ge(upd["aggout"], k - 1)
                o = bank[2 + j % 2][:, 0:P]
                nc.tensor.matmul(o, w("f2"), ST[:, j % 2, 0:P], start=True, stop=False)
                nc.tensor.matmul(o, w("r2"), ST[:, j % 2, P:2 * P], start=False, stop=False)
                nc.tensor.matmul(o, w("b2", 2), ST[0:2, j % 2, 2 * P:3 * P], start=False, stop=True).then_inc(upd["agg"], 1)

            def hid(k, j, it):
                pe.wait_ge(upd["aggout"], k + 1)
                if not (known(k) and k < 2):
                    pe.wait_ge(upd["hidout"], k - 1)
                o = bank[4 + j % 2][:, 0:P]
                nc.tensor.matmul(o, w("n1a"), NX[:, j % 2, 2 * RC:2 * RC + P], start=True, stop=False)
                nc.tensor.matmul(o, w("n1b", D + 2), ST[0:D + 2, j % 2, 2 * P:3 * P], start=False, stop=True)\
                    .then_inc(upd["hid"], 1)

            def product(k, j, it):
                pe.wait_ge(upd["hidout"], k + 1)
                if not (known(k) and k < 2):
                    pe.wait_ge(upd["finished"], k - 1)
                o = bank[6 + j % 2][:, 0:D]
                nc.tensor.matmul(o, hidden[:, j % 2, :], w("n2"), start=True, stop=False)
                nc.tensor.matmul(o, ones[0:1, :], w("bn2", 1), start=False, stop=True).then_inc(upd["product"], 1)

            def emit3(it, j):
                stage(NB, UN, it, j, 0, uturn)
                stage(NB, UN, it, j, 1, agg)
                stage(NB, UN, it, j, 2, hid)
                stage(NB, UN, it, j, 3, product)
            pipeline(pe, NB, UN, 3, emit3)

            with pe.Fori(0, LAYERS) as layer:
                nbase = layer * NB
                node_pe(pe, node, D + 1, w("types", D + 1), KT * D, nbase + TYPES)
                plain_pe(pe, plain, layers(layer), layer * NG + NG)

                def gturn(k, j, it):
                    pe.wait_ge(gru["rows"], nbase + k + 1)
                    if not (known(k) and k < 2):
                        pe.wait_ge(gru["copied"], nbase + k - 1)
                    nc.tensor.transpose(bank[j % 2][:, 0:P], S[:, j % 2, 0:P], ident[:, :]).then_inc(gru["turned"], 1)

                def gmul(k, j, it):
                    pe.wait_ge(gru["copied"], nbase + k + 1)
                    if not (known(k) and k < 2):
                        pe.wait_ge(gru["add"], nbase + k - 1)
                    o = bank[2 + j % 2][:, 0:4 * D]
                    nc.tensor.matmul(o, ST[:, j % 2, 0:P], w("gru"), start=True, stop=False)
                    nc.tensor.matmul(o, ones[0:1, :], w("gb0", 1), start=False, stop=False)
                    nc.tensor.matmul(o, ones[0:1, :], w("gb1", 1), start=False, stop=True).then_inc(gru["product"], 1)

                def gemit(it, j):
                    stage(NB, UN, it, j, 0, gturn)
                    stage(NB, UN, it, j, 1, gmul)
                pipeline(pe, NB, UN, 1, gemit)

        @block.vector
        def _(v):
            done = [0]

            def link(ins):
                done[0] += 1
                ins.then_inc(chain, 1)
                v.wait_ge(chain, done[0])

            def bc(t):
                return t.unsqueeze(2).to_broadcast([P, NB, D])

            def vec(n):
                return lng[:, n, :].unsqueeze(1).to_broadcast([P, NB, D])

            roots = [0]

            def root(src):
                roots[0] += 1
                src.then_inc(root_in, 1)
                v.wait_ge(root_out, roots[0])

            def layer_norm(src, dst, relu):
                link(nc.vector.reduce_sum(small[:, 0, :], src, AXX))
                link(nc.vector.tensor_scalar(small[:, 1, :], small[:, 0, :], 1.0 / D, None, ALU.mult))
                link(nc.vector.tensor_tensor(dst, src, bc(small[:, 1, :]), ALU.subtract))
                link(nc.vector.tensor_tensor(tmp_, dst, dst, ALU.mult))
                link(nc.vector.reduce_sum(small[:, 2, :], tmp_, AXX))
                root(nc.vector.tensor_scalar(small[:, 3, :], small[:, 2, :], 1.0 / D, EPS, ALU.mult, ALU.add))
                link(nc.vector.reciprocal(small[:, 1, :], small[:, 0, :]))
                link(nc.vector.tensor_tensor(dst, dst, bc(small[:, 1, :]), ALU.mult))
                if relu:
                    link(nc.vector.tensor_scalar(dst, dst, 0.0, None, ALU.max))

            nc.vector.memset(acc[:, :], 0.0).then_inc(acc_zero, 1)
            v.wait_ge(dst_loaded, 16)
            v.wait_ge(consts, 5)
            blocks = big[:, SPAD:SPAD + T].bitcast(I32)
            link(nc.vector.tensor_scalar(blocks, big[:, 0:T].bitcast(I32), 7, None, ALU.arith_shift_right))
            last_step = big[:, 0:T]
            link(nc.vector.tensor_tensor(last_step, blocks, itile, ALU.add))
            link(nc.vector.tensor_copy(fcol[:, 0, :], icol[:, :]))
            before = big[:, SPAD:SPAD + T]
            for c in range(CG):
                link(nc.vector.tensor_scalar(before, last_step, fcol[:, 0, c:c + 1], None, ALU.is_lt))
                link(nc.vector.reduce_sum(fcol[:, 1, c:c + 1], before, AXX))
            nc.vector.tensor_copy(tcol[:, :], fcol[:, 1, :]).then_inc(tiles_known, 1)
            link(nc.vector.tensor_tensor(fcol[:, 2, :], fcol[:, 0, :], fcol[:, 1, :], ALU.subtract))
            nc.vector.tensor_scalar(fcol[:, 3, :], fcol[:, 2, :], float(P), None, ALU.mult).then_inc(path_f, 1)
            for q in range(2):
                v.wait_ge(path_turned, q + 1)
                nc.vector.tensor_copy(pcol[:, q, :], bank[4 + q][0:CG, 0:P]).then_inc(path_copied, 1)

            v.wait_ge(consts, 11)
            nc.vector.tensor_copy(iota[:, :], iiota)
            nc.vector.memset(S[:, :, :], 1.0)
            nc.vector.memset(MS[:, :, :], 1.0)
            link(nc.vector.tensor_copy(trash[:, :], idx[:, 0:1]))

            v.wait_ge(x_loaded, 16)
            v.wait_ge(tiles_read, 1)
            v.wait_ge(path_f, 1)
            rowsi = [big[:, (2 + q) * SPAD:(3 + q) * SPAD].bitcast(I32) for q in range(3)]
            dst, valid, local, rtrash = (big[:, q * SPAD:(q + 1) * SPAD] for q in (5, 6, 0, 1))
            srcf, tsrcf = Hf[:, 0:SPAD], tmpf[:, 0:SPAD]
            link(nc.vector.tensor_copy(dst, rowsi[0]))
            link(nc.vector.tensor_copy(srcf, rowsi[1]))
            link(nc.vector.tensor_copy(rtrash, irtrash))
            link(nc.vector.tensor_copy(tsrcf, rowsi[2]))
            for c in range(CG):
                link(nc.vector.tensor_scalar(local[:, c * P:(c + 1) * P], dst[:, c * P:(c + 1) * P], fcol[:, 3, c:c + 1], None,
                                             ALU.subtract))
            link(nc.vector.tensor_scalar(valid, dst, float(N), None, ALU.is_lt))
            link(nc.vector.scalar_tensor_tensor(out=valid, in0=local, scalar=0.0, in1=valid, op0=ALU.is_ge, op1=ALU.mult))
            link(nc.vector.scalar_tensor_tensor(out=valid, in0=local, scalar=float(P - 1), in1=valid, op0=ALU.is_le, op1=ALU.mult))
            link(nc.vector.scalar_tensor_tensor(out=tsrcf, in0=tsrcf, scalar=float(NPAD), in1=srcf, op0=ALU.mult, op1=ALU.add))
            keyf = dst
            link(nc.vector.tensor_tensor(keyf, srcf, rtrash, ALU.subtract))
            link(nc.vector.tensor_tensor(keyf, keyf, valid, ALU.mult))
            link(nc.vector.tensor_tensor(keyf, keyf, rtrash, ALU.add))
            nc.vector.memset(hold2[:, :], 0.0).then_inc(idx_made, 4)
            for q, to in enumerate((dloc, srci, tsrci, key)):
                for g in range(IDXQ):
                    v.wait_ge(idx_turned, q * IDXQ + g + 1)
                    lo, hi = g * 4 * P, min((g + 1) * 4 * P, SPAD)
                    nc.vector.tensor_copy(to[:, lo:hi], bank[(q * IDXQ + g) % 2][:, 0:hi - lo]).then_inc(idx_tabled, 1)
            v.wait_ge(idx_tabled, 4 * IDXQ)

            layer_norm(X_, H_, True)
            link(nc.vector.memset(big_kv.rearrange("p (b d) -> p b d", d=KV)[:, :, KV - 1:KV], 1.0))
            node_dve(v, node, lambda k: part(Hf, k, D),
                     lambda k, ps: nc.vector.tensor_copy(part(big_kv, k, KV, 0, 2 * D), ps[:, 0:2 * D]), QKV)
            v.wait_ge(node["finished"], QKV + NB)
            nc.vector.memset(hold2[:, :], 0.0).then_inc(table_ready, 1)
            v.wait_ge(table_ready, 1)
            v.wait_ge(reverse_zero, 16 * R)
            v.wait_ge(path_loaded, 16)
            link(nc.vector.memset(hold2[:, :], 0.0))
            nc.vector.memset(hold2[:, :], 0.0).then_inc(pass_begun, 1)
            v.wait_ge(pass_begun, 1)

            one, adds = hot(v, att, 0), sum_up(v, att, 0, AC, bank[4:6])
            products = prod[:, :, :].rearrange("p a b -> p (a b)").rearrange("p (n d) -> p n d", n=GR)

            def rows(j):
                return G[:, j * GR:(j + 1) * GR, :]

            def score(q, j, it):
                v.wait_ge(gathered[j], arrived(passes(0), j, it))
                v.wait_ge(att["query"], q + 1)
                if not (known(q) and q < 1):
                    v.wait_ge(att["scored"], q)
                nc.vector.scalar_tensor_tensor(out=products, in0=bank[2 + j % 2][:, 0:GR * D].rearrange("p (n d) -> p n d", n=GR),
                                               scalar=1.0 / D ** 0.5, in1=rows(j)[:, :, 0:D], op0=ALU.mult, op1=ALU.mult)\
                    .then_inc(att["score"], 1)

            def scored(q, j, it):
                v.wait_ge(att["score"], q + 1)
                nc.vector.reduce_sum(sc[:, 0, j % 2, :], products, AXX).then_inc(att["scored"], 1)

            def clip(q, j, it):
                v.wait_ge(att["scored"], q + 1)
                if not (known(q) and q < 2):
                    v.wait_ge(att["exp"], q - 1)
                nc.vector.tensor_scalar(sc[:, 1, j % 2, :], sc[:, 0, j % 2, :], 5.0, -5.0,
                                        ALU.min, ALU.max).then_inc(att["clipped"], 1)

            def msg(q, j, it):
                v.wait_ge(att["exp"], q + 1)
                if not (known(q) and q < 2):
                    v.wait_ge(att["seg"], q - 1)
                nc.vector.tensor_tensor(messages[:, j % 2, :, 0:D + 1], rows(j)[:, :, D:KV],
                                        sc[:, 2, j % 2, :].unsqueeze(2).to_broadcast([P, GR, D + 1]), ALU.mult)\
                    .then_inc(att["msg"], 1)

            def emit(it, j):
                stage(NG, UGR, it, j, 3, msg)
                stage(NG, UGR, it, j, 5, adds[0])
                stage(NG, UGR, it, j, 0, one)
                stage(NG, UGR, it, j, 5, adds[1])
                stage(NG, UGR, it, j, 2, score)
                stage(NG, UGR, it, j, 5, adds[2])
                stage(NG, UGR, it, j, 2, scored)
                stage(NG, UGR, it, j, 5, adds[3])
                stage(NG, UGR, it, j, 2, clip)
            pipeline(v, NG, UGR, 5, emit)
            v.wait_ge(att["summed"], STEPS)

            sums = acc_[AC].rearrange("p (b d) -> p b d", d=AC)
            link(nc.vector.tensor_copy(deg[:, :], sums[:, :, D + 1]))
            link(nc.vector.tensor_scalar(small[:, 2, :], sums[:, :, D], TINY, None, ALU.max))
            link(nc.vector.reciprocal(small[:, 1, :], small[:, 2, :]))
            link(nc.vector.tensor_tensor(tmp_, sums[:, :, 0:D], bc(small[:, 1, :]), ALU.mult))
            root(nc.vector.tensor_scalar(small[:, 3, :], deg[:, :], 1.0, None, ALU.max))
            link(nc.vector.reciprocal(norm[:, :], small[:, 0, :]))
            node_dve(v, node, lambda k: part(tmpf, k, D),
                     lambda k, ps: nc.vector.tensor_tensor(part(Hf, k, D), part(Hf, k, D), ps[:, 0:D], ALU.add), ATTN)
            v.wait_ge(node["finished"], ATTN + NB)
            layer_norm(H_, H_, False)
            link(nc.vector.tensor_tensor(H_, H_, vec(0), ALU.mult))
            link(nc.vector.tensor_tensor(H_, H_, vec(1), ALU.add))
            link(nc.vector.tensor_tensor(X_, X_, H_, ALU.add))

            layer_norm(X_, H_, True)
            nc.vector.tensor_tensor(tmp_, H_, bc(norm[:, :]), ALU.mult).then_inc(table_ready, 1)
            link(nc.vector.memset(acc_[D], 0.0))
            plain_dve(v, plain, 0)
            v.wait_ge(plain["summed"], STEPS)
            v.wait_ge(table_stored, 32)
            node_dve(v, node, lambda k: part(acc_[D], k, D),
                     lambda k, ps: nc.vector.tensor_copy(part(tmpf, k, D), ps[:, 0:D]), CONV)
            v.wait_ge(node["finished"], CONV + NB)
            link(nc.vector.tensor_tensor(tmp_, tmp_, bc(norm[:, :]), ALU.mult))
            link(nc.vector.tensor_tensor(tmp_, tmp_, vec(2), ALU.add))
            link(nc.vector.tensor_tensor(X_, X_, tmp_, ALU.add))

            layer_norm(X_, H_, True)
            nc.vector.memset(hold2[:, :], 0.0).then_inc(table_ready, 1)
            v.wait_ge(table_ready, 3)
            link(nc.vector.memset(acc_[M], 0.0))
            node_dve(v, node, lambda k: part(Hf, k, D),
                     lambda k, ps: nc.vector.tensor_copy(part(big[:, :], k, 2 * M), ps[:, 0:2 * M]), PAIR)
            v.wait_ge(node["finished"], PAIR + NB)
            link(nc.vector.memset(MS[:, :, 2 * M:2 * M + 1], 1.0))
            nc.vector.memset(hold2[:, :], 0.0).then_inc(pass_begun, 1)
            v.wait_ge(pass_begun, 2)

            def hot2(k, j, it):
                if j % GR:
                    return
                if not (known(k) and k < HOT):
                    v.wait_ge(mes["seg"], k + (GR - HOT))
                onehots(k // GR if known(k) else it * (U // GR) + j // GR, j // GR).then_inc(mes["onehot"], 1)

            held = {}

            def add2(k, j, it):
                b = near(v, held, k, j)
                v.wait_ge(mes["seg"], k + 1)
                if not (known(k) and k < 1):
                    v.wait_ge(mes["summed"], k)
                to = acc_[M][:, bass.ds(b * M, M)]
                nc.vector.tensor_tensor(to, to, bank[6][:, 0:M], ALU.add).then_inc(mes["summed"], 1)

            def keys(k, j, it):
                if j % HALF:
                    return
                if not (known(k) and k < U):
                    v.wait_ge(mes["keyrow"], k + (HALF - U))
                    v.wait_ge(mes["rep"], k + (HALF - U))
                nc.vector.tensor_scalar(keyless[:, j:j + HALF], part(key[:, :], k, 1, 0, HALF), trash[:, 0:1], None,
                                        ALU.subtract).then_inc(mes["less"], 1)
                nc.vector.tensor_copy(keyslot[:, j:j + HALF], part(key[:, :], k, 1, 0, HALF)).then_inc(mes["keys"], 1)

            def equal(k, j, it):
                v.wait_ge(mes["keyrow"], k + 1)
                if not (known(k) and k < MR):
                    v.wait_ge(mes["seg"], k - MR + 1)
                nc.vector.tensor_scalar(EQ[:, j % MR, :], bank[7][:, 0:P], part(key[:, :], k, 1), None,
                                        ALU.is_equal).then_inc(mes["equal"], 1)

            def count(k, j, it):
                v.wait_ge(mes["equal"], k + 1)
                if not (known(k) and k < 2):
                    v.wait_ge(mes["rep"], k - 1)
                nc.vector.tensor_tensor_reduce(prod[:, j % 2, :], EQ[:, j % MR, :], earlier[:, :], 1.0, 0.0, ALU.mult, ALU.add,
                                               cnt[:, 0, j % 2:j % 2 + 1]).then_inc(mes["count"], 1)

            def rep(k, j, it):
                v.wait_ge(mes["count"], k + 1)
                v.wait_ge(mes["less"], it * (U // HALF) + j // HALF + 1)
                if not (known(k) and k < 2):
                    v.wait_ge(mes["index"], k - 1)
                nc.vector.tensor_scalar(cnt[:, 1, j % 2:j % 2 + 1], cnt[:, 0, j % 2:j % 2 + 1], 0.0,
                                        keyless[:, j:j + 1], ALU.is_equal, ALU.mult).then_inc(mes["rep"], 1)

            def index(k, j, it):
                v.wait_ge(mes["rep"], k + 1)
                if not (known(k) and k < U):
                    v.wait_ge(scattered[j % R], (it * (U // R) + j // R - U // R + 1) * 16)
                nc.vector.tensor_scalar(sidx[:, j:j + 1], cnt[:, 1, j % 2:j % 2 + 1], trash[:, 0:1], None,
                                        ALU.add).then_inc(mes["index"], 1)

            def emit2(it, j):
                stage(STEPS, U, it, j, 0, keys)
                stage(STEPS, U, it, j, 0, hot2)
                stage(STEPS, U, it, j, 1, equal)
                stage(STEPS, U, it, j, 2, rep)
                stage(STEPS, U, it, j, 1, count)
                stage(STEPS, U, it, j, 4, add2)
                stage(STEPS, U, it, j, 2, index)
            pipeline(v, STEPS, U, 4, emit2)
            v.wait_ge(mes["summed"], STEPS)

            def urows(k, j, it):
                r = j % 2
                if not (known(k) and k < 2):
                    v.wait_ge(upd["turned"], k - 1)
                nc.vector.tensor_copy(S[:, r, 0:M], part(acc_[M], k, M))
                nc.vector.tensor_copy(S[:, r, 2 * M + 2:2 * M + 2 + D], part(Hf, k, D))
                nc.vector.tensor_copy(S[:, r, 2 * M + 1:2 * M + 2], part(deg[:, :], k, 1))
                v.wait_ge(rev_loaded[r], (k // 2 + 1) * (16 * R) if known(k) else (it * (UN // 2) + j // 2 + 1) * (16 * R))
                if not (known(k) and k < 2):
                    v.wait_ge(upd["rows"], k - 1)
                nc.vector.tensor_tensor(NX[:, r, 0:RC], revs[:, r, 0, :], revs[:, r, 1, :], ALU.add).then_inc(upd["sums"], 1)
                nc.vector.tensor_tensor(NX[:, r, RC:2 * RC], revs[:, r, 2, :], revs[:, r, 3, :], ALU.add).then_inc(upd["sums"], 1)
                v.wait_ge(upd["sums"], k * 2 + 2)
                nc.vector.tensor_tensor(S[:, r, M:M + RC], NX[:, r, 0:RC], NX[:, r, RC:2 * RC], ALU.add).then_inc(upd["rows"], 1)

            def uend(k, j, it):
                v.wait_ge(upd["product"], k + 1)
                nc.vector.tensor_copy(part(tmpf, k, D), bank[6 + j % 2][:, 0:D]).then_inc(upd["finished"], 1)

            def uemit(it, j):
                stage(NB, UN, it, j, 0, urows)
                stage(NB, UN, it, j, 4, uend)
            pipeline(v, NB, UN, 4, uemit)
            v.wait_ge(upd["finished"], NB)
            link(nc.vector.tensor_tensor(tmp_, tmp_, H_, ALU.add))
            link(nc.vector.tensor_tensor(X_, X_, tmp_, ALU.add))
            layer_norm(X_, H_, True)
            link(nc.vector.memset(S[:, :, :], 1.0))

            with v.Fori(0, LAYERS) as layer:
                nbase = layer * NB
                node_dve(v, node, lambda k: part(Hf, k, D),
                         lambda k, ps: nc.vector.tensor_copy(part(big[:, :], k, KT * D), ps[:, 0:KT * D]), nbase + TYPES)
                v.wait_ge(node["finished"], nbase + (TYPES + NB))
                nc.vector.memset(acc_[D], 0.0).then_inc(gru_acc_zero, 1)
                v.wait_ge(gru_acc_zero, layer * 2 + 1)
                plain_dve(v, plain, layer * NG + NG)
                v.wait_ge(plain["summed"], layer * STEPS + 2 * STEPS)

                def grows(k, j, it):
                    if not (known(k) and k < 2):
                        v.wait_ge(gru["turned"], nbase + k - 1)
                    nc.vector.tensor_copy(S[:, j % 2, D:2 * D], part(Hf, k, D))
                    nc.vector.tensor_copy(S[:, j % 2, 0:D], part(acc_[D], k, D)).then_inc(gru["rows"], 1)

                def gate(k, j, it):
                    r = j % 2
                    v.wait_ge(gru["gates"], nbase + k + 1)
                    nc.vector.tensor_tensor(NX[:, r, 2 * D:3 * D], NX[:, r, 0:D], bank[2 + r][:, 3 * D:4 * D], ALU.mult)\
                        .then_inc(gru["mul"], 1)
                    v.wait_ge(gru["mul"], nbase + k + 1)
                    nc.vector.tensor_tensor(NX[:, r, 3 * D:4 * D], NX[:, r, 2 * D:3 * D], bank[2 + r][:, 2 * D:3 * D], ALU.add)\
                        .then_inc(gru["add"], 1)

                def blend(k, j, it):
                    r = j % 2
                    v.wait_ge(gru["tanh"], nbase + k + 1)
                    nc.vector.tensor_tensor(NX[:, r, 5 * D:6 * D], part(Hf, k, D), NX[:, r, 4 * D:5 * D], ALU.subtract)\
                        .then_inc(gru["diff"], 1)
                    v.wait_ge(gru["diff"], nbase + k + 1)
                    nc.vector.tensor_tensor(NX[:, r, 6 * D:7 * D], NX[:, r, D:2 * D], NX[:, r, 5 * D:6 * D], ALU.mult)\
                        .then_inc(gru["blend"], 1)
                    v.wait_ge(gru["blend"], nbase + k + 1)
                    nc.vector.tensor_tensor(part(Hf, k, D), NX[:, r, 4 * D:5 * D], NX[:, r, 6 * D:7 * D], ALU.add)\
                        .then_inc(gru["finished"], 1)

                def gemit(it, j):
                    stage(NB, UN, it, j, 0, grows)
                    stage(NB, UN, it, j, 2, gate)
                    stage(NB, UN, it, j, 3, blend)
                pipeline(v, NB, UN, 3, gemit)
                v.wait_ge(gru["finished"], nbase + NB)
                nc.vector.memset(S[:, :, D:D + 1], 1.0).then_inc(gru_acc_zero, 1)
                v.wait_ge(gru_acc_zero, layer * 2 + 2)
            nc.vector.tensor_tensor(X_, X_, H_, ALU.add).then_inc(result, 1)


def pack(i):
    import numpy as np
    g = {k: np.asarray(v) for k, v in i.items()}
    W = np.zeros((P, WTOTAL), np.float32)

    def put(name, block, row=0, col=0):
        lo = WCOLS[name][0] + col
        W[row:row + block.shape[0], lo:lo + block.shape[1]] = block

    put("qkv", g["L0_gnn_qk_w"].T)
    put("qkv", g["L0_gnn_v_w"].T, col=D)
    put("qkv", g["L0_gnn_qk_b"][None], row=D)
    put("qkv", g["L0_gnn_v_b"][None], row=D, col=D)
    put("attn", g["L0_gnn_o_w"].T)
    put("attn", g["L0_gnn_o_b"][None], row=D)
    put("conv", g["L1_gnn_weight"])
    f, r = g["L2_gnn_W1_f"], g["L2_gnn_W1_r"]
    put("pair", f[D:2 * D])
    put("pair", r[0:D], col=M)
    put("pair", g["L2_gnn_b1_f"][None], row=D)
    put("pair", g["L2_gnn_b1_r"][None], row=D, col=M)
    put("edge", f[0:D])
    put("edge", r[D:2 * D], col=M)
    put("edge", f[2 * D:], row=D)
    put("edge", r[2 * D:], row=D, col=M)
    put("f2", g["L2_gnn_W2_f"])
    put("r2", g["L2_gnn_W2_r"])
    put("b2", g["L2_gnn_b2_r"][None])
    put("b2", g["L2_gnn_b2_f"][None], row=1)
    put("n1a", g["L2_gnn_Wn1"][0:M])
    put("n1b", g["L2_gnn_Wn1"][M:], row=2)
    put("bn1", g["L2_gnn_bn1"][:, None])
    put("n2", g["L2_gnn_Wn2"])
    put("bn2", g["L2_gnn_bn2"][None])
    for t in range(KT):
        put("types", g["L3_gnn_W"][t].T, col=t * D)
        put("types", g["L3_gnn_b"][t][None], row=D, col=t * D)
    ih, hh = g["L3_gnn_w_ih"].T, g["L3_gnn_w_hh"].T
    put("gru", ih)
    put("gru", hh[:, 0:2 * D], row=D)
    put("gru", hh[:, 2 * D:], row=D, col=3 * D)
    put("gb0", g["L3_gnn_b_ih"][None])
    put("gb1", g["L3_gnn_b_hh"][None, 0:2 * D])
    put("gb1", g["L3_gnn_b_hh"][None, 2 * D:], col=3 * D)
    vectors = np.concatenate([g["L0_gnn_ln_g"], g["L0_gnn_ln_b"], g["L1_gnn_bias"]])
    return W, vectors


def kernel(**inputs):
    import numpy as np
    import concourse.bacc as bacc
    from concourse.bass_utils import run_bass_kernel_spmd

    def tiles(name, fill):
        a = np.full(((T + 1) * P,), fill, np.int32)
        a[:E] = np.asarray(inputs[name])
        return a.reshape(T + 1, P)

    x = np.zeros((NPAD, D), np.float32)
    x[:N] = np.asarray(inputs["x"])
    edge = np.zeros(((T + 1) * P, D), np.float32)
    edge[:E] = np.asarray(inputs["edge_attr_64"])
    dst = tiles("dst", PADDST)
    W, vectors = pack(inputs)
    arrays = {"x": x, "src": tiles("src", 0), "dst": dst, "type": tiles("edge_type_4", 0), "edge": edge,
              "dst_last": np.ascontiguousarray(dst[:T, P - 1]), "weights": W, "vectors": vectors}
    nc = bacc.Bacc("TRN2", target_bir_lowering=False, num_devices=1)
    aps = {n: nc.dram_tensor(f"in_{n}", v.shape, mybir.dt.from_np(v.dtype), kind="ExternalInput").ap()
           for n, v in arrays.items()}
    out = nc.dram_tensor("out_0", (N, D), F32, kind="ExternalOutput").ap()
    build(nc, aps, out)
    r = run_bass_kernel_spmd(nc, [{f"in_{n}": v for n, v in arrays.items()}], core_ids=[0])
    return r.results[0]["out_0"]
```

```python
from contextlib import ExitStack

import concourse.bass as bass
from concourse import mybir

P = 128
N = 6250
D = 64
E = 206250
NB = -(-N // P)
NPAD = NB * P
T = -(-E // P)
STEPS = T + NB - 1
CG = -(-STEPS // P)
SPAD = CG * P
M = 128
KT = 4
LAYERS = 4
KV = 2 * D + 1
AC = D + 2
RC = M + 1
R = 4
TRASH = NPAD
RROWS = NPAD + P
SLOTS = 40
HS = SLOTS // 2
ROUNDS = (-(-STEPS // SLOTS), STEPS // SLOTS)
TURNS = sum(ROUNDS)
HALF = 10
HOT = 20
GR = 4
NG = STEPS // GR
U = 40
UP = 40
UGR = UP // GR
UN = 6
GN = 4
NQ = -(-NB // GN)
G2 = 2
NP2 = -(-NB // G2)
UQ = 2
UG = 4
OHG = HOT // GR
MR = 4
EPS = 1e-5
TINY = 1e-30
TYPES_DONE = 32
PARTS = 3
PADDST = NPAD - 1
IDXQ = -(-CG // 4)
assert STEPS % HS == 0 and STEPS % SLOTS and HS % GR == 0 and U == UP == SLOTS and U % HALF == 0 and UGR % 2 == 0

F32 = mybir.dt.float32
I32 = mybir.dt.int32
I16 = mybir.dt.int16
BF16 = mybir.dt.bfloat16
ALU = mybir.AluOpType
ACT = mybir.ActivationFunctionType
AXX = mybir.AxisListType.X

WCOLS = {}
_at = 0
for _n, _w in (("qkv", 2 * D), ("attn", D), ("conv", D), ("pair", 2 * M), ("edge", 2 * M), ("f2", M), ("r2", M),
               ("n1a", M), ("n1b", M), ("n2", D), ("types", KT * D), ("gru", 4 * D), ("b2", M), ("bn1", 1),
               ("bn2", D), ("gb", 4 * D)):
    WCOLS[_n] = (_at, _at + _w)
    _at += _w
WTOTAL = _at


def known(k):
    return isinstance(k, int)


def pipeline(eng, n, unroll, lag, emit):
    for j in range(unroll):
        emit(0, j)
    with eng.Fori(1, n // unroll) as it:
        for j in range(unroll):
            emit(it, j)
    for i in range(n // unroll * unroll, n + lag):
        emit(i // unroll, i % unroll)


def stage(n, unroll, it, j, lag, body):
    k, slot, kit = it * unroll + (j - lag), (j - lag) % unroll, it + (j - lag) // unroll
    if known(k) and not 0 <= k < n:
        return
    body(k, slot, kit)


def blocks_in(k, group):
    return min(group, NB - k * group) if known(k) else group


def build(nc, a, out):
    ctx = ExitStack()
    with ctx:
        def sb(name, shape, dt=F32):
            return ctx.enter_context(nc.sbuf_tensor(name, shape, dt))

        def sem(name):
            return ctx.enter_context(nc.semaphore(name))

        def dram(name, shape, dt=F32):
            return nc.dram_tensor(name, shape, dt).ap()

        kv_table = dram("kv_table", (NPAD, KV))
        h_table = dram("h_table", (NPAD, D))
        type_table = dram("type_table", (NPAD * KT, D))
        reverse = [dram(f"reverse{r}", (RROWS, RC)) for r in range(R)]
        index_table = dram("index_table", (2, P, SPAD), I32)
        path_rows = dram("path_rows", (2 * CG, P), I32)

        X = sb("X", [P, NB, D])
        H = sb("H", [P, NB, D])
        tmp = sb("tmp", [P, NB, D])
        acc = sb("acc", [P, 50 * RC])
        big = sb("big", [P, NB * 2 * M])
        small = sb("small", [P, 4, NB])
        norm = sb("norm", [P, NB])
        deg = sb("deg", [P, NB])
        dloc = sb("dloc", [P, SPAD], I16)
        key = sb("key", [P, SPAD])
        path = sb("path", [1, 2 * SPAD], I32)
        icol = sb("icol", [P, CG], I32)
        fcol = sb("fcol", [P, 4, CG])
        tcol = sb("tcol", [P, CG], I32)
        pcol = sb("pcol", [CG, 2, P], I32)
        ident = sb("ident", [P, P])
        iota = sb("iota", [P, P])
        earlier = sb("earlier", [P, P])
        trash = sb("trash", [P, 1])
        ones = sb("ones", [1, P])
        ones2 = sb("ones2", [2, P], BF16)
        gbias = sb("gbias", [2, PARTS, 4 * D], BF16)
        gleft = sb("gleft", [2, 4 * D])
        hold_in = sb("hold_in", [P, 1])
        hold_out = sb("hold_out", [P, 1])
        scatter_hold = sb("scatter_hold", [P, 1])
        types_hold = sb("types_hold", [P, 1])
        hold2 = sb("hold2", [P, 1])
        hidden = sb("hidden", [P, 2, P])
        idx = sb("idx", [P, SLOTS], I32)
        G = sb("G", [P, SLOTS, KV])
        OH = sb("OH", [P, HOT, P])
        OT = sb("OT", [P, 2, GR * P])
        prod = sb("prod", [P, 2, P])
        sc = sb("sc", [P, 3, 2, GR])
        MS = sb("MS", [P, MR, 2 * M + 2])
        EQ = sb("EQ", [P, MR, P])
        cnt = sb("cnt", [P, 2, MR])
        sidx = sb("sidx", [P, U], I32)
        SD = sb("SD", [P, R, RC])
        keyslot = sb("keyslot", [P, U])
        keyless = sb("keyless", [P, U])
        S = sb("S", [P, 2, 3 * M])
        ST = OT[:, :, 0:3 * P]
        Sf = S[:, :, :].rearrange("p a b -> p (a b)")
        S4 = Sf[:, 0:2 * GN * (D + 1)].rearrange("p (s n c) -> p s n c", s=2, n=GN)
        S2 = Sf[:, 0:2 * G2 * 2 * D].rearrange("p (s n c) -> p s n c", s=2, n=G2)
        GX = big[:, 0:2 * G2 * 7 * D].rearrange("p (s n c) -> p s n c", s=2, n=G2)
        NX = sb("NX", [P, 2, 4 * M])
        Gf = G[:, :, :].rearrange("p a b -> p (a b)")
        itile, irtrash, iiota = (Gf[:, lo:hi].bitcast(I32) for lo, hi in ((0, T), (T, T + SPAD), (T + SPAD, T + SPAD + P)))
        srci, tsrci = (Gf[:, q * SPAD:(q + 1) * SPAD].bitcast(I32) for q in range(2))
        revs = Gf[:, 0:2 * R * RC].rearrange("p (s r c) -> p s r c", s=2, r=R)
        W = sb("W", [P, WTOTAL])
        lng = sb("lng", [P, 3, D])
        bank = [ctx.enter_context(nc.psum_tensor(f"bank{i}", [P, 512], F32)) for i in range(8)]

        def w(name, rows=P):
            lo, hi = WCOLS[name]
            return W[0:rows, lo:hi]

        messages = MS[:, :, :].rearrange("p a b -> p (a b)")[:, 0:2 * GR * AC].rearrange("p (s n c) -> p s n c", s=2, n=GR)
        acc_ = {c: acc[:, 0:NB * c] for c in (AC, D, M)}
        big_kv = big[:, 0:NB * KV]
        split = big[:, NB * KV + 1:NB * KV + 1 + NB * PARTS * D // 2].bitcast(BF16)
        OTb = OT[:, :, :].bitcast(BF16)[:, :, 0:GR * P]
        X_, H_, tmp_ = X[:, :, :], H[:, :, :], tmp[:, :, :]
        flat = {id(t): t.rearrange("p b d -> p (b d)") for t in (X_, H_, tmp_)}
        Xf, Hf, tmpf = (flat[id(t)] for t in (X_, H_, tmp_))

        def part(t, k, width, lo=0, hi=None):
            hi = width if hi is None else hi
            if known(k):
                return t[:, k * width + lo:k * width + hi]
            return t[:, bass.ds(k * width + lo, hi - lo)]

        x_loaded, dst_loaded, w_loaded, reverse_zero = (sem(n) for n in ("x_loaded", "dst_loaded", "w_loaded", "reverse_zero"))
        acc_zero, consts, path_f, tiles_known = (sem(n) for n in ("acc_zero", "consts", "path_f", "tiles_known"))
        tiles_read = sem("tiles_read")
        path_turned, path_copied, path_stored, path_loaded = (sem(n) for n in ("path_turned", "path_copied", "path_stored", "path_loaded"))
        idx_made, idx_turned, idx_tabled = (sem(n) for n in ("idx_made", "idx_turned", "idx_tabled"))
        chain = sem("chain")
        root_in, root_out = sem("root_in"), sem("root_out")
        table_ready, table_stored = sem("table_ready"), sem("table_stored")
        gathered = [sem(f"gathered{j}") for j in range(UGR)]
        tile_rows = [sem(f"tile_rows{q}") for q in range(3)]
        edge_loaded = [sem(f"edge_loaded{j}") for j in range(HALF)]
        scattered = [sem(f"scattered{r}") for r in range(R)]
        gather_go, scatter_go = sem("gather_go"), sem("scatter_go")
        index_stored = sem("index_stored")
        idx_loaded = [sem(f"idx_loaded{half}") for half in range(2)]
        rev_loaded = [sem(f"rev_loaded{r}") for r in range(2)]
        pass_begun = sem("pass_begun")
        gru_acc_zero = sem("gru_acc_zero")
        types_stored, types_go = sem("types_stored"), sem("types_go")
        result, result_stored = sem("result"), sem("result_stored")

        class Sems:
            def __init__(self, phase, names):
                self.at = {n: sem(f"{phase}_{n}") for n in names.split()}

            def __getitem__(self, n):
                return self.at[n]

        node = Sems("node", "rows turned copied product finished")
        QKV, ATTN, CONV, PAIR, TYPES = (n * NQ for n in range(5))
        att = Sems("att", "onehot turned copied query score scored clipped exp msg seg summed")
        mes = Sems("mes", "less keys keyrow equal count rep index onehot turned copied pre relu seg summed rowsout")
        plain = Sems("plain", "onehot seg summed")
        upd = Sems("upd", "sums rows turned copied agg aggout hid hidout product finished")
        gru = Sems("gru", "rows turned copied product gates mul add tanh diff blend finished")

        block = ctx.enter_context(nc.Block())

        def apart(t, n):
            return t.rearrange("p (n c) -> p n c", n=n)

        def node_pe(pe, s, rows, wt, width, base=0):
            def turn(k, j, it):
                pe.wait_ge(s["rows"], base + k + 1)
                if not (known(k) and k < 2):
                    pe.wait_ge(s["copied"], base + k - 1)
                for n in range(blocks_in(k, GN)):
                    last = nc.tensor.transpose(bank[j % 2][0:rows, n * P:(n + 1) * P], S4[:, j % 2, n, 0:rows], ident[:, :])
                last.then_inc(s["turned"], 1)

            def mul(k, j, it):
                pe.wait_ge(s["copied"], base + k + 1)
                if not (known(k) and k < 2):
                    pe.wait_ge(s["finished"], base + k - 1)
                for n in range(blocks_in(k, GN)):
                    at = n * width
                    last = nc.tensor.matmul(bank[2 + 2 * (j % 2) + at // 512][:, at % 512:at % 512 + width],
                                            OT[0:rows, j % 2, n * P:(n + 1) * P], wt, start=True, stop=True)
                last.then_inc(s["product"], 1)

            def emit(it, j):
                stage(NQ, UQ, it, j, 0, turn)
                stage(NQ, UQ, it, j, 1, mul)
            pipeline(pe, NQ, UQ, 1, emit)

        def node_act(act, s, rows, base=0):
            def copy(k, j, it):
                act.wait_ge(s["turned"], base + k + 1)
                if not (known(k) and k < 2):
                    act.wait_ge(s["product"], base + k - 1)
                cols = blocks_in(k, GN) * P
                nc.scalar.activation(OT[0:rows, j % 2, 0:cols], bank[j % 2][0:rows, 0:cols], ACT.Copy).then_inc(s["copied"], 1)
            pipeline(act, NQ, UQ, 0, lambda it, j: stage(NQ, UQ, it, j, 0, copy))

        def node_dve(v, s, source, width, finish, base=0):
            def rows(k, j, it):
                n = blocks_in(k, GN)
                if not (known(k) and k < 2):
                    v.wait_ge(s["turned"], base + k - 1)
                nc.vector.tensor_copy(S4[:, j % 2, 0:n, 0:D], apart(part(source, k, GN * D, 0, n * D), n)).then_inc(s["rows"], 1)

            def end(k, j, it):
                n, per = blocks_in(k, GN), min(GN, 512 // width)
                v.wait_ge(s["product"], base + k + 1)
                for first in range(0, n, per):
                    m = min(per, n - first)
                    last = finish(k, first, m, apart(bank[2 + 2 * (j % 2) + first // per][:, 0:m * width], m))
                last.then_inc(s["finished"], 1)

            def emit(it, j):
                stage(NQ, UQ, it, j, 0, rows)
                stage(NQ, UQ, it, j, 2, end)
            pipeline(v, NQ, UQ, 2, emit)

        def group(t, k, first, m, width):
            return apart(part(t, k, GN * width, first * width, (first + m) * width), m)

        def gather(pool, before, turns, table, width, used, used_base, also=None, lag=0, per=1):
            def get(k, j, it):
                if j % HS == 0:
                    half = j // HS
                    pool.wait_ge(idx_loaded[half], (before[half] + it + 1) * 16)
                    if not (known(k) and k < SLOTS):
                        pool.wait_ge(used, used_base + it * (UP // per) + (j - HS) // per)
                    pool.wait_ge(gather_go, turns + (it * 2 + half) + 1)
                    nc.gpsimd.tensor_tensor(hold_out[:, :], hold_in[:, :], hold_in[:, :], ALU.add)\
                        .then_inc(gather_go, 1)
                nc.gpsimd.indirect_dma_start(G[:, j, 0:width], None, table,
                                             bass.IndirectOffsetOnAxis(idx[:, j:j + 1], 0))\
                    .then_inc(gathered[j // GR], 16)

            def emit(it, j):
                stage(STEPS, UP, it, j, 0, get)
                if also:
                    stage(STEPS, UP, it, j, lag, also)
            pipeline(pool, STEPS, UP, lag, emit)

        def arrived(before, j, it):
            return (before[j // (UGR // 2)] + it + 1) * (16 * GR)

        def passes(n):
            return tuple(n * r for r in ROUNDS)

        def layers(layer):
            return tuple(layer * r + 3 * r for r in ROUNDS)

        def blocks_of(eng, k):
            _, b = nc.values_load_multi_w_load_instructions(
                path[0:1, k:k + GR] if known(k) else path[0:1, bass.ds(k, GR)], engines=(eng.engine,), min_val=0, max_val=NB - 1,
                skip_runtime_bounds_check_because="the path visits blocks of nodes only")
            return b

        def near(eng, held, k, j):
            if known(k):
                return eng.value_load(path[0:1, k:k + 1], min_val=0, max_val=NB - 1)
            if j % GR == 0:
                held["blocks"] = blocks_of(eng, k)
            return held["blocks"][j % GR]

        def onehots(group, slot):
            n = slot * GR % HOT
            return nc.vector.tensor_tensor(
                OH[:, n:n + GR, :], iota[:, :].unsqueeze(1).to_broadcast([P, GR, P]),
                part(dloc[:, :], group, GR).unsqueeze(2).to_broadcast([P, GR, P]), ALU.is_equal)

        def hot(v, s, base):
            def body(q, j, it):
                if not (known(q) and q < OHG):
                    v.wait_ge(s["seg"], base + q - OHG + 1)
                onehots(q, j).then_inc(s["onehot"], 1)
            return body

        def sum_up(v, s, base, width, banks):
            held = {}

            def addition(n):
                def body(q, j, it):
                    if n == 0:
                        held["blocks"] = blocks_of(v, q * GR)
                        v.wait_ge(s["seg"], base + q + 1)
                    if not (known(q) and q == 0 and n == 0):
                        v.wait_ge(s["summed"], (base + q) * GR + n)
                    to = acc_[width][:, bass.ds(held["blocks"][n] * width, width)]
                    nc.vector.tensor_tensor(to, to, banks[j % 2][:, n * width:(n + 1) * width], ALU.add)\
                        .then_inc(s["summed"], 1)
                return body
            return [addition(n) for n in range(GR)]

        def plain_pe(pe, s, before, base):
            def seg(q, j, it):
                pe.wait_ge(gathered[j], arrived(before, j, it))
                pe.wait_ge(s["onehot"], base + q + 1)
                if not (known(q) and q < 2):
                    pe.wait_ge(s["summed"], (base + q - 1) * GR)
                for n in range(GR):
                    last = nc.tensor.matmul(bank[j % 2][:, n * D:(n + 1) * D], OH[:, (j * GR + n) % HOT, :],
                                            G[:, j * GR + n, 0:D],
                                            start=True, stop=True)
                last.then_inc(s["seg"], 1)
            pipeline(pe, NG, UGR, 0, lambda it, j: stage(NG, UGR, it, j, 0, seg))

        def plain_dve(v, s, base):
            one, adds = hot(v, s, base), sum_up(v, s, base, D, bank[0:2])

            def emit(it, j):
                stage(NG, UGR, it, j, 0, one)
                for add in adds:
                    stage(NG, UGR, it, j, 1, add)
            pipeline(v, NG, UGR, 1, emit)

        @block.sync
        def _(sp):
            sp.dma_start(big[:, 0:T].bitcast(I32), a["dst_last"].partition_broadcast(P)).then_inc(dst_loaded, 16)
            sp.dma_start(X_, a["x"].rearrange("(b p) d -> p b d", p=P)).then_inc(x_loaded, 16)
            sp.dma_start(W[:, :], a["weights"]).then_inc(w_loaded, 16)
            sp.dma_start(lng[:, :, :].rearrange("p a d -> p (a d)"), a["vectors"].partition_broadcast(P)).then_inc(w_loaded, 16)
            sp.wait_ge(acc_zero, 1)
            for r in range(R):
                sp.dma_start(reverse[r].rearrange("(p q) d -> p (q d)", p=P), acc[:, 0:50 * RC]).then_inc(reverse_zero, 16)
            sp.wait_ge(path_copied, 2)
            sp.dma_start(path_rows.rearrange("(a c) p -> c a p", a=2), pcol[:, :, :]).then_inc(path_stored, 16)
            sp.wait_ge(path_stored, 16)
            sp.dma_start(path[:, :], path_rows.rearrange("(o c) p -> o (c p)", o=1)).then_inc(path_loaded, 16)

            def store(table, source, n, width):
                sp.wait_ge(table_ready, n)
                sp.dma_start(table.rearrange("(b p) d -> p b d", p=P),
                             source.rearrange("p (b d) -> p b d", d=width)).then_inc(table_stored, 16)

            def fetch(before, which, r, half, it):
                first = r * HS if known(r) else sp.snap(r * HS)
                if not (known(it) and known(before[half]) and before[half] + it == 0):
                    over = (before[half] + it) * (16 * GR)
                    over = over if known(over) else sp.snap(over)
                    for g in range(half * UGR // 2, (half + 1) * UGR // 2):
                        sp.wait_ge(gathered[g], over)
                sp.dma_start(idx[:, half * HS:(half + 1) * HS], index_table[which][:, bass.ds(first, HS)])\
                    .then_inc(idx_loaded[half], 16)

            def fetches(before, which):
                pipeline(sp, TURNS, 2, 0, lambda it, j: stage(TURNS, 2, it, j, 0, lambda r, half, n: fetch(
                    before, which, r, half, n)))

            sp.wait_ge(idx_tabled, 4 * IDXQ)
            for which, t in enumerate((srci, tsrci)):
                sp.dma_start(index_table[which], t).then_inc(index_stored, 16)
            sp.wait_ge(index_stored, 32)
            store(kv_table, big_kv, 1, KV)
            fetches(passes(0), 0)
            store(h_table, tmpf, 2, D)
            fetches(passes(1), 0)
            store(h_table, Hf, 3, D)
            fetch(passes(2), 0, 0, 0, 0)

            sp.wait_ge(table_stored, 48)
            sp.wait_ge(path_loaded, 16)
            def features(k, j, it):
                if j % HS == 0 and not (known(k) and k + HS >= STEPS):
                    ahead = j // HS + 1
                    fetch(passes(2), 0, k // HS + 1 if known(k) else it * 2 + ahead, ahead % 2, it + ahead // 2)
                t = sp.value_load(path[0:1, SPAD + k:SPAD + k + 1] if known(k) else path[0:1, bass.ds(k + SPAD, 1)],
                                  min_val=0, max_val=T)
                first = sp.snap(t * P)
                if not (known(k) and k < HALF):
                    sp.wait_ge(mes["turned"], k - HALF + 1)
                sp.dma_start(G[:, j, D:2 * D], a["edge"][bass.ds(first, P), :]).then_inc(edge_loaded[j % HALF], 16)
            pipeline(sp, STEPS, U, 0, lambda it, j: stage(STEPS, U, it, j, 0, features))

            for r in range(R):
                sp.wait_ge(scattered[r], 16 * (STEPS // R))
            def sums(k, j, it):
                first = k * P if known(k) else sp.snap(k * P)
                if not (known(k) and k < 2):
                    sp.wait_ge(upd["rows"], k - 1)
                for r in range(R):
                    sp.dma_start(revs[:, j % 2, r, :], reverse[r][bass.ds(first, P), :]).then_inc(rev_loaded[j % 2], 16)
            pipeline(sp, NB, UN, 0, lambda it, j: stage(NB, UN, it, j, 0, sums))

            half = NQ // 2 * GN
            halves = ((0, half), (half, NB))
            with sp.Fori(0, LAYERS) as layer:
                for lo, hi in halves:
                    sp.wait_ge(node["finished"], layer * NQ + (TYPES + -(-hi // GN)))
                    sp.dma_start(type_table.rearrange("(b p t) d -> p b (t d)", p=P, t=KT)[:, lo:hi, :],
                                 big[:, :].rearrange("p (b c) -> p b c", c=KT * D)[:, lo:hi, :]).then_inc(types_stored, 16)
                fetches(layers(layer), 1)
            sp.wait_ge(types_stored, TYPES_DONE * LAYERS)
            sp.wait_ge(result, 1)
            full = N // P
            sp.dma_start(out[0:full * P, :].rearrange("(b p) d -> p b d", p=P), X[:, 0:full, :]).then_inc(result_stored, 16)
            sp.dma_start(out[full * P:N, :], X[0:N - full * P, full, :]).then_inc(result_stored, 16)
            sp.wait_ge(result_stored, 32)

        @block.gpsimd
        def _(pool):
            nc.gpsimd.iota(itile, pattern=[[1, T]], base=0, channel_multiplier=0).then_inc(consts, 1)
            nc.gpsimd.iota(icol[:, :], pattern=[[P, CG]], base=0, channel_multiplier=1).then_inc(consts, 1)
            nc.gpsimd.iota(irtrash, pattern=[[0, CG], [1, P]], base=TRASH, channel_multiplier=0).then_inc(consts, 1)
            nc.gpsimd.iota(idx[:, 0:1], pattern=[[0, 1]], base=TRASH, channel_multiplier=1).then_inc(consts, 1)
            nc.gpsimd.iota(iiota, pattern=[[1, P]], base=0, channel_multiplier=0).then_inc(consts, 1)
            nc.gpsimd.memset(ident[:, :], 0.0).then_inc(consts, 1)
            nc.gpsimd.memset(earlier[:, :], 1.0).then_inc(consts, 1)
            nc.gpsimd.memset(hold_in[:, :], 0.0).then_inc(consts, 1)
            nc.gpsimd.memset(ones[:, :], 1.0).then_inc(consts, 1)
            pool.wait_ge(consts, 9)
            nc.gpsimd.affine_select(out=ident[:, :], in_=ident[:, :], compare_op=ALU.not_equal, fill=1.0, base=0,
                                    pattern=[[-1, P]], channel_multiplier=1).then_inc(consts, 1)
            nc.gpsimd.affine_select(out=earlier[:, :], in_=earlier[:, :], compare_op=ALU.is_gt, fill=0.0, base=0,
                                    pattern=[[-1, P]], channel_multiplier=1).then_inc(consts, 1)
            nc.gpsimd.tensor_tensor(hold_out[:, :], hold_in[:, :], hold_in[:, :], ALU.add).then_inc(gather_go, 1)

            pool.wait_ge(tiles_known, 1)
            for q, name in enumerate(("dst", "src", "type")):
                for c in range(CG):
                    lo = (2 + q) * SPAD + c * P
                    nc.gpsimd.indirect_dma_start(big[:, lo:lo + P].bitcast(I32), None, a[name],
                                                 bass.IndirectOffsetOnAxis(tcol[:, c:c + 1], 0))\
                        .then_inc(tile_rows[q], 16)
            for q in range(3):
                pool.wait_ge(tile_rows[q], 16 * CG)
            nc.gpsimd.tensor_copy(hold_in[:, :], hold_in[:, :]).then_inc(tiles_read, 1)
            pool.wait_ge(tiles_read, 1)

            pool.wait_ge(idx_tabled, 4 * IDXQ)
            pool.wait_ge(table_stored, 16)
            gather(pool, passes(0), 0, kv_table, KV, att["msg"], 0, per=GR)
            pool.wait_ge(table_stored, 32)
            gather(pool, passes(1), TURNS, h_table, D, plain["seg"], 0, per=GR)
            pool.wait_ge(table_stored, 48)
            pool.wait_ge(reverse_zero, 16 * R)

            def scatter(k, j, it):
                if j % 2 == 0:
                    pool.wait_ge(mes["index"], k + 2)
                    pool.wait_ge(mes["rowsout"], k + 2)
                    if not (known(k) and k < R):
                        for r in (j % R, j % R + 1):
                            pool.wait_ge(scattered[r], (it * (UP // R) + j // R) * 16)
                    if not (known(k) and k < 1):
                        pool.wait_ge(scatter_go, k // 2 if known(k) else it * (UP // 2) + j // 2)
                    nc.gpsimd.tensor_tensor(scatter_hold[:, :], hold_in[:, :], hold_in[:, :], ALU.add).then_inc(scatter_go, 1)
                nc.gpsimd.indirect_dma_start(reverse[j % R], bass.IndirectOffsetOnAxis(sidx[:, j:j + 1], 0),
                                             SD[:, j % R, :], None, compute_op=ALU.add).then_inc(scattered[j % R], 16)
            gather(pool, passes(2), 2 * TURNS, h_table, D, mes["turned"], 0, also=scatter, lag=16)
            with pool.Fori(0, LAYERS) as layer:
                pool.wait_ge(types_stored, layer * TYPES_DONE + TYPES_DONE)
                nc.gpsimd.tensor_tensor(types_hold[:, :], hold_in[:, :], hold_in[:, :], ALU.add).then_inc(types_go, 1)
                pool.wait_ge(types_go, layer + 1)
                gather(pool, layers(layer), layer * TURNS + 3 * TURNS, type_table, D, plain["seg"], layer * NG + NG, per=GR)

        @block.scalar
        def _(act):
            def root(n):
                act.wait_ge(root_in, n)
                nc.scalar.activation(small[:, 0, :], small[:, 3, :], ACT.Sqrt).then_inc(root_out, 1)

            root(1)
            node_act(act, node, D + 1, QKV)

            def copy(q, j, it):
                act.wait_ge(att["turned"], q + 1)
                if not (known(q) and q < 2):
                    act.wait_ge(att["query"], q - 1)
                nc.scalar.activation(OTb[:, j % 2, :], bank[j % 2][:, :], ACT.Copy).then_inc(att["copied"], 1)

            def exp(q, j, it):
                act.wait_ge(att["clipped"], q + 1)
                if not (known(q) and q < 2):
                    act.wait_ge(att["msg"], q - 1)
                nc.scalar.activation(sc[:, 2, j % 2, :], sc[:, 1, j % 2, :], ACT.Exp).then_inc(att["exp"], 1)

            def emit(it, j):
                stage(NG, UGR, it, j, 0, copy)
                stage(NG, UGR, it, j, 2, exp)
            pipeline(act, NG, UGR, 2, emit)
            root(2)
            node_act(act, node, D + 1, ATTN)
            root(3)
            root(4)
            node_act(act, node, D + 1, CONV)
            root(5)
            node_act(act, node, D + 1, PAIR)

            def copy2(k, j, it):
                act.wait_ge(mes["turned"], k + 1)
                if not (known(k) and k < 2):
                    act.wait_ge(mes["pre"], k - 1)
                nc.scalar.activation(OT[:, j % 2, 0:2 * P], bank[j % 2][:, 0:2 * P], ACT.Copy).then_inc(mes["copied"], 1)

            def relu(k, j, it):
                act.wait_ge(mes["pre"], k + 1)
                if not (known(k) and k < MR):
                    act.wait_ge(mes["seg"], k - MR + 1)
                nc.scalar.activation(MS[:, j % MR, 0:2 * M], bank[2 + j % 2][:, 0:2 * M], ACT.Relu).then_inc(mes["relu"], 1)

            def rowsout(k, j, it):
                act.wait_ge(mes["seg"], k + 1)
                if not (known(k) and k < R):
                    act.wait_ge(scattered[j % R], (it * (U // R) + j // R) * 16)
                nc.scalar.activation(SD[:, j % R, :], bank[4 + j % 2][:, 0:RC], ACT.Copy).then_inc(mes["rowsout"], 1)

            def emit2(it, j):
                stage(STEPS, U, it, j, 0, copy2)
                stage(STEPS, U, it, j, 2, relu)
                stage(STEPS, U, it, j, 4, rowsout)
            pipeline(act, STEPS, U, 4, emit2)

            def turned(k, j, it):
                act.wait_ge(upd["turned"], k + 1)
                if not (known(k) and k < 2):
                    act.wait_ge(upd["hid"], k - 1)
                nc.scalar.activation(ST[:, j % 2, 0:2 * P], bank[j % 2][:, 0:2 * P], ACT.Copy)
                nc.scalar.activation(ST[0:D + 2, j % 2, 2 * P:3 * P], bank[j % 2][0:D + 2, 2 * P:3 * P], ACT.Copy)\
                    .then_inc(upd["copied"], 1)

            def aggout(k, j, it):
                act.wait_ge(upd["agg"], k + 1)
                if not (known(k) and k < 2):
                    act.wait_ge(upd["hid"], k - 1)
                nc.scalar.activation(NX[:, j % 2, 2 * RC:2 * RC + P], bank[2 + j % 2][:, 0:P], ACT.Copy).then_inc(upd["aggout"], 1)

            def hidout(k, j, it):
                act.wait_ge(upd["hid"], k + 1)
                if not (known(k) and k < 2):
                    act.wait_ge(upd["product"], k - 1)
                nc.scalar.activation(hidden[:, j % 2, :], bank[4 + j % 2][:, 0:P], ACT.Relu, bias=w("bn1"))\
                    .then_inc(upd["hidout"], 1)

            def emit3(it, j):
                stage(NB, UN, it, j, 0, turned)
                stage(NB, UN, it, j, 1, aggout)
                stage(NB, UN, it, j, 2, hidout)
            pipeline(act, NB, UN, 2, emit3)
            root(6)

            with act.Fori(0, LAYERS) as layer:
                nbase, gbase = layer * NQ, layer * NP2
                node_act(act, node, D + 1, nbase + TYPES)

                def gturned(k, j, it):
                    cols = blocks_in(k, G2) * P
                    act.wait_ge(gru["turned"], gbase + k + 1)
                    if not (known(k) and k < 2):
                        act.wait_ge(gru["product"], gbase + k - 1)
                    nc.scalar.activation(OT[:, j % 2, 0:cols], bank[j % 2][:, 0:cols], ACT.Copy).then_inc(gru["copied"], 1)

                def gates(k, j, it):
                    n = blocks_in(k, G2)
                    act.wait_ge(gru["product"], gbase + k + 1)
                    if not (known(k) and k < 2):
                        act.wait_ge(gru["finished"], gbase + k - 1)
                    nc.scalar.activation(GX[:, j % 2, 0:n, 0:2 * D], apart(bank[2 + j % 2][:, 0:n * 4 * D], n)[:, :, 0:2 * D],
                                         ACT.Sigmoid).then_inc(gru["gates"], 1)

                def tanh(k, j, it):
                    n = blocks_in(k, G2)
                    act.wait_ge(gru["add"], gbase + k + 1)
                    nc.scalar.activation(GX[:, j % 2, 0:n, 4 * D:5 * D], GX[:, j % 2, 0:n, 3 * D:4 * D], ACT.Tanh)\
                        .then_inc(gru["tanh"], 1)

                def gemit(it, j):
                    stage(NP2, UG, it, j, 0, gturned)
                    stage(NP2, UG, it, j, 1, gates)
                    stage(NP2, UG, it, j, 2, tanh)
                pipeline(act, NP2, UG, 2, gemit)

        @block.tensor
        def _(pe):
            pe.wait_ge(consts, 11)
            pe.wait_ge(path_f, 1)
            for q in range(2):
                nc.tensor.transpose(bank[4 + q][0:CG, 0:P], fcol[:, 2 - q, :], ident[:, :]).then_inc(path_turned, 1)
            for q, srct in enumerate((big[:, 0:SPAD], Hf[:, 0:SPAD], tmpf[:, 0:SPAD], big[:, 5 * SPAD:6 * SPAD])):
                pe.wait_ge(idx_made, 4)
                for g in range(IDXQ):
                    n = q * IDXQ + g
                    if n >= 2:
                        pe.wait_ge(idx_tabled, n - 1)
                    cols = range(4 * g, min(4 * g + 4, CG))
                    for c in cols:
                        last = nc.tensor.transpose(bank[n % 2][:, (c - 4 * g) * P:(c - 4 * g + 1) * P],
                                                   srct[:, c * P:(c + 1) * P], ident[:, :])
                    last.then_inc(idx_turned, 1)
            pe.wait_ge(idx_tabled, 4 * IDXQ)
            pe.wait_ge(w_loaded, 32)
            node_pe(pe, node, D + 1, w("qkv", D + 1), 2 * D, QKV)

            def turn(q, j, it):
                pe.wait_ge(att["onehot"], q + 1)
                if not (known(q) and q < 2):
                    pe.wait_ge(att["copied"], q - 1)
                for n in range(GR):
                    last = nc.tensor.transpose(bank[j % 2][:, n * P:(n + 1) * P], OH[:, (j * GR + n) % HOT, :], ident[:, :])
                last.then_inc(att["turned"], 1)

            def query(q, j, it):
                blocks = blocks_of(pe, q * GR)
                pe.wait_ge(att["copied"], q + 1)
                if not (known(q) and q < 2):
                    pe.wait_ge(att["score"], q - 1)
                for n, b in enumerate(blocks):
                    for m in range(PARTS):
                        last = nc.tensor.matmul(bank[2 + j % 2][:, n * D:(n + 1) * D], OTb[:, j % 2, n * P:(n + 1) * P],
                                                split[:, bass.ds(b * (PARTS * D) + m * D, D)],
                                                start=m == 0, stop=m == PARTS - 1)
                last.then_inc(att["query"], 1)

            def seg(q, j, it):
                pe.wait_ge(att["msg"], q + 1)
                if not (known(q) and q < 2):
                    pe.wait_ge(att["summed"], (q - 1) * GR)
                for n in range(GR):
                    last = nc.tensor.matmul(bank[4 + j % 2][:, n * AC:(n + 1) * AC], OH[:, (j * GR + n) % HOT, :],
                                            messages[:, j % 2, n, :], start=True, stop=True)
                last.then_inc(att["seg"], 1)

            pe.wait_ge(path_loaded, 16)
            pe.wait_ge(pass_begun, 1)

            def emit(it, j):
                stage(NG, UGR, it, j, 4, seg)
                stage(NG, UGR, it, j, 0, turn)
                stage(NG, UGR, it, j, 1, query)
            pipeline(pe, NG, UGR, 4, emit)
            node_pe(pe, node, D + 1, w("attn", D + 1), D, ATTN)
            plain_pe(pe, plain, passes(1), 0)
            node_pe(pe, node, D + 1, w("conv", D + 1), D, CONV)
            node_pe(pe, node, D + 1, w("pair", D + 1), 2 * M, PAIR)

            def keyrow(k, j, it):
                pe.wait_ge(mes["keys"], it * (U // HALF) + j // HALF + 1)
                if not (known(k) and k < 1):
                    pe.wait_ge(mes["equal"], k)
                nc.tensor.transpose(bank[7][:, 0:P], keyslot[:, j:j + 1].to_broadcast([P, P]), ident[:, :])\
                    .then_inc(mes["keyrow"], 1)

            def turn2(k, j, it):
                if j % GR == 0:
                    pe.wait_ge(mes["onehot"], it * (U // GR) + j // GR + 1)
                    pe.wait_ge(gathered[j // GR], arrived(passes(2), j // GR, it))
                pe.wait_ge(edge_loaded[j % HALF], (it * (U // HALF) + j // HALF + 1) * 16)
                if not (known(k) and k < 2):
                    pe.wait_ge(mes["copied"], k - 1)
                nc.tensor.transpose(bank[j % 2][:, P:2 * P], OH[:, j % HOT, :], ident[:, :])
                nc.tensor.transpose(bank[j % 2][:, 0:P], G[:, j, 0:2 * D], ident[:, :]).then_inc(mes["turned"], 1)

            held = {}

            def pre(k, j, it):
                b = near(pe, held, k, j + 1)
                pe.wait_ge(mes["copied"], k + 1)
                if not (known(k) and k < 2):
                    pe.wait_ge(mes["relu"], k - 1)
                nc.tensor.matmul(bank[2 + j % 2][:, 0:2 * M], OT[:, j % 2, 0:P], w("edge"), start=True, stop=False)
                nc.tensor.matmul(bank[2 + j % 2][:, 0:2 * M], OT[:, j % 2, P:2 * P], big[:, bass.ds(b * 2 * M, 2 * M)],
                                 start=False, stop=True).then_inc(mes["pre"], 1)

            def seg2(k, j, it):
                pe.wait_ge(mes["relu"], k + 1)
                pe.wait_ge(mes["equal"], k + 1)
                if not (known(k) and k < 1):
                    pe.wait_ge(mes["summed"], k)
                if not (known(k) and k < 2):
                    pe.wait_ge(mes["rowsout"], k - 1)
                nc.tensor.matmul(bank[6][:, 0:M], OH[:, j % HOT, :], MS[:, j % MR, 0:M], start=True, stop=True)
                nc.tensor.matmul(bank[4 + j % 2][:, 0:RC], EQ[:, j % MR, :], MS[:, j % MR, M:M + RC],
                                 start=True, stop=True).then_inc(mes["seg"], 1)

            pe.wait_ge(pass_begun, 2)

            def emit2(it, j):
                stage(STEPS, U, it, j, 0, keyrow)
                stage(STEPS, U, it, j, 0, turn2)
                stage(STEPS, U, it, j, 1, pre)
                stage(STEPS, U, it, j, 3, seg2)
            pipeline(pe, STEPS, U, 3, emit2)

            def uturn(k, j, it):
                pe.wait_ge(upd["rows"], k + 1)
                if not (known(k) and k < 2):
                    pe.wait_ge(upd["copied"], k - 1)
                for c, width in ((0, P), (1, P), (2, D + 2)):
                    last = nc.tensor.transpose(bank[j % 2][0:width, c * P:(c + 1) * P],
                                               S[:, j % 2, c * P:c * P + width], ident[:, :])
                last.then_inc(upd["turned"], 1)

            def agg(k, j, it):
                pe.wait_ge(upd["copied"], k + 1)
                if not (known(k) and k < 2):
                    pe.wait_ge(upd["aggout"], k - 1)
                o = bank[2 + j % 2][:, 0:P]
                nc.tensor.matmul(o, w("f2"), ST[:, j % 2, 0:P], start=True, stop=False)
                nc.tensor.matmul(o, w("r2"), ST[:, j % 2, P:2 * P], start=False, stop=False)
                nc.tensor.matmul(o, w("b2", 2), ST[0:2, j % 2, 2 * P:3 * P], start=False, stop=True).then_inc(upd["agg"], 1)

            def hid(k, j, it):
                pe.wait_ge(upd["aggout"], k + 1)
                if not (known(k) and k < 2):
                    pe.wait_ge(upd["hidout"], k - 1)
                o = bank[4 + j % 2][:, 0:P]
                nc.tensor.matmul(o, w("n1a"), NX[:, j % 2, 2 * RC:2 * RC + P], start=True, stop=False)
                nc.tensor.matmul(o, w("n1b", D + 2), ST[0:D + 2, j % 2, 2 * P:3 * P], start=False, stop=True)\
                    .then_inc(upd["hid"], 1)

            def product(k, j, it):
                pe.wait_ge(upd["hidout"], k + 1)
                if not (known(k) and k < 2):
                    pe.wait_ge(upd["finished"], k - 1)
                o = bank[6 + j % 2][:, 0:D]
                nc.tensor.matmul(o, hidden[:, j % 2, :], w("n2"), start=True, stop=False)
                nc.tensor.matmul(o, ones[0:1, :], w("bn2", 1), start=False, stop=True).then_inc(upd["product"], 1)

            def emit3(it, j):
                stage(NB, UN, it, j, 0, uturn)
                stage(NB, UN, it, j, 1, agg)
                stage(NB, UN, it, j, 2, hid)
                stage(NB, UN, it, j, 3, product)
            pipeline(pe, NB, UN, 3, emit3)

            with pe.Fori(0, LAYERS) as layer:
                nbase, gbase = layer * NQ, layer * NP2
                node_pe(pe, node, D + 1, w("types", D + 1), KT * D, nbase + TYPES)
                plain_pe(pe, plain, layers(layer), layer * NG + NG)

                def gturn(k, j, it):
                    pe.wait_ge(gru["rows"], gbase + k + 1)
                    if not (known(k) and k < 2):
                        pe.wait_ge(gru["copied"], gbase + k - 1)
                    for n in range(blocks_in(k, G2)):
                        last = nc.tensor.transpose(bank[j % 2][:, n * P:(n + 1) * P], S2[:, j % 2, n, :], ident[:, :])
                    last.then_inc(gru["turned"], 1)

                def gmul(k, j, it):
                    pe.wait_ge(gru["copied"], gbase + k + 1)
                    if not (known(k) and k < 2):
                        pe.wait_ge(gru["add"], gbase + k - 1)
                    for n in range(blocks_in(k, G2)):
                        o = bank[2 + j % 2][:, n * 4 * D:(n + 1) * 4 * D]
                        nc.tensor.matmul(o, OT[:, j % 2, n * P:(n + 1) * P], w("gru"), start=True, stop=False)
                        for m in range(PARTS):
                            last = nc.tensor.matmul(o, ones2[:, :], gbias[:, m, :], start=False, stop=m == PARTS - 1)
                    last.then_inc(gru["product"], 1)

                def gemit(it, j):
                    stage(NP2, UG, it, j, 0, gturn)
                    stage(NP2, UG, it, j, 1, gmul)
                pipeline(pe, NP2, UG, 1, gemit)

        @block.vector
        def _(v):
            done = [0]

            def link(ins):
                done[0] += 1
                ins.then_inc(chain, 1)
                v.wait_ge(chain, done[0])

            def bc(t):
                return t.unsqueeze(2).to_broadcast([P, NB, D])

            def vec(n):
                return lng[:, n, :].unsqueeze(1).to_broadcast([P, NB, D])

            roots = [0]

            def root(src):
                roots[0] += 1
                src.then_inc(root_in, 1)
                v.wait_ge(root_out, roots[0])

            def layer_norm(src, dst, relu):
                link(nc.vector.reduce_sum(small[:, 0, :], src, AXX))
                link(nc.vector.tensor_scalar(small[:, 1, :], small[:, 0, :], 1.0 / D, None, ALU.mult))
                link(nc.vector.tensor_tensor(dst, src, bc(small[:, 1, :]), ALU.subtract))
                link(nc.vector.tensor_tensor(tmp_, dst, dst, ALU.mult))
                link(nc.vector.reduce_sum(small[:, 2, :], tmp_, AXX))
                root(nc.vector.tensor_scalar(small[:, 3, :], small[:, 2, :], 1.0 / D, EPS, ALU.mult, ALU.add))
                link(nc.vector.reciprocal(small[:, 1, :], small[:, 0, :]))
                link(nc.vector.tensor_tensor(dst, dst, bc(small[:, 1, :]), ALU.mult))
                if relu:
                    link(nc.vector.tensor_scalar(dst, dst, 0.0, None, ALU.max))

            nc.vector.memset(acc[:, :], 0.0).then_inc(acc_zero, 1)
            v.wait_ge(dst_loaded, 16)
            v.wait_ge(consts, 5)
            blocks = big[:, SPAD:SPAD + T].bitcast(I32)
            link(nc.vector.tensor_scalar(blocks, big[:, 0:T].bitcast(I32), 7, None, ALU.arith_shift_right))
            last_step = big[:, 0:T]
            link(nc.vector.tensor_tensor(last_step, blocks, itile, ALU.add))
            link(nc.vector.tensor_copy(fcol[:, 0, :], icol[:, :]))
            before = big[:, SPAD:SPAD + T]
            for c in range(CG):
                link(nc.vector.tensor_scalar(before, last_step, fcol[:, 0, c:c + 1], None, ALU.is_lt))
                link(nc.vector.reduce_sum(fcol[:, 1, c:c + 1], before, AXX))
            nc.vector.tensor_copy(tcol[:, :], fcol[:, 1, :]).then_inc(tiles_known, 1)
            link(nc.vector.tensor_tensor(fcol[:, 2, :], fcol[:, 0, :], fcol[:, 1, :], ALU.subtract))
            nc.vector.tensor_scalar(fcol[:, 3, :], fcol[:, 2, :], float(P), None, ALU.mult).then_inc(path_f, 1)
            for q in range(2):
                v.wait_ge(path_turned, q + 1)
                nc.vector.tensor_copy(pcol[:, q, :], bank[4 + q][0:CG, 0:P]).then_inc(path_copied, 1)

            v.wait_ge(consts, 11)
            nc.vector.tensor_copy(iota[:, :], iiota)
            nc.vector.memset(S[:, :, :], 1.0)
            nc.vector.memset(MS[:, :, :], 1.0)
            link(nc.vector.tensor_copy(trash[:, :], idx[:, 0:1]))

            v.wait_ge(x_loaded, 16)
            v.wait_ge(tiles_read, 1)
            v.wait_ge(path_f, 1)
            rowsi = [big[:, (2 + q) * SPAD:(3 + q) * SPAD].bitcast(I32) for q in range(3)]
            dst, valid, local, rtrash = (big[:, q * SPAD:(q + 1) * SPAD] for q in (5, 6, 0, 1))
            srcf, tsrcf = Hf[:, 0:SPAD], tmpf[:, 0:SPAD]
            link(nc.vector.tensor_copy(dst, rowsi[0]))
            link(nc.vector.tensor_copy(srcf, rowsi[1]))
            link(nc.vector.tensor_copy(rtrash, irtrash))
            link(nc.vector.tensor_copy(tsrcf, rowsi[2]))
            for c in range(CG):
                link(nc.vector.tensor_scalar(local[:, c * P:(c + 1) * P], dst[:, c * P:(c + 1) * P], fcol[:, 3, c:c + 1], None,
                                             ALU.subtract))
            link(nc.vector.tensor_scalar(valid, dst, float(N), None, ALU.is_lt))
            link(nc.vector.scalar_tensor_tensor(out=valid, in0=local, scalar=0.0, in1=valid, op0=ALU.is_ge, op1=ALU.mult))
            link(nc.vector.scalar_tensor_tensor(out=valid, in0=local, scalar=float(P - 1), in1=valid, op0=ALU.is_le, op1=ALU.mult))
            link(nc.vector.scalar_tensor_tensor(out=tsrcf, in0=srcf, scalar=float(KT), in1=tsrcf, op0=ALU.mult, op1=ALU.add))
            keyf = dst
            link(nc.vector.tensor_tensor(keyf, srcf, rtrash, ALU.subtract))
            link(nc.vector.tensor_tensor(keyf, keyf, valid, ALU.mult))
            link(nc.vector.tensor_tensor(keyf, keyf, rtrash, ALU.add))
            nc.vector.memset(hold2[:, :], 0.0).then_inc(idx_made, 4)
            for q, to in enumerate((dloc, srci, tsrci, key)):
                for g in range(IDXQ):
                    v.wait_ge(idx_turned, q * IDXQ + g + 1)
                    lo, hi = g * 4 * P, min((g + 1) * 4 * P, SPAD)
                    nc.vector.tensor_copy(to[:, lo:hi], bank[(q * IDXQ + g) % 2][:, 0:hi - lo]).then_inc(idx_tabled, 1)
            v.wait_ge(idx_tabled, 4 * IDXQ)

            layer_norm(X_, H_, True)
            link(nc.vector.memset(big_kv.rearrange("p (b d) -> p b d", d=KV)[:, :, KV - 1:KV], 1.0))
            node_dve(v, node, Hf, 2 * D, lambda k, f, m, ps: nc.vector.tensor_copy(
                group(big_kv, k, f, m, KV)[:, :, 0:2 * D], ps), QKV)
            v.wait_ge(node["finished"], QKV + NQ)
            nc.vector.memset(hold2[:, :], 0.0).then_inc(table_ready, 1)
            v.wait_ge(table_ready, 1)
            part_of = split.rearrange("p (b m d) -> p b m d", b=NB, m=PARTS)
            rest = big_kv.rearrange("p (b d) -> p b d", d=KV)[:, :, 0:D]
            for m in range(PARTS):
                link(nc.vector.tensor_copy(part_of[:, :, m, :], rest))
                if m < PARTS - 1:
                    link(nc.vector.tensor_tensor(tmp_, rest, part_of[:, :, m, :], ALU.subtract))
                    rest = tmp_
            v.wait_ge(reverse_zero, 16 * R)
            v.wait_ge(path_loaded, 16)
            link(nc.vector.memset(hold2[:, :], 0.0))
            nc.vector.memset(hold2[:, :], 0.0).then_inc(pass_begun, 1)
            v.wait_ge(pass_begun, 1)

            one, adds = hot(v, att, 0), sum_up(v, att, 0, AC, bank[4:6])
            products = prod[:, :, :].rearrange("p a b -> p (a b)").rearrange("p (n d) -> p n d", n=GR)

            def rows(j):
                return G[:, j * GR:(j + 1) * GR, :]

            def score(q, j, it):
                v.wait_ge(gathered[j], arrived(passes(0), j, it))
                v.wait_ge(att["query"], q + 1)
                if not (known(q) and q < 1):
                    v.wait_ge(att["scored"], q)
                nc.vector.scalar_tensor_tensor(out=products, in0=bank[2 + j % 2][:, 0:GR * D].rearrange("p (n d) -> p n d", n=GR),
                                               scalar=1.0 / D ** 0.5, in1=rows(j)[:, :, 0:D], op0=ALU.mult, op1=ALU.mult)\
                    .then_inc(att["score"], 1)

            def scored(q, j, it):
                v.wait_ge(att["score"], q + 1)
                nc.vector.reduce_sum(sc[:, 0, j % 2, :], products, AXX).then_inc(att["scored"], 1)

            def clip(q, j, it):
                v.wait_ge(att["scored"], q + 1)
                if not (known(q) and q < 2):
                    v.wait_ge(att["exp"], q - 1)
                nc.vector.tensor_scalar(sc[:, 1, j % 2, :], sc[:, 0, j % 2, :], 5.0, -5.0,
                                        ALU.min, ALU.max).then_inc(att["clipped"], 1)

            def msg(q, j, it):
                v.wait_ge(att["exp"], q + 1)
                if not (known(q) and q < 2):
                    v.wait_ge(att["seg"], q - 1)
                nc.vector.tensor_tensor(messages[:, j % 2, :, 0:D + 1], rows(j)[:, :, D:KV],
                                        sc[:, 2, j % 2, :].unsqueeze(2).to_broadcast([P, GR, D + 1]), ALU.mult)\
                    .then_inc(att["msg"], 1)

            def emit(it, j):
                stage(NG, UGR, it, j, 3, msg)
                stage(NG, UGR, it, j, 5, adds[0])
                stage(NG, UGR, it, j, 0, one)
                stage(NG, UGR, it, j, 5, adds[1])
                stage(NG, UGR, it, j, 2, score)
                stage(NG, UGR, it, j, 5, adds[2])
                stage(NG, UGR, it, j, 2, scored)
                stage(NG, UGR, it, j, 5, adds[3])
                stage(NG, UGR, it, j, 2, clip)
            pipeline(v, NG, UGR, 5, emit)
            v.wait_ge(att["summed"], STEPS)

            sums = acc_[AC].rearrange("p (b d) -> p b d", d=AC)
            link(nc.vector.tensor_copy(deg[:, :], sums[:, :, D + 1]))
            link(nc.vector.tensor_scalar(small[:, 2, :], sums[:, :, D], TINY, None, ALU.max))
            link(nc.vector.reciprocal(small[:, 1, :], small[:, 2, :]))
            link(nc.vector.tensor_tensor(tmp_, sums[:, :, 0:D], bc(small[:, 1, :]), ALU.mult))
            root(nc.vector.tensor_scalar(small[:, 3, :], deg[:, :], 1.0, None, ALU.max))
            link(nc.vector.reciprocal(norm[:, :], small[:, 0, :]))
            node_dve(v, node, tmpf, D, lambda k, f, m, ps: nc.vector.tensor_tensor(
                group(Hf, k, f, m, D), group(Hf, k, f, m, D), ps, ALU.add), ATTN)
            v.wait_ge(node["finished"], ATTN + NQ)
            layer_norm(H_, H_, False)
            link(nc.vector.tensor_tensor(H_, H_, vec(0), ALU.mult))
            link(nc.vector.tensor_tensor(H_, H_, vec(1), ALU.add))
            link(nc.vector.tensor_tensor(X_, X_, H_, ALU.add))

            layer_norm(X_, H_, True)
            nc.vector.tensor_tensor(tmp_, H_, bc(norm[:, :]), ALU.mult).then_inc(table_ready, 1)
            link(nc.vector.memset(acc_[D], 0.0))
            plain_dve(v, plain, 0)
            v.wait_ge(plain["summed"], STEPS)
            v.wait_ge(table_stored, 32)
            node_dve(v, node, acc_[D], D, lambda k, f, m, ps: nc.vector.tensor_copy(group(tmpf, k, f, m, D), ps), CONV)
            v.wait_ge(node["finished"], CONV + NQ)
            link(nc.vector.tensor_tensor(tmp_, tmp_, bc(norm[:, :]), ALU.mult))
            link(nc.vector.tensor_tensor(tmp_, tmp_, vec(2), ALU.add))
            link(nc.vector.tensor_tensor(X_, X_, tmp_, ALU.add))

            layer_norm(X_, H_, True)
            nc.vector.memset(hold2[:, :], 0.0).then_inc(table_ready, 1)
            v.wait_ge(table_ready, 3)
            link(nc.vector.memset(acc_[M], 0.0))
            node_dve(v, node, Hf, 2 * M, lambda k, f, m, ps: nc.vector.tensor_copy(
                group(big[:, :], k, f, m, 2 * M), ps), PAIR)
            v.wait_ge(node["finished"], PAIR + NQ)
            link(nc.vector.memset(MS[:, :, 2 * M:2 * M + 1], 1.0))
            nc.vector.memset(hold2[:, :], 0.0).then_inc(pass_begun, 1)
            v.wait_ge(pass_begun, 2)

            def hot2(k, j, it):
                if j % GR:
                    return
                if not (known(k) and k < HOT):
                    v.wait_ge(mes["seg"], k + (GR - HOT))
                onehots(k // GR if known(k) else it * (U // GR) + j // GR, j // GR).then_inc(mes["onehot"], 1)

            held = {}

            def add2(k, j, it):
                b = near(v, held, k, j)
                v.wait_ge(mes["seg"], k + 1)
                if not (known(k) and k < 1):
                    v.wait_ge(mes["summed"], k)
                to = acc_[M][:, bass.ds(b * M, M)]
                nc.vector.tensor_tensor(to, to, bank[6][:, 0:M], ALU.add).then_inc(mes["summed"], 1)

            def keys(k, j, it):
                if j % HALF:
                    return
                if not (known(k) and k < U):
                    v.wait_ge(mes["keyrow"], k + (HALF - U))
                    v.wait_ge(mes["rep"], k + (HALF - U))
                nc.vector.tensor_scalar(keyless[:, j:j + HALF], part(key[:, :], k, 1, 0, HALF), trash[:, 0:1], None,
                                        ALU.subtract).then_inc(mes["less"], 1)
                nc.vector.tensor_copy(keyslot[:, j:j + HALF], part(key[:, :], k, 1, 0, HALF)).then_inc(mes["keys"], 1)

            def equal(k, j, it):
                v.wait_ge(mes["keyrow"], k + 1)
                if not (known(k) and k < MR):
                    v.wait_ge(mes["seg"], k - MR + 1)
                nc.vector.tensor_scalar(EQ[:, j % MR, :], bank[7][:, 0:P], part(key[:, :], k, 1), None,
                                        ALU.is_equal).then_inc(mes["equal"], 1)

            def count(k, j, it):
                v.wait_ge(mes["equal"], k + 1)
                if not (known(k) and k < 2):
                    v.wait_ge(mes["rep"], k - 1)
                nc.vector.tensor_tensor_reduce(prod[:, j % 2, :], EQ[:, j % MR, :], earlier[:, :], 1.0, 0.0, ALU.mult, ALU.add,
                                               cnt[:, 0, j % 2:j % 2 + 1]).then_inc(mes["count"], 1)

            def rep(k, j, it):
                v.wait_ge(mes["count"], k + 1)
                v.wait_ge(mes["less"], it * (U // HALF) + j // HALF + 1)
                if not (known(k) and k < 2):
                    v.wait_ge(mes["index"], k - 1)
                nc.vector.tensor_scalar(cnt[:, 1, j % 2:j % 2 + 1], cnt[:, 0, j % 2:j % 2 + 1], 0.0,
                                        keyless[:, j:j + 1], ALU.is_equal, ALU.mult).then_inc(mes["rep"], 1)

            def index(k, j, it):
                v.wait_ge(mes["rep"], k + 1)
                if not (known(k) and k < U):
                    v.wait_ge(scattered[j % R], (it * (U // R) + j // R - U // R + 1) * 16)
                nc.vector.tensor_scalar(sidx[:, j:j + 1], cnt[:, 1, j % 2:j % 2 + 1], trash[:, 0:1], None,
                                        ALU.add).then_inc(mes["index"], 1)

            def emit2(it, j):
                stage(STEPS, U, it, j, 0, keys)
                stage(STEPS, U, it, j, 0, hot2)
                stage(STEPS, U, it, j, 1, equal)
                stage(STEPS, U, it, j, 2, rep)
                stage(STEPS, U, it, j, 1, count)
                stage(STEPS, U, it, j, 4, add2)
                stage(STEPS, U, it, j, 2, index)
            pipeline(v, STEPS, U, 4, emit2)
            v.wait_ge(mes["summed"], STEPS)

            def urows(k, j, it):
                r = j % 2
                if not (known(k) and k < 2):
                    v.wait_ge(upd["turned"], k - 1)
                nc.vector.tensor_copy(S[:, r, 0:M], part(acc_[M], k, M))
                nc.vector.tensor_copy(S[:, r, 2 * M + 2:2 * M + 2 + D], part(Hf, k, D))
                nc.vector.tensor_copy(S[:, r, 2 * M + 1:2 * M + 2], part(deg[:, :], k, 1))
                v.wait_ge(rev_loaded[r], (k // 2 + 1) * (16 * R) if known(k) else (it * (UN // 2) + j // 2 + 1) * (16 * R))
                if not (known(k) and k < 2):
                    v.wait_ge(upd["rows"], k - 1)
                nc.vector.tensor_tensor(NX[:, r, 0:RC], revs[:, r, 0, :], revs[:, r, 1, :], ALU.add).then_inc(upd["sums"], 1)
                nc.vector.tensor_tensor(NX[:, r, RC:2 * RC], revs[:, r, 2, :], revs[:, r, 3, :], ALU.add).then_inc(upd["sums"], 1)
                v.wait_ge(upd["sums"], k * 2 + 2)
                nc.vector.tensor_tensor(S[:, r, M:M + RC], NX[:, r, 0:RC], NX[:, r, RC:2 * RC], ALU.add).then_inc(upd["rows"], 1)

            def uend(k, j, it):
                v.wait_ge(upd["product"], k + 1)
                nc.vector.tensor_copy(part(tmpf, k, D), bank[6 + j % 2][:, 0:D]).then_inc(upd["finished"], 1)

            def uemit(it, j):
                stage(NB, UN, it, j, 0, urows)
                stage(NB, UN, it, j, 4, uend)
            pipeline(v, NB, UN, 4, uemit)
            v.wait_ge(upd["finished"], NB)
            link(nc.vector.tensor_tensor(tmp_, tmp_, H_, ALU.add))
            link(nc.vector.tensor_tensor(X_, X_, tmp_, ALU.add))
            layer_norm(X_, H_, True)
            link(nc.vector.memset(S[:, :, :], 1.0))

            link(nc.vector.memset(ones2[:, :], 1.0))
            left = w("gb", 2)
            for m in range(PARTS):
                link(nc.vector.tensor_copy(gbias[:, m, :], left))
                if m < PARTS - 1:
                    link(nc.vector.tensor_tensor(gleft[:, :], left, gbias[:, m, :], ALU.subtract))
                    left = gleft[:, :]
            with v.Fori(0, LAYERS) as layer:
                nbase, gbase = layer * NQ, layer * NP2
                node_dve(v, node, Hf, KT * D, lambda k, f, m, ps: nc.vector.tensor_copy(
                    group(big[:, :], k, f, m, KT * D), ps), nbase + TYPES)
                v.wait_ge(node["finished"], nbase + (TYPES + NQ))
                nc.vector.memset(acc_[D], 0.0).then_inc(gru_acc_zero, 1)
                v.wait_ge(gru_acc_zero, layer * 2 + 1)
                plain_dve(v, plain, layer * NG + NG)
                v.wait_ge(plain["summed"], layer * STEPS + 2 * STEPS)
                v.wait_ge(types_stored, layer * TYPES_DONE + TYPES_DONE)

                def grows(k, j, it):
                    n = blocks_in(k, G2)
                    if not (known(k) and k < 2):
                        v.wait_ge(gru["turned"], gbase + k - 1)
                    nc.vector.tensor_copy(S2[:, j % 2, 0:n, D:2 * D], apart(part(Hf, k, G2 * D, 0, n * D), n))
                    nc.vector.tensor_copy(S2[:, j % 2, 0:n, 0:D], apart(part(acc_[D], k, G2 * D, 0, n * D), n))\
                        .then_inc(gru["rows"], 1)

                def gate(k, j, it):
                    r, n = j % 2, blocks_in(k, G2)
                    product = apart(bank[2 + r][:, 0:n * 4 * D], n)
                    v.wait_ge(gru["gates"], gbase + k + 1)
                    nc.vector.tensor_tensor(GX[:, r, 0:n, 2 * D:3 * D], GX[:, r, 0:n, 0:D], product[:, :, 3 * D:4 * D], ALU.mult)\
                        .then_inc(gru["mul"], 1)
                    v.wait_ge(gru["mul"], gbase + k + 1)
                    nc.vector.tensor_tensor(GX[:, r, 0:n, 3 * D:4 * D], GX[:, r, 0:n, 2 * D:3 * D], product[:, :, 2 * D:3 * D],
                                            ALU.add).then_inc(gru["add"], 1)

                def blend(k, j, it):
                    r, n = j % 2, blocks_in(k, G2)
                    state = apart(part(Hf, k, G2 * D, 0, n * D), n)
                    v.wait_ge(gru["tanh"], gbase + k + 1)
                    nc.vector.tensor_tensor(GX[:, r, 0:n, 5 * D:6 * D], state, GX[:, r, 0:n, 4 * D:5 * D], ALU.subtract)\
                        .then_inc(gru["diff"], 1)
                    v.wait_ge(gru["diff"], gbase + k + 1)
                    nc.vector.tensor_tensor(GX[:, r, 0:n, 6 * D:7 * D], GX[:, r, 0:n, D:2 * D], GX[:, r, 0:n, 5 * D:6 * D],
                                            ALU.mult).then_inc(gru["blend"], 1)
                    v.wait_ge(gru["blend"], gbase + k + 1)
                    nc.vector.tensor_tensor(state, GX[:, r, 0:n, 4 * D:5 * D], GX[:, r, 0:n, 6 * D:7 * D], ALU.add)\
                        .then_inc(gru["finished"], 1)

                def gemit(it, j):
                    stage(NP2, UG, it, j, 0, grows)
                    stage(NP2, UG, it, j, 2, gate)
                    stage(NP2, UG, it, j, 3, blend)
                pipeline(v, NP2, UG, 3, gemit)
                v.wait_ge(gru["finished"], gbase + NP2)
                nc.vector.memset(S4[:, :, :, D:D + 1], 1.0).then_inc(gru_acc_zero, 1)
                v.wait_ge(gru_acc_zero, layer * 2 + 2)
            nc.vector.tensor_tensor(X_, X_, H_, ALU.add).then_inc(result, 1)


def pack(i):
    import numpy as np
    g = {k: np.asarray(v) for k, v in i.items()}
    W = np.zeros((P, WTOTAL), np.float32)

    def put(name, block, row=0, col=0):
        lo = WCOLS[name][0] + col
        W[row:row + block.shape[0], lo:lo + block.shape[1]] = block

    put("qkv", g["L0_gnn_qk_w"].T)
    put("qkv", g["L0_gnn_v_w"].T, col=D)
    put("qkv", g["L0_gnn_qk_b"][None], row=D)
    put("qkv", g["L0_gnn_v_b"][None], row=D, col=D)
    put("attn", g["L0_gnn_o_w"].T)
    put("attn", g["L0_gnn_o_b"][None], row=D)
    put("conv", g["L1_gnn_weight"])
    f, r = g["L2_gnn_W1_f"], g["L2_gnn_W1_r"]
    put("pair", f[D:2 * D])
    put("pair", r[0:D], col=M)
    put("pair", g["L2_gnn_b1_f"][None], row=D)
    put("pair", g["L2_gnn_b1_r"][None], row=D, col=M)
    put("edge", f[0:D])
    put("edge", r[D:2 * D], col=M)
    put("edge", f[2 * D:], row=D)
    put("edge", r[2 * D:], row=D, col=M)
    put("f2", g["L2_gnn_W2_f"])
    put("r2", g["L2_gnn_W2_r"])
    put("b2", g["L2_gnn_b2_r"][None])
    put("b2", g["L2_gnn_b2_f"][None], row=1)
    put("n1a", g["L2_gnn_Wn1"][0:M])
    put("n1b", g["L2_gnn_Wn1"][M:], row=2)
    put("bn1", g["L2_gnn_bn1"][:, None])
    put("n2", g["L2_gnn_Wn2"])
    put("bn2", g["L2_gnn_bn2"][None])
    for t in range(KT):
        put("types", g["L3_gnn_W"][t].T, col=t * D)
        put("types", g["L3_gnn_b"][t][None], row=D, col=t * D)
    ih, hh = g["L3_gnn_w_ih"].T, g["L3_gnn_w_hh"].T
    put("gru", ih)
    put("gru", hh[:, 0:2 * D], row=D)
    put("gru", hh[:, 2 * D:], row=D, col=3 * D)
    put("gb", g["L3_gnn_b_ih"][None])
    put("gb", g["L3_gnn_b_hh"][None, 0:2 * D], row=1)
    put("gb", g["L3_gnn_b_hh"][None, 2 * D:], row=1, col=3 * D)
    vectors = np.concatenate([g["L0_gnn_ln_g"], g["L0_gnn_ln_b"], g["L1_gnn_bias"]])
    return W, vectors


def kernel(**inputs):
    import numpy as np
    import concourse.bacc as bacc
    from concourse.bass_utils import run_bass_kernel_spmd

    def tiles(name, fill):
        a = np.full(((T + 1) * P,), fill, np.int32)
        a[:E] = np.asarray(inputs[name])
        return a.reshape(T + 1, P)

    x = np.zeros((NPAD, D), np.float32)
    x[:N] = np.asarray(inputs["x"])
    edge = np.zeros(((T + 1) * P, D), np.float32)
    edge[:E] = np.asarray(inputs["edge_attr_64"])
    dst = tiles("dst", PADDST)
    W, vectors = pack(inputs)
    arrays = {"x": x, "src": tiles("src", 0), "dst": dst, "type": tiles("edge_type_4", 0), "edge": edge,
              "dst_last": np.ascontiguousarray(dst[:T, P - 1]), "weights": W, "vectors": vectors}
    nc = bacc.Bacc("TRN2", target_bir_lowering=False, num_devices=1)
    aps = {n: nc.dram_tensor(f"in_{n}", v.shape, mybir.dt.from_np(v.dtype), kind="ExternalInput").ap()
           for n, v in arrays.items()}
    out = nc.dram_tensor("out_0", (N, D), F32, kind="ExternalOutput").ap()
    build(nc, aps, out)
    r = run_bass_kernel_spmd(nc, [{f"in_{n}": v for n, v in arrays.items()}], core_ids=[0])
    return r.results[0]["out_0"]
```
